# Optimizing a Trainium2 kernel written in Bass

```python
import numpy as np
import jax
import jax.numpy as jnp

def _softmax(x, axis=-1):
    return jax.nn.softmax(x, axis=axis)

def _gelu(x):
    return jax.nn.gelu(x, approximate=True)

def _silu(x):
    return jax.nn.silu(x)

def _sigmoid(x):
    return jax.nn.sigmoid(x)

def _layernorm(x, axis=-1, eps=1e-05):
    m = jnp.mean(x, axis=axis, keepdims=True)
    v = jnp.var(x, axis=axis, keepdims=True)
    return (x - m) / jnp.sqrt(v + eps)

def _scatter_add(tgt, idx, src, axis=0):
    return tgt.at[idx].add(src)

def _segment_sum(src, seg, n):
    return jax.ops.segment_sum(src, seg, n)
kernel_name = 'mk_macaron_d2_jaxref_r8_f6b7a7'

def setup_inputs(seed: int=0):
    np.random.seed(seed)
    _w = jnp.asarray

    def _L0_attn_setup():
        import jax, jax.numpy as jnp
        import numpy as np
        B, L, H, U = (4, 512, 128, 128)
        key = jax.random.key(seed)
        k0, k1, k2, k3 = jax.random.split(key, 4)
        inputs = jax.random.normal(k0, (B, L, H), dtype=jnp.float32)
        W_rkv = jax.random.normal(k1, (H, 3 * U), dtype=jnp.float32) / np.sqrt(H)
        b_rkv = jnp.zeros((3 * U,), dtype=jnp.float32)
        W_o = jax.random.normal(k2, (U, H), dtype=jnp.float32) / np.sqrt(U)
        b_o = jnp.zeros((H,), dtype=jnp.float32)
        r_min, r_max = (0.9, 0.999)
        u = jax.random.uniform(k3, (U,), dtype=jnp.float32)
        nu_log = jnp.log(-0.5 * jnp.log(u * (r_max ** 2 - r_min ** 2) + r_min ** 2))
        gamma_log = jnp.zeros((U,), dtype=jnp.float32)
        return {'inputs': inputs, 'W_rkv': W_rkv, 'b_rkv': b_rkv, 'W_o': W_o, 'b_o': b_o, 'nu_log': nu_log, 'gamma_log': gamma_log}
    _L0_attn_in = _L0_attn_setup()

    def _L0_ffn_setup():
        import jax, jax.numpy as jnp
        import numpy as np
        H = 128
        I = 128
        E = 8
        key = jax.random.key(seed)
        ks = jax.random.split(key, 8)
        s = 0.02
        x = jax.random.normal(ks[0], (4, 256, H), dtype=jnp.float32)
        Wg = jax.random.normal(ks[1], (H, E), dtype=jnp.float32) * s
        bg = jnp.zeros((E,), dtype=jnp.float32)
        W1 = jax.random.normal(ks[2], (E, H, I), dtype=jnp.float32) * s
        b1 = jnp.zeros((E, I), dtype=jnp.float32)
        W2 = jax.random.normal(ks[3], (E, I, H), dtype=jnp.float32) * s
        b2 = jnp.zeros((E, H), dtype=jnp.float32)
        return {'x': x, 'Wg': Wg, 'bg': bg, 'W1': W1, 'b1': b1, 'W2': W2, 'b2': b2}
    _L0_ffn_in = _L0_ffn_setup()

    def _L1_attn_setup():
        import jax, jax.numpy as jnp
        import numpy as np
        EMBED_DIM = 128
        NUM_HEADS = 16
        HEAD_DIM = EMBED_DIM // NUM_HEADS

        def _sinusoid_pos_emb(seq_len, dim):
            pos = jnp.arange(seq_len, dtype=jnp.float32)
            idx = jnp.arange(dim // 2, dtype=jnp.float32)
            inv_freq = 1.0 / 10000.0 ** (2.0 * idx / dim)
            ang = pos[:, None] * inv_freq[None, :]
            return jnp.concatenate([jnp.sin(ang), jnp.cos(ang)], axis=-1)

        def _relative_shift(x):
            b, h, s, _ = x.shape
            x = jnp.pad(x, ((0, 0), (0, 0), (0, 0), (1, 0)))
            x = x.reshape(b, h, s + 1, s)
            return x[:, :, 1:, :].reshape(b, h, s, s)
        key = jax.random.key(seed)
        ks = jax.random.split(key, 12)
        D = EMBED_DIM
        sc = 1.0 / np.sqrt(D)
        inp = {'x': jax.random.normal(ks[0], (2, 256, D), dtype=jnp.float32)}
        for i, name in enumerate(['Wq', 'Wk', 'Wv', 'Wp', 'Wo']):
            inp[name] = jax.random.normal(ks[1 + i], (D, D), dtype=jnp.float32) * sc
            inp['b' + name[1].lower()] = jnp.zeros((D,), dtype=jnp.float32)
        inp['u'] = jax.random.normal(ks[6], (1, NUM_HEADS, 1, HEAD_DIM), dtype=jnp.float32) * 0.05
        inp['v'] = jax.random.normal(ks[7], (1, NUM_HEADS, 1, HEAD_DIM), dtype=jnp.float32) * 0.05
        return inp
    _L1_attn_in = _L1_attn_setup()

    def _L1_ffn_setup():
        import jax, jax.numpy as jnp
        import numpy as np
        H = 128
        E = 8
        TOP_K = 2
        FF = 4 * H
        B, S = (2, 256)

        def _moe_forward(x, gate_w, gate_b, w1, b1, w2, b2, sw1, sb1, sw2, sb2):
            b, s, h = x.shape
            xf = x.reshape(-1, h)
            scores = jax.nn.sigmoid(xf @ gate_w.T + gate_b)
            top_scores, top_idx = jax.lax.top_k(scores, TOP_K)
            top_scores = top_scores / (top_scores.sum(-1, keepdims=True) + 1e-06)
            comb = (jax.nn.one_hot(top_idx, E, dtype=xf.dtype) * top_scores[..., None]).sum(1)
            hdn = jax.nn.gelu(jnp.einsum('th,ehf->etf', xf, w1) + b1[:, None, :], approximate=False)
            y = jnp.einsum('etf,efh->eth', hdn, w2) + b2[:, None, :]
            routed = jnp.einsum('te,eth->th', comb, y)
            shared = (jax.nn.gelu(xf @ sw1 + sb1, approximate=False) @ sw2 + sb2) * 0.1
            return (routed + shared).reshape(b, s, h)
        key = jax.random.key(seed)
        ks = jax.random.split(key, 12)
        std = 0.02 / np.sqrt(H)
        return {'x': jax.random.normal(ks[0], (B, S, H), dtype=jnp.float32), 'gate_w': jax.random.normal(ks[1], (E, H), dtype=jnp.float32) * std, 'gate_b': jnp.zeros((E,), dtype=jnp.float32), 'w1': jax.random.normal(ks[2], (E, H, FF), dtype=jnp.float32) * (1.0 / np.sqrt(H)), 'b1': jnp.zeros((E, FF), dtype=jnp.float32), 'w2': jax.random.normal(ks[3], (E, FF, H), dtype=jnp.float32) * (1.0 / np.sqrt(FF)), 'b2': jnp.zeros((E, H), dtype=jnp.float32), 'sw1': jax.random.normal(ks[4], (H, FF), dtype=jnp.float32) * (1.0 / np.sqrt(H)), 'sb1': jnp.zeros((FF,), dtype=jnp.float32), 'sw2': jax.random.normal(ks[5], (FF, H), dtype=jnp.float32) * (1.0 / np.sqrt(FF)), 'sb2': jnp.zeros((H,), dtype=jnp.float32)}
    _L1_ffn_in = _L1_ffn_setup()
    _d = {'L0_attn_inputs': _L0_attn_in['inputs'], 'L0_attn_W_rkv': _L0_attn_in['W_rkv'], 'L0_attn_b_rkv': _L0_attn_in['b_rkv'], 'L0_attn_W_o': _L0_attn_in['W_o'], 'L0_attn_b_o': _L0_attn_in['b_o'], 'L0_attn_nu_log': _L0_attn_in['nu_log'], 'L0_attn_gamma_log': _L0_attn_in['gamma_log'], 'L0_ffn_Wg': _L0_ffn_in['Wg'], 'L0_ffn_bg': _L0_ffn_in['bg'], 'L0_ffn_W1': _L0_ffn_in['W1'], 'L0_ffn_b1': _L0_ffn_in['b1'], 'L0_ffn_W2': _L0_ffn_in['W2'], 'L0_ffn_b2': _L0_ffn_in['b2'], 'L1_attn_Wq': _L1_attn_in['Wq'], 'L1_attn_bq': _L1_attn_in['bq'], 'L1_attn_Wk': _L1_attn_in['Wk'], 'L1_attn_bk': _L1_attn_in['bk'], 'L1_attn_Wv': _L1_attn_in['Wv'], 'L1_attn_bv': _L1_attn_in['bv'], 'L1_attn_Wp': _L1_attn_in['Wp'], 'L1_attn_bp': _L1_attn_in['bp'], 'L1_attn_Wo': _L1_attn_in['Wo'], 'L1_attn_bo': _L1_attn_in['bo'], 'L1_attn_u': _L1_attn_in['u'], 'L1_attn_v': _L1_attn_in['v'], 'L1_ffn_gate_w': _L1_ffn_in['gate_w'], 'L1_ffn_gate_b': _L1_ffn_in['gate_b'], 'L1_ffn_w1': _L1_ffn_in['w1'], 'L1_ffn_b1': _L1_ffn_in['b1'], 'L1_ffn_w2': _L1_ffn_in['w2'], 'L1_ffn_b2': _L1_ffn_in['b2'], 'L1_ffn_sw1': _L1_ffn_in['sw1'], 'L1_ffn_sb1': _L1_ffn_in['sb1'], 'L1_ffn_sw2': _L1_ffn_in['sw2'], 'L1_ffn_sb2': _L1_ffn_in['sb2']}
    _x0 = _d['L0_attn_inputs']
    _d['L0_attn_inputs'] = jax.random.normal(jax.random.fold_in(jax.random.key(seed), 1), (16, 512, 128), dtype=_x0.dtype)
    del _x0
    return _d

def reference(L0_attn_inputs, L0_attn_W_rkv, L0_attn_b_rkv, L0_attn_W_o, L0_attn_b_o, L0_attn_nu_log, L0_attn_gamma_log, L0_ffn_Wg, L0_ffn_bg, L0_ffn_W1, L0_ffn_b1, L0_ffn_W2, L0_ffn_b2, L1_attn_Wq, L1_attn_bq, L1_attn_Wk, L1_attn_bk, L1_attn_Wv, L1_attn_bv, L1_attn_Wp, L1_attn_bp, L1_attn_Wo, L1_attn_bo, L1_attn_u, L1_attn_v, L1_ffn_gate_w, L1_ffn_gate_b, L1_ffn_w1, L1_ffn_b1, L1_ffn_w2, L1_ffn_b2, L1_ffn_sw1, L1_ffn_sb1, L1_ffn_sw2, L1_ffn_sb2):

    def _L0_attn_ref(inputs, W_rkv, b_rkv, W_o, b_o, nu_log, gamma_log):
        import jax, jax.numpy as jnp
        import numpy as np
        B, L, H, U = (4, 512, 128, 128)
        rkv = jnp.einsum('blh,hu->blu', inputs, W_rkv) + b_rkv
        r, k, v = jnp.split(rkv, 3, axis=-1)
        r = jax.nn.sigmoid(r)
        k = jnp.exp(k)
        kv = k * v
        u = jnp.concatenate([kv, k], axis=-1)
        nu = jnp.exp(jnp.concatenate([nu_log, nu_log]))
        gamma = jnp.exp(nu_log + gamma_log) - 1.0
        lam = jnp.exp(-nu)
        a = jnp.broadcast_to(lam, u.shape)

        def combine(c1, c2):
            a1, x1 = c1
            a2, x2 = c2
            return (a1 * a2, x1 * a2 + x2)
        _, y = jax.lax.associative_scan(combine, (a, u), axis=1)
        u1, u2 = jnp.split(y, 2, axis=-1)
        x = (u1 + gamma * kv) / (u2 + gamma * k + 1e-06) * r
        return jnp.einsum('blu,uh->blh', x, W_o) + b_o

    def _L0_ffn_ref(x, Wg, bg, W1, b1, W2, b2):
        import jax, jax.numpy as jnp
        import numpy as np
        H = 128
        I = 128
        E = 8
        B, S, Hd = x.shape
        xf = x.reshape(-1, Hd)
        logits = xf @ Wg + bg
        gates = jax.nn.softmax(logits, axis=-1)
        idx = jnp.argmax(gates, axis=-1)
        h = jax.nn.gelu(jnp.einsum('th,ehi->tei', xf, W1) + b1, approximate=False)
        y = jnp.einsum('tei,eih->teh', h, W2) + b2
        out = jnp.take_along_axis(y, idx[:, None, None], axis=1)[:, 0, :]
        return out.reshape(B, S, Hd)

    def _L1_attn_ref(x, Wq, bq, Wk, bk, Wv, bv, Wp, bp, Wo, bo, u, v):
        import jax, jax.numpy as jnp
        import numpy as np
        EMBED_DIM = 128
        NUM_HEADS = 16
        HEAD_DIM = EMBED_DIM // NUM_HEADS

        def _sinusoid_pos_emb(seq_len, dim):
            pos = jnp.arange(seq_len, dtype=jnp.float32)
            idx = jnp.arange(dim // 2, dtype=jnp.float32)
            inv_freq = 1.0 / 10000.0 ** (2.0 * idx / dim)
            ang = pos[:, None] * inv_freq[None, :]
            return jnp.concatenate([jnp.sin(ang), jnp.cos(ang)], axis=-1)

        def _relative_shift(x):
            b, h, s, _ = x.shape
            x = jnp.pad(x, ((0, 0), (0, 0), (0, 0), (1, 0)))
            x = x.reshape(b, h, s + 1, s)
            return x[:, :, 1:, :].reshape(b, h, s, s)
        B, S, D = x.shape
        H, P = (NUM_HEADS, HEAD_DIM)

        def heads(t):
            return t.reshape(B, S, H, P).transpose(0, 2, 1, 3)
        q = heads(x @ Wq + bq)
        k = heads(x @ Wk + bk)
        val = heads(x @ Wv + bv)
        pos = _sinusoid_pos_emb(S, D) @ Wp + bp
        pos = pos.reshape(S, H, P).transpose(1, 0, 2)
        content_score = jnp.einsum('bhsp,bhtp->bhst', q + u, k)
        pos_score = jnp.einsum('bhsp,htp->bhst', q + v, pos)
        pos_score = _relative_shift(pos_score)
        score = (content_score + pos_score) / jnp.sqrt(jnp.float32(P))
        weights = jax.nn.softmax(score, axis=-1)
        out = jnp.einsum('bhst,bhtp->bhsp', weights, val)
        out = out.transpose(0, 2, 1, 3).reshape(B, S, D)
        return out @ Wo + bo

    def _L1_ffn_ref(x, gate_w, gate_b, w1, b1, w2, b2, sw1, sb1, sw2, sb2):
        import jax, jax.numpy as jnp
        import numpy as np
        H = 128
        E = 8
        TOP_K = 2
        FF = 4 * H
        B, S = (2, 256)

        def _moe_forward(x, gate_w, gate_b, w1, b1, w2, b2, sw1, sb1, sw2, sb2):
            b, s, h = x.shape
            xf = x.reshape(-1, h)
            scores = jax.nn.sigmoid(xf @ gate_w.T + gate_b)
            top_scores, top_idx = jax.lax.top_k(scores, TOP_K)
            top_scores = top_scores / (top_scores.sum(-1, keepdims=True) + 1e-06)
            comb = (jax.nn.one_hot(top_idx, E, dtype=xf.dtype) * top_scores[..., None]).sum(1)
            hdn = jax.nn.gelu(jnp.einsum('th,ehf->etf', xf, w1) + b1[:, None, :], approximate=False)
            y = jnp.einsum('etf,efh->eth', hdn, w2) + b2[:, None, :]
            routed = jnp.einsum('te,eth->th', comb, y)
            shared = (jax.nn.gelu(xf @ sw1 + sb1, approximate=False) @ sw2 + sb2) * 0.1
            return (routed + shared).reshape(b, s, h)
        return _moe_forward(x, gate_w, gate_b, w1, b1, w2, b2, sw1, sb1, sw2, sb2)
    x = L0_attn_inputs
    x = x + 0.5 * _L0_ffn_ref(_layernorm(x, axis=-1), L0_ffn_Wg, L0_ffn_bg, L0_ffn_W1, L0_ffn_b1, L0_ffn_W2, L0_ffn_b2)
    x = x + _L0_attn_ref(_layernorm(x, axis=-1), L0_attn_W_rkv, L0_attn_b_rkv, L0_attn_W_o, L0_attn_b_o, L0_attn_nu_log, L0_attn_gamma_log)
    x = x + 0.5 * _L0_ffn_ref(_layernorm(x, axis=-1), L0_ffn_Wg, L0_ffn_bg, L0_ffn_W1, L0_ffn_b1, L0_ffn_W2, L0_ffn_b2)
    x = x + 0.5 * _L1_ffn_ref(_layernorm(x, axis=-1), L1_ffn_gate_w, L1_ffn_gate_b, L1_ffn_w1, L1_ffn_b1, L1_ffn_w2, L1_ffn_b2, L1_ffn_sw1, L1_ffn_sb1, L1_ffn_sw2, L1_ffn_sb2)
    x = x + _L1_attn_ref(_layernorm(x, axis=-1), L1_attn_Wq, L1_attn_bq, L1_attn_Wk, L1_attn_bk, L1_attn_Wv, L1_attn_bv, L1_attn_Wp, L1_attn_bp, L1_attn_Wo, L1_attn_bo, L1_attn_u, L1_attn_v)
    x = x + 0.5 * _L1_ffn_ref(_layernorm(x, axis=-1), L1_ffn_gate_w, L1_ffn_gate_b, L1_ffn_w1, L1_ffn_b1, L1_ffn_w2, L1_ffn_b2, L1_ffn_sw1, L1_ffn_sb1, L1_ffn_sw2, L1_ffn_sb2)
    return x

_drawn_inputs = setup_inputs


def setup_inputs(seed=0):
    import zlib

    import numpy as np

    out = dict(_drawn_inputs(seed))
    spreads = {'L0_attn_b_rkv': (0.0, 0.1),
     'L0_attn_b_o': (0.0, 0.1),
     'L0_attn_gamma_log': (0.0, 2.0),
     'L0_ffn_bg': (0.0, 0.1),
     'L0_ffn_b1': (0.0, 0.276),
     'L0_ffn_b2': (0.0, 0.1),
     'L1_attn_bq': (0.0, 0.399),
     'L1_attn_bk': (0.0, 2.0),
     'L1_attn_bv': (0.0, 0.1),
     'L1_attn_bp': (0.0, 0.707),
     'L1_attn_bo': (0.0, 0.1),
     'L1_ffn_gate_b': (0.0, 0.1),
     'L1_ffn_b1': (0.0, 0.1),
     'L1_ffn_b2': (0.0, 0.1),
     'L1_ffn_sb1': (0.0, 0.787),
     'L1_ffn_sb2': (0.0, 0.579)}
    factors = {'L1_attn_u': 4.535, 'L1_attn_v': 8.0}
    for name, (base, spread) in spreads.items():
        noise = np.random.default_rng([zlib.crc32(name.encode()), seed]).standard_normal(out[name].shape)
        drawn = base * np.exp(spread * noise) if base else spread * noise
        out[name] = jnp.asarray(drawn.astype(out[name].dtype))
    for name, factor in factors.items():
        out[name] = (out[name] * factor).astype(out[name].dtype)
    return out
```

```python
from contextlib import ExitStack

import numpy as np

import concourse.bass as bass
from concourse import mybir

F32 = mybir.dt.float32
U32 = mybir.dt.uint32
ALU = mybir.AluOpType
ACT = mybir.ActivationFunctionType
AX = mybir.AxisListType

P = 128
B = 16
S = 512
D = 128
TILES = S // P
EXPERTS = 8
HEADS = 16
HD = D // HEADS
EPS = 1e-5

HALF = 8
ROWS = P // HALF
GROUPS = S // ROWS
POS_W = 560
POS_0 = 17


class Phase:

    def __init__(self, nc, name):
        self.nc, self.name, self.ctx, self.sems = nc, name, ExitStack(), []

    def __enter__(self):
        return self

    def __exit__(self, *exc):
        if self.sems and exc[0] is None:
            with self.nc.Block() as block:
                @block.sync
                def _(sp):
                    for sem in self.sems:
                        sp.sem_clear(sem)
        return self.ctx.__exit__(*exc)

    def sb(self, name, shape, dt=F32):
        return self.ctx.enter_context(self.nc.sbuf_tensor(f"{self.name}_{name}", shape, dt))

    def ps(self, name, shape):
        return self.ctx.enter_context(self.nc.psum_tensor(f"{self.name}_{name}", shape, F32))

    def sem(self, name):
        self.sems.append(self.ctx.enter_context(self.nc.semaphore(f"{self.name}_{name}")))
        return self.sems[-1]


def rows_at(x, b):
    return x[:, bass.ds(b * (TILES * D), TILES * D)]


def tile_at(x, b, t):
    return x[:, bass.ds(b * (TILES * D) + t * D, D)]


def over_batches(eng, body):
    with eng.Fori(0, B // 2 - 1) as i:
        body(2 * i, 0)
        body(2 * i + 1, 1)
    body(B - 2, 0)
    body(B - 1, 1)


def has_next(b):
    return not (isinstance(b, int) and b == B - 1)


def wait_apart(eng, sem, value, passed):
    eng.wait_ge(sem, value)
    eng.sem_inc(passed, 1)


class LayerNorm:

    def __init__(self, ph, x, ident, transposed_psum):
        self.x, self.ident, self.xT = x, ident, transposed_psum
        self.stats = ph.sb("stats", [P, TILES * 6])
        self.mv = ph.sb("mv", [P, TILES * 2])
        self.var = ph.sb("var", [P, TILES])
        self.rstd = ph.sb("rstd", [P, TILES])
        self.minus_half = ph.sb("minus_half", [P, TILES])
        self.xn = ph.sb("xn", [P, S])
        self.xnT = [ph.sb(f"xnT{i}", [P, S]) for i in range(2)]
        self.passed = ph.sem("passed")
        self.stats_done = ph.sem("stats_done")
        self.mv_done = ph.sem("mv_done")
        self.const_done = ph.sem("ln_const")
        self.var_done = ph.sem("var_done")
        self.rstd_done = ph.sem("rstd_done")
        self.xn_done = ph.sem("xn_done")
        self.xT_ready = ph.sem("xT_ready")
        self.xnT_done = ph.sem("xnT_done")

    def pool_setup(self, pool):
        pool.memset(self.minus_half[:], -0.5).then_inc(self.const_done, 1)
        pool.wait_ge(self.const_done, 1)

    def dve_stats(self, dve, b):
        for t in range(TILES):
            last = dve.bn_stats(self.stats[:, t * 6:(t + 1) * 6], tile_at(self.x, b, t))
        last.then_inc(self.stats_done, 1)
        wait_apart(dve, self.stats_done, b + 1, self.passed)
        for t in range(TILES):
            last = dve.bn_aggr(self.mv[:, 2 * t:2 * t + 2], self.stats[:, t * 6:(t + 1) * 6])
        last.then_inc(self.mv_done, 1)

    def pool_rstd(self, pool, b):
        wait_apart(pool, self.mv_done, b + 1, self.passed)
        pool.tensor_scalar(self.var[:], self.mv[:].rearrange("p (t two) -> p t two", two=2)[:, :, 1],
                           EPS, None, ALU.add).then_inc(self.var_done, 1)
        pool.wait_ge(self.var_done, b + 1)
        pool.tensor_tensor(self.rstd[:], self.var[:], self.minus_half[:], ALU.pow).then_inc(self.rstd_done, 1)

    def dve_norm(self, dve, b):
        dve.wait_ge(self.rstd_done, b + 1)
        dve.wait_ge(self.xT_ready, b)
        for t in range(TILES):
            last = dve.tensor_scalar(self.xn[:, t * D:(t + 1) * D], tile_at(self.x, b, t),
                                     self.mv[:, 2 * t:2 * t + 1], self.rstd[:, t:t + 1],
                                     ALU.subtract, ALU.mult)
        last.then_inc(self.xn_done, 1)

    def pe_transpose(self, pe, b):
        pe.wait_ge(self.xn_done, b + 1)
        pe.wait_ge(self.xnT_done, b)
        for t in range(TILES):
            last = pe.transpose(self.xT[:, t * P:(t + 1) * P], self.xn[:, t * D:(t + 1) * D], self.ident[:])
        last.then_inc(self.xT_ready, 1)

    def act_copy(self, act, b, par):
        act.wait_ge(self.xT_ready, b + 1)
        act.copy(self.xnT[par][:], self.xT[:]).then_inc(self.xnT_done, 1)


def ffn_phase(nc, name, x, ident, iota, w, top2, x_in=None):
    E = EXPERTS + 1 if top2 else EXPERTS
    C = 4 if top2 else 1
    units = E + 1
    WEIGHT = 0.5
    H_PRE, Y_PRE = 4, 3
    with Phase(nc, name) as ph:
        w1 = ph.sb("w1", [P, E * C * P])
        b1 = ph.sb("b1", [P, E * C])
        w2 = ph.sb("w2", [P, E * C * D])
        b2 = ph.sb("b2", [E, D])
        wg = ph.sb("wg", [P, EXPERTS])
        bg = ph.sb("bg", [P, TILES * EXPERTS])
        hT = [ph.sb(f"hT{i}", [P, C, S]) for i in range(2)]
        logits = ph.sb("logits", [P, TILES * EXPERTS])
        top = ph.sb("top", [P, TILES, 8])
        idx = ph.sb("idx", [P, TILES, 8], U32)
        idxf = ph.sb("idxf", [P, TILES, 8])
        comb = [ph.sb(f"comb{i}", [P, TILES, E]) for i in range(2)]
        combT = [ph.sb(f"combT{i}", [E, S]) for i in range(2)]
        if top2:
            neg_exp = ph.sb("neg_exp", [P, TILES, 2])
            one_plus = ph.sb("one_plus", [P, TILES, 2])
            score = ph.sb("score", [P, TILES, 2])
            total = ph.sb("total", [P, TILES, 1])
            inv_total = ph.sb("inv_total", [P, TILES, 1])
            share = ph.sb("share", [P, TILES, 2])
            pick = [ph.sb(f"pick{i}", [P, TILES, EXPERTS]) for i in range(2)]
            neg_exp_done = ph.sem("neg_exp_done")
            one_plus_done = ph.sem("one_plus_done")
            score_done = ph.sem("score_done")
            total_done = ph.sem("total_done")
            inv_done = ph.sem("inv_done")
            share_done = ph.sem("share_done")
            pick_done = ph.sem("pick_done")
        h_ps = [ph.ps(f"h{i}", [P, S]) for i in range(4)]
        y_ps = [ph.ps(f"y{i}", [P, S]) for i in range(2)]
        t_ps = ph.ps("t", [P, S])
        c_ps = ph.ps("c", [P, S])
        lg_ps = t_ps[:, 0:TILES * EXPERTS]
        ln = LayerNorm(ph, x, ident, t_ps)
        loaded = ph.sem("loaded")
        const_done = ph.sem("const_done")
        logits_ready = ph.sem("logits_ready")
        logits_done = ph.sem("logits_done")
        top_done = ph.sem("top_done")
        idx_done = ph.sem("idx_done")
        idxf_done = ph.sem("idxf_done")
        comb_done = ph.sem("comb_done")
        combT_ready = ph.sem("combT_ready")
        combT_done = ph.sem("combT_done")
        h_ready = ph.sem("h_ready")
        h_done = ph.sem("h_done")
        y_ready = ph.sem("y_ready")
        y_used = ph.sem("y_used")

        loads = [(w1[:], w["w1"]), (b1[:], w["b1"]), (w2[:], w["w2"]), (b2[:], w["b2"]), (wg[:], w["wg"]),
                 (bg[:], w["bg"].to_broadcast([P, TILES * EXPERTS]))]
        if x_in is not None:
            loads += [(rows_at(x, b).rearrange("p (t h) -> p t h", t=TILES), x_in[b]) for b in range(B)]
        all_loaded = 16 * len(loads)

        def ring(b, par, per, k, slots):
            return (par * per + k) % slots

        with nc.Block() as block:

            @block.sync
            def _(sp):
                for dst, src in loads:
                    sp.dma_start(dst, src).then_inc(loaded, 16)

            @block.gpsimd
            def _(pool):
                ln.pool_setup(pool)
                ln.pool_rstd(pool, 0)

                def body(b, par):
                    if has_next(b):
                        ln.pool_rstd(pool, b + 1)
                over_batches(pool, body)

            @block.tensor
            def _(pe):
                pe.sem_inc(y_ready, Y_PRE)

                def router(b, par):
                    pe.wait_ge(ln.xnT_done, b + 1)
                    for t in range(TILES):
                        last = pe.matmul(lg_ps[:, t * EXPERTS:(t + 1) * EXPERTS],
                                         ln.xnT[par][:, t * P:(t + 1) * P], wg[:], start=True, stop=True)
                    last.then_inc(logits_ready, 1)

                def transpose(b):
                    pe.wait_ge(logits_done, b)
                    ln.pe_transpose(pe, b)

                def comb_transpose(b, par):
                    pe.wait_ge(comb_done, b + 1)
                    pe.wait_ge(combT_done, b)
                    for t in range(TILES):
                        last = pe.matmul(c_ps[0:E, t * P:(t + 1) * P], comb[par][:, t, :], ident[:],
                                         start=True, stop=True)
                    last.then_inc(combT_ready, 1)

                def up(b, par, e):
                    for c in range(C):
                        k = e * C + c
                        pe.wait_ge(h_done, H_PRE + b * (E * C) + k - 3)
                        pe.matmul(h_ps[k % 4][:], w1[:, k * P:(k + 1) * P], ln.xnT[par][:],
                                  start=True, stop=True).then_inc(h_ready, 1)

                def down(b, par, e):
                    y = y_ps[ring(b, par, units, e, 2)]
                    h = hT[ring(b, par, E, e, 2)]
                    pe.wait_ge(h_done, H_PRE + b * (E * C) + (e + 1) * C)
                    pe.wait_ge(y_used, Y_PRE + b * units + e - 1)
                    for t in range(TILES):
                        for c in range(C):
                            k = e * C + c
                            last = pe.matmul(y[:, t * D:(t + 1) * D], h[:, c, t * P:(t + 1) * P],
                                             w2[:, k * D:(k + 1) * D], start=c == 0, stop=c == C - 1)
                    last.then_inc(y_ready, 1)

                def bias_term(b, par):
                    y = y_ps[ring(b, par, units, E, 2)]
                    pe.wait_ge(combT_done, b + 1)
                    pe.wait_ge(y_used, Y_PRE + b * units + E - 1)
                    for t in range(TILES):
                        last = pe.matmul(y[:, t * D:(t + 1) * D], combT[par][:, t * P:(t + 1) * P], b2[:],
                                         start=True, stop=True)
                    last.then_inc(y_ready, 1)

                pe.wait_ge(loaded, all_loaded)
                pe.wait_ge(const_done, 1)
                transpose(0)
                router(0, 0)
                comb_transpose(0, 0)

                def body(b, par):
                    for e in range(E):
                        if e == 0:
                            pe.wait_ge(ln.xnT_done, b + 1)
                        up(b, par, e)
                        if e:
                            down(b, par, e - 1)
                        if has_next(b):
                            if e == 3:
                                transpose(b + 1)
                            if e == 5:
                                router(b + 1, 1 - par)
                            if e == 7:
                                comb_transpose(b + 1, 1 - par)
                    down(b, par, E - 1)
                    bias_term(b, par)
                over_batches(pe, body)

            @block.scalar
            def _(act):
                act.sem_inc(h_done, H_PRE)
                act.wait_ge(loaded, all_loaded)

                def sigmoid_exp(b):
                    if top2:
                        act.wait_ge(top_done, b + 1)
                        act.activation(neg_exp[:], top[:, :, 0:2], ACT.Exp, scale=-1.0).then_inc(neg_exp_done, 1)

                ln.act_copy(act, 0, 0)
                sigmoid_exp(0)

                def body(b, par):
                    for e in range(E):
                        h = hT[ring(b, par, E, e, 2)]
                        before = e - 2 if e >= 2 else e - 3
                        act.wait_ge(y_ready, Y_PRE + b * units + before + 1)
                        for c in range(C):
                            k = e * C + c
                            act.wait_ge(h_ready, b * (E * C) + k + 1)
                            act.activation(h[:, c, :], h_ps[k % 4][:], ACT.Gelu, bias=b1[:, k:k + 1],
                                           scale=1.0).then_inc(h_done, 1)
                        if has_next(b):
                            if e == 4:
                                ln.act_copy(act, b + 1, 1 - par)
                            if e == 6:
                                sigmoid_exp(b + 1)
                over_batches(act, body)

            @block.vector
            def _(dve):
                dve.sem_inc(y_used, Y_PRE)
                if top2:
                    for i in range(2):
                        last = dve.memset(comb[i][:, :, EXPERTS:E], WEIGHT * float(np.float32(0.1)))
                    last.then_inc(const_done, 1)
                else:
                    dve.sem_inc(const_done, 1)
                dve.wait_ge(loaded, all_loaded)

                def choose(b, par):
                    dve.wait_ge(logits_ready, b + 1)
                    dve.tensor_tensor(logits[:], lg_ps, bg[:], ALU.add).then_inc(logits_done, 1)
                    wait_apart(dve, logits_done, b + 1, ln.passed)
                    for t in range(TILES):
                        last = dve.max(top[:, t, :], logits[:, t * 8:(t + 1) * 8])
                    last.then_inc(top_done, 1)
                    wait_apart(dve, top_done, b + 1, ln.passed)
                    for t in range(TILES):
                        last = dve.max_index(idx[:, t, :], top[:, t, :], logits[:, t * 8:(t + 1) * 8])
                    last.then_inc(idx_done, 1)
                    dve.wait_ge(idx_done, b + 1)
                    dve.tensor_copy(idxf[:], idx[:]).then_inc(idxf_done, 1)
                    dve.wait_ge(idxf_done, b + 1)
                    if not top2:
                        for t in range(TILES):
                            last = dve.tensor_scalar(comb[par][:, t, :], iota[:], idxf[:, t, 0:1], WEIGHT,
                                                     ALU.is_equal, ALU.mult)
                        last.then_inc(comb_done, 1)

                def weigh(b, par):
                    if top2:
                        dve.wait_ge(neg_exp_done, b + 1)
                        dve.tensor_scalar(one_plus[:], neg_exp[:], 1.0, None, ALU.add).then_inc(one_plus_done, 1)
                        dve.wait_ge(one_plus_done, b + 1)
                        dve.reciprocal(score[:], one_plus[:]).then_inc(score_done, 1)
                        dve.wait_ge(score_done, b + 1)
                        dve.scalar_tensor_tensor(total[:], score[:, :, 0:1], 1e-6, score[:, :, 1:2], ALU.add,
                                                 ALU.add).then_inc(total_done, 1)
                        dve.wait_ge(total_done, b + 1)
                        dve.reciprocal(inv_total[:], total[:]).then_inc(inv_done, 1)
                        dve.wait_ge(inv_done, b + 1)
                        dve.scalar_tensor_tensor(share[:], score[:], WEIGHT,
                                                 inv_total[:].to_broadcast([P, TILES, 2]), ALU.mult,
                                                 ALU.mult).then_inc(share_done, 1)
                        dve.wait_ge(share_done, b + 1)
                        for i in range(2):
                            for t in range(TILES):
                                last = dve.tensor_scalar(pick[i][:, t, :], iota[:], idxf[:, t, i:i + 1],
                                                         share[:, t, i:i + 1], ALU.is_equal, ALU.mult)
                        last.then_inc(pick_done, 1)
                        dve.wait_ge(pick_done, b + 1)
                        dve.tensor_tensor(comb[par][:, :, 0:EXPERTS], pick[0][:], pick[1][:],
                                          ALU.add).then_inc(comb_done, 1)

                def comb_copy(b, par):
                    dve.wait_ge(combT_ready, b + 1)
                    dve.tensor_copy(combT[par][:], c_ps[0:E, :]).then_inc(combT_done, 1)

                def add(b, par, e):
                    y = y_ps[ring(b, par, units, e, 2)]
                    dve.wait_ge(y_ready, Y_PRE + b * units + e + 1)
                    dve.wait_ge(y_used, Y_PRE + b * units + e)
                    if e < E:
                        for t in range(TILES):
                            last = dve.scalar_tensor_tensor(tile_at(x, b, t), y[:, t * D:(t + 1) * D],
                                                            comb[par][:, t, e:e + 1], tile_at(x, b, t),
                                                            ALU.mult, ALU.add)
                    else:
                        last = dve.tensor_tensor(rows_at(x, b), y[:], rows_at(x, b), ALU.add)
                    last.then_inc(y_used, 1)

                ln.dve_stats(dve, 0)
                ln.dve_norm(dve, 0)
                choose(0, 0)
                weigh(0, 0)
                comb_copy(0, 0)

                def body(b, par):
                    dve.wait_ge(comb_done, b + 1)
                    for e in range(E):
                        if has_next(b):
                            if e == 0:
                                ln.dve_stats(dve, b + 1)
                            if e == 1:
                                ln.dve_norm(dve, b + 1)
                            if e == 5:
                                choose(b + 1, 1 - par)
                            if e == 6:
                                weigh(b + 1, 1 - par)
                            if e == 7:
                                comb_copy(b + 1, 1 - par)
                        add(b, par, e)
                    add(b, par, E)
                over_batches(dve, body)


def decay_attention_phase(nc, x, ident, w):
    with Phase(nc, "dec") as ph:
        wrkv = ph.sb("wrkv", [P, 3 * D])
        brkv = ph.sb("brkv", [P, 3])
        wo = ph.sb("wo", [P, D])
        bo = ph.sb("bo", [P, S])
        nu_log = ph.sb("nu_log", [P, 1])
        gamma_log = ph.sb("gamma_log", [P, 1])
        nu = ph.sb("nu", [P, 1])
        lam = ph.sb("lam", [P, 1])
        egamma = ph.sb("egamma", [P, 1])
        gamma = ph.sb("gamma", [P, 1])
        neg_br = ph.sb("neg_br", [P, 1])
        zeros = ph.sb("zeros", [P, S])
        lam_row = ph.sb("lam_row", [P, S])
        er = [ph.sb(f"er{i}", [P, S]) for i in range(2)]
        k = [ph.sb(f"k{i}", [P, S]) for i in range(2)]
        er1 = ph.sb("one_plus_er", [P, S])
        kv = ph.sb("kv", [P, S])
        u1 = ph.sb("u1", [P, S])
        u2 = ph.sb("u2", [P, S])
        num = ph.sb("num", [P, S])
        den = ph.sb("den", [P, S])
        den_r = ph.sb("den_r", [P, S])
        inv = ph.sb("inv", [P, S])
        mixed = ph.sb("mixed", [P, S])
        rkv_ps = [[ph.ps(f"{n}_ps{i}", [P, S]) for n in "rkv"] for i in range(2)]
        t_ps = ph.ps("t", [P, S])
        o_ps = ph.ps("o", [P, S])
        ln = LayerNorm(ph, x, ident, t_ps)
        loaded = ph.sem("loaded")
        nu_done, lam_done, sum_done, egamma_done = ph.sem("nu"), ph.sem("lam"), ph.sem("nugamma"), ph.sem("egamma")
        const_done = ph.sem("const_done")
        lam_row_done = ph.sem("lam_row_done")
        rkv_ready = ph.sem("rkv_ready")
        act_done = ph.sem("act_done")
        er1_done = ph.sem("er1_done")
        kv_done = ph.sem("kv_done")
        scan_done = ph.sem("scan_done")
        frac_done = ph.sem("frac_done")
        den_r_done = ph.sem("den_r_done")
        er1_used = ph.sem("er1_used")
        rkv_used = ph.sem("rkv_used")
        inv_done = ph.sem("inv_done")
        mixed_done = ph.sem("mixed_done")
        o_ready = ph.sem("o_ready")
        o_used = ph.sem("o_used")
        x_done = ph.sem("x_done")
        loads = [(wrkv[:], w["wrkv"]), (brkv[:], w["brkv"]), (wo[:], w["wo"]),
                 (bo[:], w["bo"].to_broadcast([P, S])), (nu_log[:], w["nu_log"]),
                 (gamma_log[:], w["gamma_log"])]
        all_loaded = 16 * len(loads)

        with nc.Block() as block:

            @block.sync
            def _(sp):
                for dst, src in loads:
                    sp.dma_start(dst, src).then_inc(loaded, 16)

            @block.gpsimd
            def _(pool):
                ln.pool_setup(pool)
                pool.wait_ge(loaded, all_loaded)
                ln.pool_rstd(pool, 0)

                def body(b, par):
                    pool.wait_ge(act_done, b + 1)
                    wait_apart(pool, er1_used, b + 1, ln.passed)
                    pool.tensor_scalar(er1[:], er[par][:], 1.0, None, ALU.add).then_inc(er1_done, 1)
                    if has_next(b):
                        ln.pool_rstd(pool, b + 1)
                    pool.wait_ge(o_used, b + 1)
                    pool.tensor_tensor(rows_at(x, b), rows_at(x, b), bo[:], ALU.add).then_inc(x_done, 1)
                over_batches(pool, body)

            @block.tensor
            def _(pe):
                def project(b, par):
                    pe.wait_ge(ln.xnT_done, b + 1)
                    for i in range(3):
                        last = pe.matmul(rkv_ps[par][i][:], wrkv[:, i * D:(i + 1) * D], ln.xnT[par][:],
                                         start=True, stop=True)
                    last.then_inc(rkv_ready, 1)

                pe.wait_ge(loaded, all_loaded)
                ln.pe_transpose(pe, 0)
                project(0, 0)

                def body(b, par):
                    if has_next(b):
                        ln.pe_transpose(pe, b + 1)
                        pe.wait_ge(rkv_used, b + 1)
                        project(b + 1, 1 - par)
                    pe.wait_ge(mixed_done, b + 1)
                    for t in range(TILES):
                        last = pe.matmul(o_ps[:, t * D:(t + 1) * D], mixed[:, t * P:(t + 1) * P], wo[:],
                                         start=True, stop=True)
                    last.then_inc(o_ready, 1)
                over_batches(pe, body)

            @block.scalar
            def _(act):
                act.wait_ge(loaded, all_loaded)
                act.activation(nu[:], nu_log[:], ACT.Exp).then_inc(nu_done, 1)
                act.wait_ge(nu_done, 1)
                act.activation(lam[:], nu[:], ACT.Exp, scale=-1.0).then_inc(lam_done, 1)
                act.activation(egamma[:], nu_log[:], ACT.Exp, bias=gamma_log[:]).then_inc(egamma_done, 1)
                act.wait_ge(const_done, 1)
                act.wait_ge(lam_done, 1)
                act.activation(lam_row[:], zeros[:], ACT.Identity, bias=lam[:]).then_inc(lam_row_done, 1)
                ln.act_copy(act, 0, 0)

                def body(b, par):
                    act.wait_ge(rkv_ready, b + 1)
                    act.activation(er[par][:], rkv_ps[par][0][:], ACT.Exp, bias=neg_br[:], scale=-1.0)
                    act.activation(k[par][:], rkv_ps[par][1][:], ACT.Exp, bias=brkv[:, 1:2]).then_inc(act_done, 1)
                    if has_next(b):
                        ln.act_copy(act, b + 1, 1 - par)
                over_batches(act, body)

            @block.vector
            def _(dve):
                dve.memset(zeros[:], 0.0)
                dve.sem_inc(er1_used, 1)
                dve.sem_inc(rkv_used, 1)
                dve.wait_ge(loaded, all_loaded)
                dve.tensor_scalar(neg_br[:], brkv[:, 0:1], -1.0, None, ALU.mult).then_inc(const_done, 1)
                dve.wait_ge(egamma_done, 1)
                dve.tensor_scalar(gamma[:], egamma[:], -1.0, None, ALU.add).then_inc(sum_done, 1)
                dve.wait_ge(sum_done, 1)
                dve.wait_ge(lam_row_done, 1)
                ln.dve_stats(dve, 0)
                ln.dve_norm(dve, 0)

                def body(b, par):
                    if has_next(b):
                        ln.dve_stats(dve, b + 1)
                    dve.wait_ge(act_done, b + 1)
                    dve.scalar_tensor_tensor(kv[:], rkv_ps[par][2][:], brkv[:, 2:3], k[par][:], ALU.add,
                                             ALU.mult).then_inc(kv_done, 1)
                    dve.tensor_tensor_scan(u2[:], lam_row[:], k[par][:], 0.0, ALU.mult, ALU.add)
                    dve.wait_ge(kv_done, b + 1)
                    dve.tensor_tensor_scan(u1[:], lam_row[:], kv[:], 0.0, ALU.mult, ALU.add).then_inc(scan_done, 1)
                    if has_next(b):
                        ln.dve_norm(dve, b + 1)
                    dve.wait_ge(scan_done, b + 1)
                    dve.scalar_tensor_tensor(den[:], k[par][:], gamma[:], u2[:], ALU.mult, ALU.add)
                    dve.scalar_tensor_tensor(num[:], kv[:], gamma[:], u1[:], ALU.mult,
                                             ALU.add).then_inc(frac_done, 1)
                    dve.wait_ge(frac_done, b + 1)
                    dve.wait_ge(er1_done, b + 1)
                    dve.scalar_tensor_tensor(den_r[:], den[:], 1e-6, er1[:], ALU.add,
                                             ALU.mult).then_inc(den_r_done, 1)
                    dve.wait_ge(den_r_done, b + 1)
                    dve.sem_inc(er1_used, 1)
                    dve.reciprocal(inv[:], den_r[:]).then_inc(inv_done, 1)
                    dve.wait_ge(inv_done, b + 1)
                    dve.sem_inc(rkv_used, 1)
                    dve.tensor_tensor(mixed[:], num[:], inv[:], ALU.mult).then_inc(mixed_done, 1)
                    dve.wait_ge(o_ready, b + 1)
                    dve.tensor_tensor(rows_at(x, b), o_ps[:], rows_at(x, b), ALU.add).then_inc(o_used, 1)
                over_batches(dve, body)


def qkv_phase(nc, x, ident, w, v_all, scratch):
    SCALE = float(1.0 / np.sqrt(np.float32(HD)))
    FREE = 2 * 48
    with Phase(nc, "qkv") as ph:
        wq, wk, wv, wp = (ph.sb(n, [P, D]) for n in ("wq", "wk", "wv", "wp"))
        bq, bk, bp, u, v = (ph.sb(n, [P, 1]) for n in ("bq", "bk", "bp", "u", "v"))
        bv = ph.sb("bv", [P, S])
        embT = ph.sb("embT", [P, S])
        bias_u, bias_v = ph.sb("bias_u", [P, 1]), ph.sb("bias_v", [P, 1])
        sum_u, sum_v = ph.sb("sum_u", [P, 1]), ph.sb("sum_v", [P, 1])
        qu = [ph.sb(f"qu{i}", [P, ROWS, GROUPS]) for i in range(2)]
        qv = [ph.sb(f"qv{i}", [P, ROWS, GROUPS]) for i in range(2)]
        kT = [ph.sb(f"kT{i}", [P, S]) for i in range(2)]
        pos = ph.sb("pos", [P, POS_W])
        q_ps = [ph.ps(f"qps{i}", [P, S]) for i in range(2)]
        k_ps = [ph.ps(f"kps{i}", [P, S]) for i in range(2)]
        v_ps = [ph.ps(f"vps{i}", [P, S]) for i in range(2)]
        t_ps = ph.ps("t", [P, S])
        pos_ps = ph.ps("pos_ps", [P, S])
        ln = LayerNorm(ph, x, ident, t_ps)
        loaded = ph.sem("loaded")
        sums_done = ph.sem("sums_done")
        bias_done = ph.sem("bias_done")
        pos_ready = ph.sem("pos_ready")
        pos_done = ph.sem("pos_done")
        qkv_ready = ph.sem("qkv_ready")
        qk_done = ph.sem("qk_done")
        v_done = ph.sem("v_done")
        stored = ph.sem("stored")
        stored_qk = ph.sem("stored_qk")
        loads = [(wq[:], w["wq"]), (wk[:], w["wk"]), (wv[:], w["wv"]), (wp[:], w["wp"]), (bq[:], w["bq"]),
                 (bk[:], w["bk"]), (bp[:], w["bp"]), (u[:], w["u"]), (v[:], w["v"]),
                 (bv[:], w["bv"].to_broadcast([P, S])), (embT[:], w["embT"])]
        all_loaded = 16 * len(loads)
        v_out = v_all[:].rearrange("p (j h b c) -> p j h b c", j=TILES, h=HEADS, b=B)

        with nc.Block() as block:

            @block.sync
            def _(sp):
                sp.sem_inc(stored_qk, FREE)
                for dst, src in loads:
                    sp.dma_start(dst, src).then_inc(loaded, 16)
                for b in range(B):
                    sp.dma_start(scratch["x_rows"][b], rows_at(x, b).rearrange("p (t h) -> p t h", t=TILES))\
                        .then_inc(stored, 16)
                sp.wait_ge(pos_done, 2)
                sp.dma_start(scratch["pos"], pos[:]).then_inc(stored, 16)

                with sp.Fori(0, B // 2) as i:
                    for par in range(2):
                        b = 2 * i + par
                        wait_apart(sp, qk_done, 1 + b + 1, ln.passed)
                        sp.dma_start(scratch["qu"][:, bass.ds(b * S, S)],
                                     qu[par][:].rearrange("p r g -> p (r g)")).then_inc(stored_qk, 16)
                        sp.dma_start(scratch["qv"][:, :, bass.ds(b * GROUPS, GROUPS)],
                                     qv[par][:]).then_inc(stored_qk, 16)
                        sp.dma_start(scratch["k"][:, bass.ds(b * S, S)], kT[par][:]).then_inc(stored_qk, 16)
                        wait_apart(sp, stored_qk, FREE + (b + 1) * 48, ln.passed)
                sp.wait_ge(stored, 16 * (B + 1))

            @block.gpsimd
            def _(pool):
                ln.pool_setup(pool)
                pool.memset(pos[:, 0:POS_0], 0.0)
                pool.memset(pos[:, POS_0 + S:POS_W], 0.0).then_inc(pos_done, 1)
                ln.pool_rstd(pool, 0)

                def body(b, par):
                    if has_next(b):
                        ln.pool_rstd(pool, b + 1)
                over_batches(pool, body)

            @block.tensor
            def _(pe):
                pe.wait_ge(loaded, all_loaded)
                pe.matmul(pos_ps[:], wp[:], embT[:], start=True, stop=True).then_inc(pos_ready, 1)
                ln.pe_transpose(pe, 0)

                def body(b, par):
                    pe.wait_ge(ln.xnT_done, b + 1)
                    pe.matmul(q_ps[par][:], wq[:], ln.xnT[par][:], start=True, stop=True)
                    pe.matmul(k_ps[par][:], wk[:], ln.xnT[par][:], start=True, stop=True)
                    for t in range(TILES):
                        last = pe.matmul(v_ps[par][:, t * D:(t + 1) * D], ln.xnT[par][:, t * P:(t + 1) * P],
                                         wv[:], start=True, stop=True)
                    last.then_inc(qkv_ready, 1)
                    if has_next(b):
                        ln.pe_transpose(pe, b + 1)
                        pe.wait_ge(v_done, 1 + b)
                        pe.wait_ge(qk_done, 1 + b)
                over_batches(pe, body)

            @block.scalar
            def _(act):
                act.sem_inc(qk_done, 1)
                act.wait_ge(bias_done, 1)
                act.wait_ge(pos_ready, 1)
                act.activation(pos[:, POS_0:POS_0 + S], pos_ps[:], ACT.Identity, bias=bp[:]).then_inc(pos_done, 1)
                ln.act_copy(act, 0, 0)

                def body(b, par):
                    act.wait_ge(qkv_ready, b + 1)
                    act.wait_ge(stored_qk, FREE + (b - 1) * 48)
                    q_view = q_ps[par][:].rearrange("p (g r) -> p r g", r=ROWS)
                    act.activation(qu[par][:], q_view, ACT.Identity, bias=bias_u[:], scale=SCALE)
                    act.activation(qv[par][:], q_view, ACT.Identity, bias=bias_v[:], scale=SCALE)
                    act.activation(kT[par][:], k_ps[par][:], ACT.Identity, bias=bk[:]).then_inc(qk_done, 1)
                    if has_next(b):
                        ln.act_copy(act, b + 1, 1 - par)
                over_batches(act, body)

            @block.vector
            def _(dve):
                dve.sem_inc(v_done, 1)
                dve.wait_ge(loaded, all_loaded)
                dve.tensor_tensor(sum_u[:], bq[:], u[:], ALU.add)
                dve.tensor_tensor(sum_v[:], bq[:], v[:], ALU.add).then_inc(sums_done, 1)
                dve.wait_ge(sums_done, 1)
                dve.tensor_scalar(bias_u[:], sum_u[:], SCALE, None, ALU.mult)
                dve.tensor_scalar(bias_v[:], sum_v[:], SCALE, None, ALU.mult).then_inc(bias_done, 1)
                ln.dve_stats(dve, 0)
                ln.dve_norm(dve, 0)

                def body(b, par):
                    if has_next(b):
                        ln.dve_stats(dve, b + 1)
                        ln.dve_norm(dve, b + 1)
                    dve.wait_ge(qkv_ready, b + 1)
                    for t in range(TILES):
                        last = dve.tensor_tensor(
                            v_slice(v_all, t, b),
                            v_ps[par][:, t * D:(t + 1) * D].rearrange("p (h c) -> p h c", h=HEADS),
                            bv[:, 0:D].rearrange("p (h c) -> p h c", h=HEADS), ALU.add)
                    last.then_inc(v_done, 1)
                over_batches(dve, body)


def v_slice(v_all, t, b):
    flat = v_all[:].rearrange("p (j h b c) -> p j h b c", j=TILES, h=HEADS, b=B)
    return flat[:, t, :, bass.ds(b, 1), :].rearrange("p h b c -> p h (b c)")


def relative_attention_phase(nc, ident, w, v_all, o_all, scratch):
    PRE = 4
    N_TILES = 2 * GROUPS
    N_BLOCKS = N_TILES // 8
    with Phase(nc, "rel") as ph:
        left = [ph.sb(f"left{i}", [P, ROWS * HALF * GROUPS]) for i in range(2)]
        right = [ph.sb(f"right{i}", [P, ROWS * HALF * GROUPS]) for i in range(2)]
        cont = [ph.sb(f"cont{i}", [P, HALF * ROWS * GROUPS]) for i in range(2)]
        keys = [ph.sb(f"keys{i}", [P, S]) for i in range(2)]
        pos_l = [ph.sb(f"pos_l{i}", [P, S]) for i in range(2)]
        pos_r = [ph.sb(f"pos_r{i}", [P, S]) for i in range(2)]
        mask = ph.sb("mask", [P, HALF])
        neg_max = ph.sb("neg_max", [P, 4])
        row_sum = ph.sb("row_sum", [P, N_TILES])
        probs = [ph.sb(f"probs{i}", [P, S]) for i in range(4)]
        probsT = [ph.sb(f"probsT{i}", [P, S]) for i in range(2)]
        own = ph.sb("own", [P, 8 * HALF * HD])
        picked = ph.sb("picked", [P, 8 * HD])
        inv_sum = ph.sb("inv_sum", [P, 8, 1])
        s_ps = [ph.ps(f"s{i}", [P, S]) for i in range(4)]
        t_ps = [ph.ps(f"tps{i}", [P, S]) for i in range(2)]
        o_ps = [ph.ps(f"o{i}", [P, S]) for i in range(2)]
        zeroed = ph.sem("zeroed")
        passed = ph.sem("passed")
        mask_loaded = ph.sem("mask_loaded")
        loaded = [ph.sem(f"loaded{i}") for i in range(2)]
        s_ready = ph.sem("s_ready")
        max_done = ph.sem("max_done")
        p_done = ph.sem("p_done")
        t_ready = ph.sem("t_ready")
        pt_done = ph.sem("pt_done")
        pv_done = ph.sem("pv_done")
        own_done = ph.sem("own_done")
        picked_done = ph.sem("picked_done")
        o_done = ph.sem("o_done")
        LOADS = 3 + 2 * ROWS + HALF + 1

        with nc.Block() as block:

            @block.sync
            def _(sp):
                sp.dma_start(mask[:], w["mask"]).then_inc(mask_loaded, 16)

                def load(h, half):
                    done = loaded[half]

                    def get(dst, src):
                        sp.dma_start(dst, src).then_inc(done, 16)

                    c0 = h * HD
                    get(pos_r[half][:], pos_table(scratch, h, 0))
                    get(pos_l[half][:], pos_table(scratch, h, POS_0))
                    get(keys[half][0:HALF * HD, :], key_rows(scratch, h, half))
                    for b in range(HALF):
                        get(cont[half][b * HD:(b + 1) * HD, :].rearrange("c (r b g) -> c r b g", r=ROWS, b=HALF)
                            [:, :, b, :],
                            scratch["qu"][bass.ds(c0, HD), (half * HALF + b) * S:(half * HALF + b + 1) * S]
                            .rearrange("c (r g) -> c r g", r=ROWS))
                    plane = HALF * GROUPS
                    for n in range(ROWS):
                        s = ROWS - 1 - n
                        rows = slice(n * HD, (n + 1) * HD)
                        mine = slice(half * plane, (half + 1) * plane)
                        get(left[half][rows, s * plane:(s + 1) * plane], scratch["qv"][bass.ds(c0, HD), s, mine])
                        if s < ROWS - 1:
                            get(right[half][rows, s * plane:(s + 1) * plane],
                                scratch["qv"][bass.ds(c0, HD), s + 1, mine])
                        else:
                            dst = right[half][rows, s * plane:(s + 1) * plane].rearrange("c (b g) -> c b g", b=HALF)
                            src = scratch["qv"][bass.ds(c0, HD), 0, mine].rearrange("c (b g) -> c b g", b=HALF)
                            for b0 in (0, HALF // 2):
                                get(dst[:, b0:b0 + HALF // 2, 0:GROUPS - 1],
                                    src[:, b0:b0 + HALF // 2, 1:GROUPS])

                sp.wait_ge(zeroed, 6 + 2)
                load(0, 0)
                load(0, 1)
                with sp.Fori(0, HEADS - 1) as h:
                    for half in range(2):
                        wait_apart(sp, s_ready, h * N_TILES + (half + 1) * GROUPS, passed)
                        load(h + 1, half)

            @block.gpsimd
            def _(pool):
                for half in range(2):
                    for buf in (cont, left, right):
                        pool.memset(buf[half][:], 0.0).then_inc(zeroed, 1)

            @block.tensor
            def _(pe):
                def scores(h, n):
                    half, g = divmod(n, GROUPS)
                    i0 = g * ROWS
                    N = h * N_TILES + n
                    if g == 0:
                        pe.wait_ge(loaded[half], (h + 1) * (LOADS * 16))
                    pe.wait_ge(p_done, PRE + N - 3)
                    out = s_ps[n % 4]
                    pe.matmul(out[:], cont[half][:].rearrange("p (r g) -> p r g", g=GROUPS)[:, :, g],
                              keys[half][:], start=True, stop=False)
                    pe.matmul(out[:, 0:i0 + ROWS],
                              left[half][:].rearrange("p (r g) -> p r g", g=GROUPS)[:, :, g],
                              pos_l[half][:, S - ROWS - i0:S], start=False, stop=False)
                    pe.matmul(out[:, i0:S],
                              right[half][:].rearrange("p (r g) -> p r g", g=GROUPS)[:, :, g],
                              pos_r[half][:, 0:S - i0], start=False, stop=True).then_inc(s_ready, 1)

                def transpose(h, n):
                    N = h * N_TILES + n
                    pe.wait_ge(p_done, PRE + N + 1)
                    pe.wait_ge(pt_done, PRE + N - 1)
                    for j in range(TILES):
                        last = pe.transpose(t_ps[n % 2][:, j * P:(j + 1) * P], probs[n % 4][:, j * P:(j + 1) * P],
                                            ident[:])
                    last.then_inc(t_ready, 1)

                def values(h, n):
                    N = h * N_TILES + n
                    half = n // GROUPS
                    pe.wait_ge(pt_done, PRE + N + 1)
                    if n % 8 == 0:
                        pe.wait_ge(o_done, PRE + h * N_BLOCKS + n // 8 - 1)
                    out = o_ps[n // 8 % 2][:, (n % 8) * (HALF * HD):(n % 8 + 1) * (HALF * HD)]
                    for j in range(TILES):
                        start = j * (HEADS * B * HD) + half * (HALF * HD)
                        last = pe.matmul(out, probsT[n % 2][:, j * P:(j + 1) * P],
                                         v_all[:, bass.ds(h * (B * HD) + start, HALF * HD)],
                                         start=j == 0, stop=j == TILES - 1)
                    last.then_inc(pv_done, 1)

                pe.sem_inc(pv_done, PRE)
                pe.sem_inc(t_ready, PRE)
                with pe.Fori(0, HEADS) as h:
                    for n in range(N_TILES + 3):
                        if n < N_TILES:
                            scores(h, n)
                        if 2 <= n < N_TILES + 2:
                            transpose(h, n - 2)
                        if n >= 3:
                            values(h, n - 3)

            @block.scalar
            def _(act):
                act.sem_inc(p_done, PRE)
                with act.Fori(0, HEADS) as h:
                    for n in range(N_TILES):
                        N = h * N_TILES + n
                        act.wait_ge(max_done, N + 1)
                        act.wait_ge(t_ready, PRE + N - 3)
                        act.activation(probs[n % 4][:], s_ps[n % 4][:], ACT.Exp, bias=neg_max[:, n % 4:n % 4 + 1],
                                       scale=1.0, accum_out=row_sum[:, n:n + 1]).then_inc(p_done, 1)

            @block.vector
            def _(dve):
                dve.sem_inc(pt_done, PRE)
                dve.sem_inc(o_done, PRE)
                for half in range(2):
                    dve.memset(keys[half][HALF * HD:P, :], 0.0).then_inc(zeroed, 1)
                dve.wait_ge(mask_loaded, 16)

                def maxima(h, n):
                    dve.wait_ge(s_ready, h * N_TILES + n + 1)
                    dve.tensor_reduce(neg_max[:, n % 4:n % 4 + 1], s_ps[n % 4][:], AX.X, ALU.max,
                                      negate=True).then_inc(max_done, 1)

                def copy(h, n):
                    N = h * N_TILES + n
                    dve.wait_ge(t_ready, PRE + N + 1)
                    dve.wait_ge(pv_done, PRE + N - 1)
                    dve.tensor_copy(probsT[n % 2][:], t_ps[n % 2][:]).then_inc(pt_done, 1)

                def outputs(h, g):
                    G = h * N_BLOCKS + g
                    dve.wait_ge(pv_done, PRE + 8 * G + 8)
                    dve.tensor_tensor(
                        own[:].rearrange("p (a b c) -> p a b c", a=8, b=HALF),
                        o_ps[g % 2][:].rearrange("p (a b c) -> p a b c", a=8, b=HALF),
                        mask[:].rearrange("p (a b c) -> p a b c", a=1, c=1).to_broadcast([P, 8, HALF, HD]),
                        ALU.mult).then_inc(own_done, 1)
                    dve.reciprocal(inv_sum[:, :, 0], row_sum[:, 8 * g:8 * g + 8])
                    dve.wait_ge(own_done, G + 1)
                    dve.tensor_reduce(picked[:].rearrange("p (a c) -> p a c", a=8),
                                      own[:].rearrange("p (a b c) -> p a c b", a=8, b=HALF), AX.X,
                                      ALU.add).then_inc(picked_done, 1)
                    dve.wait_ge(picked_done, G + 1)
                    dve.tensor_tensor(
                        o_all[:].rearrange("p (a e) -> p a e", e=D)[:, 8 * g:8 * g + 8, bass.ds(h * HD, HD)],
                        picked[:].rearrange("p (a c) -> p a c", a=8),
                        inv_sum[:].to_broadcast([P, 8, HD]), ALU.mult).then_inc(o_done, 1)

                with dve.Fori(0, HEADS) as h:
                    for n in range(N_TILES + 2):
                        if n < N_TILES:
                            maxima(h, n)
                        if n >= 2:
                            copy(h, n - 2)
                        if n >= 12 and n % 8 == 4:
                            outputs(h, n // 8 - 1)
                    outputs(h, N_BLOCKS - 1)


def pos_table(scratch, h, first):
    row = scratch["pos"].tensor
    return bass.AP(tensor=row, offset=h * (HD * POS_W) + first, ap=[[1, ROWS], [POS_W, HD], [1, S]])


def key_rows(scratch, h, half):
    return bass.AP(tensor=scratch["k"].tensor, offset=h * (HD * B * S) + half * HALF * S,
                   ap=[[S, HALF], [B * S, HD], [1, S]])


def out_projection_phase(nc, x, ident, w, o_all, scratch):
    with Phase(nc, "proj") as ph:
        wo = ph.sb("wo", [P, D])
        bo = ph.sb("bo", [P, S])
        oT = [ph.sb(f"oT{i}", [P, S]) for i in range(2)]
        t_ps = [ph.ps(f"tps{i}", [P, S]) for i in range(2)]
        y_ps = [ph.ps(f"y{i}", [P, S]) for i in range(2)]
        loaded = ph.sem("loaded")
        t_ready = ph.sem("t_ready")
        oT_done = ph.sem("oT_done")
        y_ready = ph.sem("y_ready")
        x_done = ph.sem("x_done")
        bias_done = ph.sem("bias_done")
        PRE = 2
        loads = [(wo[:], w["wo"]), (bo[:], w["bo"].to_broadcast([P, S]))]
        n_loads = len(loads) + 4 * B

        with nc.Block() as block:

            @block.sync
            def _(sp):
                for dst, src in loads:
                    sp.dma_start(dst, src).then_inc(loaded, 16)
                for half in range(2):
                    for g in range(GROUPS):
                        T = half * GROUPS + g
                        sp.dma_start(x[:, T * D:(T + 1) * D],
                                     token_rows(scratch["x"], half, g)).then_inc(loaded, 16)

            @block.tensor
            def _(pe):
                def body(b, par):
                    pe.wait_ge(oT_done, PRE + b - 1)
                    for t in range(TILES):
                        last = pe.transpose(t_ps[par][:, t * P:(t + 1) * P], tile_at(o_all, b, t), ident[:])
                    last.then_inc(t_ready, 1)
                    pe.wait_ge(oT_done, PRE + b + 1)
                    pe.wait_ge(x_done, PRE + b - 1)
                    for t in range(TILES):
                        last = pe.matmul(y_ps[par][:, t * D:(t + 1) * D], oT[par][:, t * P:(t + 1) * P], wo[:],
                                         start=True, stop=True)
                    last.then_inc(y_ready, 1)
                pe.wait_ge(loaded, 16 * n_loads)
                for b in range(B):
                    body(b, b % 2)

            @block.scalar
            def _(act):
                act.sem_inc(oT_done, PRE)

                def body(b, par):
                    act.wait_ge(t_ready, b + 1)
                    act.copy(oT[par][:], t_ps[par][:]).then_inc(oT_done, 1)
                over_batches(act, body)

            @block.gpsimd
            def _(pool):
                pool.wait_ge(loaded, 16 * n_loads)
                with pool.Fori(0, B) as b:
                    pool.tensor_tensor(rows_at(x, b), rows_at(x, b), bo[:], ALU.add).then_inc(bias_done, 1)

            @block.vector
            def _(dve):
                dve.sem_inc(x_done, PRE)

                def body(b, par):
                    dve.wait_ge(y_ready, b + 1)
                    dve.wait_ge(bias_done, b + 1)
                    dve.tensor_tensor(rows_at(x, b), y_ps[par][:], rows_at(x, b), ALU.add).then_inc(x_done, 1)
                over_batches(dve, body)


def token_rows(dram, half, g):
    return bass.AP(tensor=dram.tensor, offset=(half * HALF * S + g * ROWS) * D,
                   ap=[[D, ROWS], [S * D, HALF], [1, D]])


def build(nc, a, out):
    x_dram = nc.dram_tensor("x_scratch", [B * S, D], F32).ap()
    scratch = {
        "x": x_dram,
        "x_rows": x_dram.rearrange("(b t p) h -> b p t h", b=B, p=P),
        "qu": nc.dram_tensor("qu_scratch", [P, B * S], F32).ap(),
        "qv": nc.dram_tensor("qv_scratch", [P, ROWS, B * GROUPS], F32).ap(),
        "k": nc.dram_tensor("k_scratch", [P, B * S], F32).ap(),
        "pos": nc.dram_tensor("pos_scratch", [P, POS_W], F32).ap(),
    }
    x_in = a["x"].rearrange("b (t p) h -> b p t h", p=P)
    moe0 = {n: a["e0_" + n] for n in ("w1", "b1", "w2", "b2", "wg", "bg")}
    moe1 = {n: a["e1_" + n] for n in ("w1", "b1", "w2", "b2", "wg", "bg")}
    with Phase(nc, "all") as ph:
        x = ph.sb("x", [P, B * S])
        ident = ph.sb("ident", [P, P])
        iota = ph.sb("iota", [P, EXPERTS])
        ready = ph.sem("ready")
        with nc.Block() as block:
            @block.sync
            def _(sp):
                sp.dma_start(ident[:], a["ident"]).then_inc(ready, 16)
                sp.dma_start(iota[:], a["iota"].to_broadcast([P, EXPERTS])).then_inc(ready, 16)
                sp.wait_ge(ready, 32)

        flat = out.rearrange("b s h -> (b s) h")

        ffn_phase(nc, "moe0a", x, ident, iota, moe0, False, x_in=x_in)
        decay_attention_phase(nc, x, ident, {n: a["d_" + n] for n in ("wrkv", "brkv", "wo", "bo", "nu_log", "gamma_log")})
        ffn_phase(nc, "moe0b", x, ident, iota, moe0, False)
        ffn_phase(nc, "moe1a", x, ident, iota, moe1, True)
        o_all = x
        with Phase(nc, "attv") as attv:
            v_all = attv.sb("v_all", [P, B * S])
            qkv_phase(nc, x, ident, {n: a["r_" + n] for n in ("wq", "wk", "wv", "wp", "bq", "bk", "bp", "u", "v",
                                                              "bv", "embT")}, v_all, scratch)
            relative_attention_phase(nc, ident, {"mask": a["mask"]}, v_all, o_all, scratch)
        x = ph.sb("x_permuted", [P, B * S])
        out_projection_phase(nc, x, ident, {"wo": a["r_wo"], "bo": a["r_bo"]}, o_all, scratch)
        ffn_phase(nc, "moe1b", x, ident, iota, moe1, True)
        with Phase(nc, "fin") as fin:
            stored = fin.sem("stored")
            with nc.Block() as block:
                @block.sync
                def _(sp):
                    for half in range(2):
                        for g in range(GROUPS):
                            T = half * GROUPS + g
                            sp.dma_start(token_rows(flat, half, g), x[:, T * D:(T + 1) * D]).then_inc(stored, 16)
                    sp.wait_ge(stored, 16 * 2 * GROUPS)


def lay_out(i):
    def col(v):
        return np.ascontiguousarray(np.reshape(v, (D, 1)))

    def row(v, times):
        return np.ascontiguousarray(np.tile(np.reshape(v, (1, -1)), (1, times)))

    a = {"x": i["L0_attn_inputs"]}
    f = "L0_ffn_"
    a["e0_w1"] = i[f + "W1"].transpose(1, 0, 2).reshape(P, -1)
    a["e0_b1"] = i[f + "b1"].T
    a["e0_w2"] = i[f + "W2"].transpose(1, 0, 2).reshape(P, -1)
    a["e0_b2"] = i[f + "b2"]
    a["e0_wg"] = i[f + "Wg"]
    a["e0_bg"] = row(i[f + "bg"], TILES)
    f = "L1_ffn_"
    w1 = np.concatenate([i[f + "w1"], i[f + "sw1"][None]])
    w2 = np.concatenate([i[f + "w2"], i[f + "sw2"][None]])
    b1 = np.concatenate([i[f + "b1"], i[f + "sb1"][None]])
    a["e1_w1"] = w1.transpose(1, 0, 2).reshape(P, -1)
    a["e1_b1"] = b1.reshape(-1, P).T
    a["e1_w2"] = w2.reshape(9, 4, P, D).transpose(2, 0, 1, 3).reshape(P, -1)
    a["e1_b2"] = np.concatenate([i[f + "b2"], i[f + "sb2"][None]])
    a["e1_wg"] = i[f + "gate_w"].T
    a["e1_bg"] = row(i[f + "gate_b"], TILES)
    f = "L0_attn_"
    a["d_wrkv"] = i[f + "W_rkv"]
    a["d_brkv"] = i[f + "b_rkv"].reshape(3, D).T
    a["d_wo"] = i[f + "W_o"]
    a["d_bo"] = row(i[f + "b_o"], TILES)
    a["d_nu_log"] = col(i[f + "nu_log"])
    a["d_gamma_log"] = col(i[f + "gamma_log"])
    f = "L1_attn_"
    for n in "qkvp":
        a["r_w" + n] = i[f + "W" + n]
    a["r_wo"] = i[f + "Wo"]
    for n in "qkp":
        a["r_b" + n] = col(i[f + "b" + n])
    a["r_bv"] = row(i[f + "bv"], TILES)
    a["r_bo"] = row(i[f + "bo"], TILES)
    a["r_u"] = col(i[f + "u"])
    a["r_v"] = col(i[f + "v"])
    pos = np.arange(S, dtype=np.float32)
    freq = (1.0 / np.float32(10000.0) ** (np.float32(2.0) * np.arange(D // 2, dtype=np.float32) / np.float32(D))).astype(np.float32)
    ang = pos[:, None] * freq[None, :]
    a["r_embT"] = np.concatenate([np.sin(ang), np.cos(ang)], axis=-1).astype(np.float32).T
    a["ident"] = np.eye(P, dtype=np.float32)
    a["iota"] = np.arange(EXPERTS, dtype=np.float32)[None]
    a["mask"] = (np.arange(P)[:, None] % HALF == np.arange(HALF)[None]).astype(np.float32)
    return {n: np.ascontiguousarray(v) for n, v in a.items()}





def kernel(**inputs):
    import concourse.bacc as bacc
    from concourse.bass_utils import run_bass_kernel_spmd

    arrays = lay_out({n: np.asarray(v) for n, v in inputs.items()})
    nc = bacc.Bacc("TRN2", target_bir_lowering=False, num_devices=1)
    aps = {n: nc.dram_tensor(f"in_{n}", v.shape, mybir.dt.from_np(v.dtype), kind="ExternalInput").ap()
           for n, v in arrays.items()}
    out = nc.dram_tensor("out", (B, S, D), F32, kind="ExternalOutput").ap()
    build(nc, aps, out)
    r = run_bass_kernel_spmd(nc, [{f"in_{n}": v for n, v in arrays.items()}], core_ids=[0])
    return r.results[0]["out"]
```

```python
from contextlib import ExitStack

import numpy as np

import concourse.bass as bass
from concourse import mybir

F32 = mybir.dt.float32
U32 = mybir.dt.uint32
F32R = mybir.dt.float32r
ALU = mybir.AluOpType
ACT = mybir.ActivationFunctionType
AX = mybir.AxisListType

P = 128
B = 16
S = 512
D = 128
TILES = S // P
EXPERTS = 8
HEADS = 16
HD = D // HEADS
EPS = 1e-5

HALF = 8
ROWS = P // HALF
GROUPS = S // ROWS
SPANS = 2
SPAN = GROUPS // SPANS
POS_W = 560
POS_0 = 17
W_COLS = 2 * (EXPERTS + 1) * 4 * P
LO_ROW = 32


class Phase:

    def __init__(self, nc, name):
        self.nc, self.name, self.ctx, self.sems = nc, name, ExitStack(), []

    def __enter__(self):
        return self

    def __exit__(self, *exc):
        if self.sems and exc[0] is None:
            with self.nc.Block() as block:
                @block.sync
                def _(sp):
                    for sem in self.sems:
                        sp.sem_clear(sem)
        return self.ctx.__exit__(*exc)

    def sb(self, name, shape, dt=F32):
        return self.ctx.enter_context(self.nc.sbuf_tensor(f"{self.name}_{name}", shape, dt))

    def ps(self, name, shape):
        return self.ctx.enter_context(self.nc.psum_tensor(f"{self.name}_{name}", shape, F32))

    def sem(self, name):
        self.sems.append(self.ctx.enter_context(self.nc.semaphore(f"{self.name}_{name}")))
        return self.sems[-1]


def rows_at(x, b):
    return x[:, bass.ds(b * (TILES * D), TILES * D)]


def tile_at(x, b, t):
    return x[:, bass.ds(b * (TILES * D) + t * D, D)]


def over_batches(eng, body, peel_first=False):
    if peel_first:
        body(0, 0)
        body(1, 1)
    with eng.Fori(1 if peel_first else 0, B // 2 - 1) as i:
        body(2 * i, 0)
        body(2 * i + 1, 1)
    body(B - 2, 0)
    body(B - 1, 1)


def has_next(b):
    return not (isinstance(b, int) and b == B - 1)


def has_previous(b):
    return not (isinstance(b, int) and b == 0)


def wait_from(eng, sem, value):
    if not (isinstance(value, int) and value <= 0):
        eng.wait_ge(sem, value)


def wait_apart(eng, sem, value, passed):
    eng.wait_ge(sem, value)
    eng.sem_inc(passed, 1)


class LayerNorm:

    def __init__(self, ph, x, ident, transposed_psum):
        self.x, self.ident, self.xT = x, ident, transposed_psum
        self.stats = ph.sb("stats", [P, TILES * 6])
        self.mv = ph.sb("mv", [P, TILES * 2])
        self.var = ph.sb("var", [P, TILES])
        self.rstd = ph.sb("rstd", [P, TILES])
        self.minus_half = ph.sb("minus_half", [P, TILES])
        self.xn = ph.sb("xn", [P, S])
        self.xnT = [ph.sb(f"xnT{i}", [P, S]) for i in range(2)]
        self.passed = ph.sem("passed")
        self.stats_done = ph.sem("stats_done")
        self.mv_done = ph.sem("mv_done")
        self.const_done = ph.sem("ln_const")
        self.var_done = ph.sem("var_done")
        self.rstd_done = ph.sem("rstd_done")
        self.xn_done = ph.sem("xn_done")
        self.xT_ready = ph.sem("xT_ready")
        self.xnT_done = ph.sem("xnT_done")

    def pool_setup(self, pool):
        pool.memset(self.minus_half[:], -0.5).then_inc(self.const_done, 1)
        pool.wait_ge(self.const_done, 1)

    def dve_stats(self, dve, b):
        for t in range(TILES):
            last = dve.bn_stats(self.stats[:, t * 6:(t + 1) * 6], tile_at(self.x, b, t))
        last.then_inc(self.stats_done, 1)
        wait_apart(dve, self.stats_done, b + 1, self.passed)
        for t in range(TILES):
            last = dve.bn_aggr(self.mv[:, 2 * t:2 * t + 2], self.stats[:, t * 6:(t + 1) * 6])
        last.then_inc(self.mv_done, 1)

    def pool_rstd(self, pool, b):
        wait_apart(pool, self.mv_done, b + 1, self.passed)
        pool.tensor_scalar(self.var[:], self.mv[:].rearrange("p (t two) -> p t two", two=2)[:, :, 1],
                           EPS, None, ALU.add).then_inc(self.var_done, 1)
        pool.wait_ge(self.var_done, b + 1)
        pool.tensor_tensor(self.rstd[:], self.var[:], self.minus_half[:], ALU.pow).then_inc(self.rstd_done, 1)

    def dve_norm(self, dve, b):
        dve.wait_ge(self.rstd_done, b + 1)
        dve.wait_ge(self.xT_ready, b)
        for t in range(TILES):
            last = dve.tensor_scalar(self.xn[:, t * D:(t + 1) * D], tile_at(self.x, b, t),
                                     self.mv[:, 2 * t:2 * t + 1], self.rstd[:, t:t + 1],
                                     ALU.subtract, ALU.mult)
        last.then_inc(self.xn_done, 1)

    def pe_transpose(self, pe, b):
        pe.wait_ge(self.xn_done, b + 1)
        pe.wait_ge(self.xnT_done, b)
        for t in range(TILES):
            last = pe.transpose(self.xT[:, t * P:(t + 1) * P], self.xn[:, t * D:(t + 1) * D], self.ident[:])
        last.then_inc(self.xT_ready, 1)

    def act_copy(self, act, b, par):
        act.wait_ge(self.xT_ready, b + 1)
        act.copy(self.xnT[par][:], self.xT[:]).then_inc(self.xnT_done, 1)


class Router:

    WEIGHT = 0.5

    def __init__(self, ph, ln, iota, bg, logits_psum, top2, width, copies=(0,)):
        self.ln, self.iota, self.bg, self.top2, self.copies = ln, iota, bg, top2, copies
        self.lg_ps = logits_psum
        self.logits = ph.sb("logits", [P, TILES * EXPERTS])
        self.top = ph.sb("top", [P, TILES, 8])
        self.idx = ph.sb("idx", [P, TILES, 8], U32)
        self.idxf = ph.sb("idxf", [P, TILES, 8])
        self.comb = [ph.sb(f"comb{i}", [P, TILES, width]) for i in range(2)]
        if top2:
            self.neg_exp = ph.sb("neg_exp", [P, TILES, 2])
            self.one_plus = ph.sb("one_plus", [P, TILES, 2])
            self.score = ph.sb("score", [P, TILES, 2])
            self.total = ph.sb("total", [P, TILES, 1])
            self.inv_total = ph.sb("inv_total", [P, TILES, 1])
            self.share = ph.sb("share", [P, TILES, 2])
            self.pick = [ph.sb(f"pick{i}", [P, TILES, EXPERTS]) for i in range(2)]
            self.neg_exp_done = ph.sem("neg_exp_done")
            self.one_plus_done = ph.sem("one_plus_done")
            self.score_done = ph.sem("score_done")
            self.total_done = ph.sem("total_done")
            self.inv_done = ph.sem("inv_done")
            self.share_done = ph.sem("share_done")
            self.pick_done = ph.sem("pick_done")
        self.logits_ready = ph.sem("logits_ready")
        self.logits_done = ph.sem("logits_done")
        self.top_done = ph.sem("top_done")
        self.idx_done = ph.sem("idx_done")
        self.idxf_done = ph.sem("idxf_done")
        self.comb_done = ph.sem("comb_done")

    def pe_logits(self, pe, b, par, wg):
        pe.wait_ge(self.ln.xnT_done, b + 1)
        for t in range(TILES):
            last = pe.matmul(self.lg_ps[:, t * EXPERTS:(t + 1) * EXPERTS],
                             self.ln.xnT[par][:, t * P:(t + 1) * P], wg[:], start=True, stop=True)
        last.then_inc(self.logits_ready, 1)

    def act_exp(self, act, b):
        if self.top2:
            act.wait_ge(self.top_done, b + 1)
            act.activation(self.neg_exp[:], self.top[:, :, 0:2], ACT.Exp, scale=-1.0).then_inc(self.neg_exp_done, 1)

    def dve_choose(self, dve, b, par):
        dve.wait_ge(self.logits_ready, b + 1)
        dve.tensor_tensor(self.logits[:], self.lg_ps, self.bg[:], ALU.add).then_inc(self.logits_done, 1)
        wait_apart(dve, self.logits_done, b + 1, self.ln.passed)
        for t in range(TILES):
            last = dve.max(self.top[:, t, :], self.logits[:, t * 8:(t + 1) * 8])
        last.then_inc(self.top_done, 1)
        wait_apart(dve, self.top_done, b + 1, self.ln.passed)
        for t in range(TILES):
            last = dve.max_index(self.idx[:, t, :], self.top[:, t, :], self.logits[:, t * 8:(t + 1) * 8])
        last.then_inc(self.idx_done, 1)
        dve.wait_ge(self.idx_done, b + 1)
        dve.tensor_copy(self.idxf[:], self.idx[:]).then_inc(self.idxf_done, 1)
        dve.wait_ge(self.idxf_done, b + 1)
        if not self.top2:
            for t in range(TILES):
                last = dve.tensor_scalar(self.comb[par][:, t, :], self.iota[:], self.idxf[:, t, 0:1], self.WEIGHT,
                                         ALU.is_equal, ALU.mult)
            last.then_inc(self.comb_done, 1)

    def dve_weigh(self, dve, b, par):
        if self.top2:
            dve.wait_ge(self.neg_exp_done, b + 1)
            dve.tensor_scalar(self.one_plus[:], self.neg_exp[:], 1.0, None, ALU.add).then_inc(self.one_plus_done, 1)
            dve.wait_ge(self.one_plus_done, b + 1)
            dve.reciprocal(self.score[:], self.one_plus[:]).then_inc(self.score_done, 1)
            dve.wait_ge(self.score_done, b + 1)
            dve.scalar_tensor_tensor(self.total[:], self.score[:, :, 0:1], 1e-6, self.score[:, :, 1:2], ALU.add,
                                     ALU.add).then_inc(self.total_done, 1)
            dve.wait_ge(self.total_done, b + 1)
            dve.reciprocal(self.inv_total[:], self.total[:]).then_inc(self.inv_done, 1)
            dve.wait_ge(self.inv_done, b + 1)
            dve.scalar_tensor_tensor(self.share[:], self.score[:], self.WEIGHT,
                                     self.inv_total[:].to_broadcast([P, TILES, 2]), ALU.mult,
                                     ALU.mult).then_inc(self.share_done, 1)
            dve.wait_ge(self.share_done, b + 1)
            for i in range(2):
                for t in range(TILES):
                    last = dve.tensor_scalar(self.pick[i][:, t, :], self.iota[:], self.idxf[:, t, i:i + 1],
                                             self.share[:, t, i:i + 1], ALU.is_equal, ALU.mult)
            last.then_inc(self.pick_done, 1)
            dve.wait_ge(self.pick_done, b + 1)
            for at in self.copies:
                last = dve.tensor_tensor(self.comb[par][:, :, at:at + EXPERTS], self.pick[0][:], self.pick[1][:],
                                         ALU.add)
            last.then_inc(self.comb_done, 1)


class WeightSplit:

    def __init__(self, ph, parts, src):
        self.parts, self.src = parts, src
        self.raw = ph.sb("raw_weights", [P, W_COLS])
        self.raw_loaded = ph.sem("raw_loaded")
        self.hi_done = ph.sem("w_hi_done")

    def sp_load(self, sp):
        sp.dma_start(self.raw[:], self.src).then_inc(self.raw_loaded, 16)

    def pool_split(self, pool, b):
        own = bass.ds(b * (W_COLS // B), W_COLS // B)
        pool.wait_ge(self.raw_loaded, 16)
        pool.tensor_copy(self.parts[:, 0, own], self.raw[:, own]).then_inc(self.hi_done, 1)
        pool.wait_ge(self.hi_done, b + 1)
        pool.tensor_tensor(self.parts[:, 1, own], self.raw[:, own], self.parts[:, 0, own].bitcast(F32),
                           ALU.subtract)


def top1_ffn_phase(nc, name, x, ident, iota, w, x_in=None, first_loads=(), weight_split=None):
    E = EXPERTS
    units = E + 1
    H_PRE, Y_PRE = 4, 3
    with Phase(nc, name) as ph:
        w1 = ph.sb("w1", [P, E * P])
        b1 = ph.sb("b1", [P, E])
        w2 = ph.sb("w2", [P, E * D])
        b2 = ph.sb("b2", [E, D])
        wg = ph.sb("wg", [P, EXPERTS])
        bg = ph.sb("bg", [P, TILES * EXPERTS])
        hT = [ph.sb(f"hT{i}", [P, S]) for i in range(2)]
        combT = [ph.sb(f"combT{i}", [E, S]) for i in range(2)]
        h_ps = [ph.ps(f"h{i}", [P, S]) for i in range(4)]
        y_ps = [ph.ps(f"y{i}", [P, S]) for i in range(2)]
        t_ps = ph.ps("t", [P, S])
        c_ps = ph.ps("c", [P, S])
        lg_ps = t_ps[:, 0:TILES * EXPERTS]
        ln = LayerNorm(ph, x, ident, t_ps)
        router = Router(ph, ln, iota, bg, lg_ps, False, E)
        comb = router.comb
        prepare = WeightSplit(ph, *weight_split) if weight_split else None
        loaded = ph.sem("loaded")
        x_loaded = ph.sem("x_loaded")
        combT_ready = ph.sem("combT_ready")
        combT_done = ph.sem("combT_done")
        h_ready = ph.sem("h_ready")
        h_done = ph.sem("h_done")
        y_ready = ph.sem("y_ready")
        y_used = ph.sem("y_used")

        loads = [(w1[:], w["w1"]), (b1[:], w["b1"]), (w2[:], w["w2"]), (b2[:], w["b2"]), (wg[:], w["wg"]),
                 (bg[:], w["bg"].to_broadcast([P, TILES * EXPERTS]))]
        loads += first_loads
        later_loads = []
        if x_in is not None:
            x_loads = [(rows_at(x, b).rearrange("p (t h) -> p t h", t=TILES), x_in[b]) for b in range(B)]
            loads = x_loads[:1] + loads
            later_loads = x_loads[1:]
        all_loaded = 16 * len(loads)
        all_x_loaded = 16 * len(later_loads)

        def ring(b, par, per, k, slots):
            return (par * per + k) % slots

        with nc.Block() as block:

            @block.sync
            def _(sp):
                for dst, src in loads:
                    sp.dma_start(dst, src).then_inc(loaded, 16)
                for dst, src in later_loads:
                    sp.dma_start(dst, src).then_inc(x_loaded, 16)
                if prepare:
                    prepare.sp_load(sp)

            @block.gpsimd
            def _(pool):
                ln.pool_setup(pool)
                ln.pool_rstd(pool, 0)

                def body(b, par):
                    if has_next(b):
                        ln.pool_rstd(pool, b + 1)
                    if prepare:
                        prepare.pool_split(pool, b)
                over_batches(pool, body)

            @block.tensor
            def _(pe):
                pe.sem_inc(y_ready, Y_PRE)

                def transpose(b):
                    pe.wait_ge(router.logits_done, b)
                    ln.pe_transpose(pe, b)

                def comb_transpose(b, par):
                    pe.wait_ge(router.comb_done, b + 1)
                    pe.wait_ge(combT_done, b)
                    for t in range(TILES):
                        last = pe.matmul(c_ps[0:E, t * P:(t + 1) * P], comb[par][:, t, :], ident[:],
                                         start=True, stop=True)
                    last.then_inc(combT_ready, 1)

                def up(b, par, e):
                    pe.wait_ge(h_done, H_PRE + b * E + e - 3)
                    pe.matmul(h_ps[ring(b, par, E, e, 4)][:], w1[:, e * P:(e + 1) * P], ln.xnT[par][:],
                              start=True, stop=True).then_inc(h_ready, 1)

                def down(b, par, e):
                    y = y_ps[ring(b, par, units, e, 2)]
                    h = hT[ring(b, par, E, e, 2)]
                    pe.wait_ge(h_done, H_PRE + b * E + e + 1)
                    pe.wait_ge(y_used, Y_PRE + b * units + e - 1)
                    for t in range(TILES):
                        last = pe.matmul(y[:, t * D:(t + 1) * D], h[:, t * P:(t + 1) * P],
                                         w2[:, e * D:(e + 1) * D], start=True, stop=True)
                    last.then_inc(y_ready, 1)

                def bias_term(b, par):
                    y = y_ps[ring(b, par, units, E, 2)]
                    pe.wait_ge(combT_done, b + 1)
                    pe.wait_ge(y_used, Y_PRE + b * units + E - 1)
                    for t in range(TILES):
                        last = pe.matmul(y[:, t * D:(t + 1) * D], combT[par][:, t * P:(t + 1) * P], b2[:],
                                         start=True, stop=True)
                    last.then_inc(y_ready, 1)

                pe.wait_ge(loaded, all_loaded)
                transpose(0)
                router.pe_logits(pe, 0, 0, wg)
                comb_transpose(0, 0)

                def body(b, par):
                    for e in range(E):
                        if e == 0:
                            pe.wait_ge(ln.xnT_done, b + 1)
                        up(b, par, e)
                        if e:
                            down(b, par, e - 1)
                        if has_next(b):
                            if e == 3:
                                transpose(b + 1)
                            if e == 5:
                                router.pe_logits(pe, b + 1, 1 - par, wg)
                            if e == 7:
                                comb_transpose(b + 1, 1 - par)
                    down(b, par, E - 1)
                    bias_term(b, par)
                over_batches(pe, body)

            @block.scalar
            def _(act):
                act.sem_inc(h_done, H_PRE)
                act.wait_ge(loaded, all_loaded)

                ln.act_copy(act, 0, 0)

                def body(b, par):
                    for e in range(E):
                        h = hT[ring(b, par, E, e, 2)]
                        before = e - 2 if e >= 2 else e - 3
                        act.wait_ge(y_ready, Y_PRE + b * units + before + 1)
                        act.wait_ge(h_ready, b * E + e + 1)
                        act.activation(h[:], h_ps[ring(b, par, E, e, 4)][:], ACT.Gelu, bias=b1[:, e:e + 1],
                                       scale=1.0).then_inc(h_done, 1)
                        if has_next(b) and e == 4:
                            ln.act_copy(act, b + 1, 1 - par)
                over_batches(act, body)

            @block.vector
            def _(dve):
                dve.sem_inc(y_used, Y_PRE)
                dve.wait_ge(loaded, all_loaded)

                def comb_copy(b, par):
                    dve.wait_ge(combT_ready, b + 1)
                    dve.tensor_copy(combT[par][:], c_ps[0:E, :]).then_inc(combT_done, 1)

                def add(b, par, e):
                    y = y_ps[ring(b, par, units, e, 2)]
                    dve.wait_ge(y_ready, Y_PRE + b * units + e + 1)
                    dve.wait_ge(y_used, Y_PRE + b * units + e)
                    if e < E:
                        for t in range(TILES):
                            last = dve.scalar_tensor_tensor(tile_at(x, b, t), y[:, t * D:(t + 1) * D],
                                                            comb[par][:, t, e:e + 1], tile_at(x, b, t),
                                                            ALU.mult, ALU.add)
                    else:
                        last = dve.tensor_tensor(rows_at(x, b), y[:], rows_at(x, b), ALU.add)
                    last.then_inc(y_used, 1)

                ln.dve_stats(dve, 0)
                ln.dve_norm(dve, 0)
                router.dve_choose(dve, 0, 0)
                comb_copy(0, 0)

                def body(b, par):
                    dve.wait_ge(router.comb_done, b + 1)
                    for e in range(E):
                        if has_next(b):
                            if e == 0:
                                if later_loads:
                                    dve.wait_ge(x_loaded, all_x_loaded)
                                ln.dve_stats(dve, b + 1)
                            if e == 1:
                                ln.dve_norm(dve, b + 1)
                            if e == 5:
                                router.dve_choose(dve, b + 1, 1 - par)
                            if e == 7:
                                comb_copy(b + 1, 1 - par)
                        add(b, par, e)
                    add(b, par, E)
                over_batches(dve, body)


def top2_ffn_phase(nc, name, x, ident, iota, w, w_parts, store_to=None):
    E = EXPERTS + 1
    C = 4
    SHARED = Router.WEIGHT * float(np.float32(0.1))
    CW = LO_ROW + E
    PRODUCTS = ((0, 0), (1, 0), (0, 1))
    with Phase(nc, name) as ph:
        b1 = ph.sb("b1", [P, E * C])
        b2 = ph.sb("b2", [CW, D])
        wg = ph.sb("wg", [P, EXPERTS])
        bg = ph.sb("bg", [P, TILES * EXPERTS])
        b2_parts = ph.sb("b2_parts", [CW, 2, D], F32R)
        sel = ph.sb("sel", [CW, E, P], F32R)
        h32 = ph.sb("h32", [P, C, S])
        hT = [ph.sb(f"hT{i}", [P, 2, C, S], F32R) for i in range(2)]
        xnT_parts = [ph.sb(f"xnT_parts{i}", [P, 2, S], F32R) for i in range(2)]
        combT = [ph.sb(f"combT{i}", [CW, S], F32R) for i in range(2)]
        comb_all = [ph.sb(f"comb_all{i}", [P, S]) for i in range(2)]
        weighted = [ph.sb(f"weighted{i}", [P, S]) for i in range(2)]
        acc = [ph.sb(f"acc{i}", [P, S]) for i in range(2)]
        h_ps = [ph.ps(f"h{i}", [P, S]) for i in range(3)]
        y_ps = [ph.ps(f"y{i}", [P, S]) for i in range(2)]
        comb_ps = ph.ps("comb_ps", [P, S])
        t_ps = ph.ps("t", [P, S])
        c_ps = ph.ps("c", [P, S])
        ln = LayerNorm(ph, x, ident, t_ps)
        router = Router(ph, ln, iota, bg, t_ps[:, 0:TILES * EXPERTS], True, CW, (0, LO_ROW))
        comb = router.comb
        loaded = ph.sem("loaded")
        zero_done = ph.sem("zero_done")
        const_done = ph.sem("const_done")
        b2_hi_done = ph.sem("b2_hi_done")
        xnT_split = ph.sem("xnT_split")
        combT_ready = ph.sem("combT_ready")
        combT_hi = ph.sem("combT_hi")
        combT_done = ph.sem("combT_done")
        bias_ready = ph.sem("bias_ready")
        acc_set = ph.sem("acc_set")
        back_ready = ph.sem("back_ready")
        x_done = ph.sem("x_done")
        h_ready = ph.sem("h_ready")
        h_done = ph.sem("h_done")
        hi_done = ph.sem("hi_done")
        h_split = ph.sem("h_split")
        comb_ready = ph.sem("comb_ready")
        comb_copied = ph.sem("comb_copied")
        y_ready = ph.sem("y_ready")
        y_used = ph.sem("y_used")
        summed = ph.sem("summed")
        stored = ph.sem("stored")

        loads = [(b1[:], w["b1"]), (b2[:], w["b2"]), (wg[:], w["wg"]),
                 (bg[:], w["bg"].to_broadcast([P, TILES * EXPERTS]))]
        all_loaded = 16 * len(loads)

        def slot(par, e, slots):
            return (par * E + e) % slots

        with nc.Block() as block:

            @block.sync
            def _(sp):
                for dst, src in loads:
                    sp.dma_start(dst, src).then_inc(loaded, 16)
                if store_to is not None:
                    for half in range(2):
                        with sp.Fori(0, B // 2) as i:
                            wait_apart(sp, x_done, i + half * (B // 2) + 1, ln.passed)
                            for t in range(TILES):
                                sp.dma_start(token_rows(store_to, half, i * TILES + t),
                                             tile_at(x, i + half * (B // 2), t)).then_inc(stored, 16)
                    sp.wait_ge(stored, 16 * B * TILES)

            @block.gpsimd
            def _(pool):
                ln.pool_setup(pool)
                ln.pool_rstd(pool, 0)

                def body(b, par):
                    if has_next(b):
                        ln.pool_rstd(pool, b + 1)
                    pool.wait_ge(acc_set, b + 1)
                    for e in range(E):
                        N = b * E + e
                        wait_from(pool, summed, N)
                        pool.wait_ge(y_used, N + 1)
                        pool.tensor_tensor(acc[par][:], acc[par][:], weighted[slot(par, e, 2)][:],
                                           ALU.add).then_inc(summed, 1)
                over_batches(pool, body, peel_first=True)

            @block.tensor
            def _(pe):
                def transpose(b):
                    wait_from(pe, router.logits_done, b)
                    ln.pe_transpose(pe, b)

                def comb_transpose(b, par):
                    pe.wait_ge(router.comb_done, b + 1)
                    wait_from(pe, x_done, b - 1)
                    for t in range(TILES):
                        last = pe.matmul(c_ps[0:CW, t * P:(t + 1) * P], comb[par][:, t, :], ident[:],
                                         start=True, stop=True)
                    last.then_inc(combT_ready, 1)

                def bias_term(b, par):
                    pe.wait_ge(combT_done, b + 1)
                    for a in range(2):
                        last = pe.matmul(c_ps[:], b2_parts[:, a, :], combT[par][:], start=a == 0, stop=a == 1)
                    last.then_inc(bias_ready, 1)

                def back(b, par):
                    pe.wait_ge(summed, (b + 1) * E)
                    pe.wait_ge(acc_set, b + 2 if has_next(b) else B)
                    for t in range(TILES):
                        last = pe.transpose(c_ps[:, t * D:(t + 1) * D], acc[par][:, t * P:(t + 1) * P], ident[:])
                    last.then_inc(back_ready, 1)

                def up(b, par, e):
                    for c in range(C):
                        K = (b * E + e) * C + c
                        k = e * C + c
                        wait_from(pe, h_done, K - 2)
                        for i, (p, q) in enumerate(PRODUCTS):
                            last = pe.matmul(h_ps[((par * E + e) * C + c) % 3][:],
                                             w_parts[:, p, k * P:(k + 1) * P], xnT_parts[par][:, q, :],
                                             start=i == 0, stop=i == 2)
                        last.then_inc(h_ready, 1)

                def down(b, par, e):
                    N = b * E + e
                    wait_from(pe, comb_copied, N)
                    pe.matmul(comb_ps[:], sel[:, e, :], combT[par][:], start=True, stop=True).then_inc(comb_ready, 1)
                    wait_from(pe, y_used, N - 1)
                    for c in range(C):
                        pe.wait_ge(h_split, N * C + c + 1)
                        k = E * C + e * C + c
                        for i, (p, q) in enumerate(PRODUCTS):
                            last = pe.matmul(y_ps[slot(par, e, 2)][:], w_parts[:, p, k * D:(k + 1) * D],
                                             hT[slot(par, e, 2)][:, q, c, :],
                                             start=c == 0 and i == 0, stop=c == C - 1 and i == 2)
                    last.then_inc(y_ready, 1)

                pe.wait_ge(loaded, all_loaded)
                pe.wait_ge(const_done, 1)
                transpose(0)
                router.pe_logits(pe, 0, 0, wg)
                comb_transpose(0, 0)

                def body(b, par):
                    pe.wait_ge(xnT_split, b + 1)
                    for e in range(E):
                        up(b, par, e)
                        if e:
                            down(b, par, e - 1)
                        elif has_previous(b):
                            down(b - 1, 1 - par, E - 1)
                        if e == 0:
                            bias_term(b, par)
                        if e == 3 and has_previous(b):
                            back(b - 1, 1 - par)
                        if has_next(b):
                            if e == 2:
                                transpose(b + 1)
                            if e == 4:
                                router.pe_logits(pe, b + 1, 1 - par, wg)
                            if e == 7:
                                comb_transpose(b + 1, 1 - par)
                over_batches(pe, body, peel_first=True)
                down(B - 1, 1, E - 1)
                back(B - 1, 1)

            @block.scalar
            def _(act):
                act.wait_ge(loaded, all_loaded)

                def copy_xnT(b, par):
                    act.wait_ge(ln.xT_ready, b + 1)
                    act.copy(xnT_parts[par][:, 0, :], t_ps[:])
                    act.copy(ln.xnT[par][:], t_ps[:]).then_inc(ln.xnT_done, 1)

                def copy_comb(b, par, e):
                    N = b * E + e
                    act.wait_ge(comb_ready, N + 1)
                    wait_from(act, y_used, N - 1)
                    act.copy(comb_all[slot(par, e, 2)][:], comb_ps[:]).then_inc(comb_copied, 1)

                copy_xnT(0, 0)
                router.act_exp(act, 0)

                def body(b, par):
                    for e in range(E):
                        N = b * E + e
                        wait_from(act, y_ready, N - 1)
                        for c in range(C):
                            K = N * C + c
                            act.wait_ge(h_ready, K + 1)
                            wait_from(act, h_split, K - 3)
                            h = h_ps[((par * E + e) * C + c) % 3]
                            bias = b1[:, e * C + c:e * C + c + 1]
                            last = act.activation(h32[:, c, :], h[:], ACT.Gelu, bias=bias, scale=1.0)
                            if c % 2:
                                last = act.activation(hT[slot(par, e, 2)][:, 0, c, :], h[:], ACT.Gelu, bias=bias,
                                                      scale=1.0)
                            last.then_inc(h_done, 1)
                        if e:
                            copy_comb(b, par, e - 1)
                        elif has_previous(b):
                            copy_comb(b - 1, 1 - par, E - 1)
                        if e == 0:
                            act.wait_ge(bias_ready, b + 1)
                            wait_from(act, back_ready, b - 1)
                            act.copy(acc[par][:], c_ps[:]).then_inc(acc_set, 1)
                        if has_next(b):
                            if e == 3:
                                copy_xnT(b + 1, 1 - par)
                            if e == 6:
                                router.act_exp(act, b + 1)
                over_batches(act, body, peel_first=True)
                copy_comb(B - 1, 1, E - 1)

            @block.vector
            def _(dve):
                dve.memset(sel[:].bitcast(F32), 0.0)
                for i in range(2):
                    last = dve.memset(comb[i][:], 0.0)
                last.then_inc(zero_done, 1)
                dve.wait_ge(zero_done, 1)
                for at in (0, LO_ROW):
                    dve.tensor_copy(sel[at:at + E, :, :],
                                    ident[at:at + E, at:at + E].rearrange("p (e m) -> p e m", m=1).to_broadcast([E, E, P]))
                    for i in range(2):
                        dve.memset(comb[i][:, :, at + EXPERTS:at + E], SHARED)
                dve.wait_ge(loaded, all_loaded)
                split(dve, b2_parts[:, 0, :], b2_parts[:, 1, :], b2[:], b2_hi_done, 1).then_inc(const_done, 1)

                def split_xnT(b, par):
                    dve.wait_ge(ln.xnT_done, b + 1)
                    dve.tensor_tensor(xnT_parts[par][:, 1, :], ln.xnT[par][:],
                                      xnT_parts[par][:, 0, :].bitcast(F32), ALU.subtract).then_inc(xnT_split, 1)

                def split_combT(b, par):
                    dve.wait_ge(combT_ready, b + 1)
                    dve.tensor_copy(combT[par][:], c_ps[0:CW, :]).then_inc(combT_hi, 1)
                    dve.wait_ge(combT_hi, b + 1)
                    lo = combT[par][LO_ROW:CW, :]
                    dve.tensor_tensor(lo, c_ps[LO_ROW:CW, :], lo.bitcast(F32), ALU.subtract).then_inc(combT_done, 1)

                def split_hidden(b, par, e):
                    N = b * E + e
                    for c in range(C):
                        K = N * C + c
                        hi, lo = (hT[slot(par, e, 2)][:, a, c, :] for a in range(2))
                        dve.wait_ge(h_done, K + 1)
                        if c % 2 == 0:
                            dve.tensor_copy(hi, h32[:, c, :]).then_inc(hi_done, 1)
                            dve.wait_ge(hi_done, N * (C // 2) + c // 2 + 1)
                        dve.tensor_tensor(lo, h32[:, c, :], hi.bitcast(F32), ALU.subtract).then_inc(h_split, 1)

                def weigh(b, par, e):
                    N = b * E + e
                    dve.wait_ge(comb_copied, N + 1)
                    dve.wait_ge(y_ready, N + 1)
                    wait_from(dve, summed, N - 1)
                    dve.tensor_tensor(weighted[slot(par, e, 2)][:], y_ps[slot(par, e, 2)][:],
                                      comb_all[slot(par, e, 2)][:], ALU.mult).then_inc(y_used, 1)

                def add(b):
                    dve.wait_ge(back_ready, b + 1)
                    dve.tensor_tensor(rows_at(x, b), c_ps[:], rows_at(x, b), ALU.add).then_inc(x_done, 1)

                ln.dve_stats(dve, 0)
                ln.dve_norm(dve, 0)
                split_xnT(0, 0)
                router.dve_choose(dve, 0, 0)
                router.dve_weigh(dve, 0, 0)
                split_combT(0, 0)

                def body(b, par):
                    for e in range(E):
                        split_hidden(b, par, e)
                        if has_next(b):
                            if e == 0:
                                ln.dve_stats(dve, b + 1)
                            if e == 1:
                                ln.dve_norm(dve, b + 1)
                            if e == 3:
                                split_xnT(b + 1, 1 - par)
                            if e == 5:
                                router.dve_choose(dve, b + 1, 1 - par)
                            if e == 6:
                                router.dve_weigh(dve, b + 1, 1 - par)
                            if e == 8:
                                split_combT(b + 1, 1 - par)
                        if e == 4 and has_previous(b):
                            add(b - 1)
                        if e:
                            weigh(b, par, e - 1)
                        elif has_previous(b):
                            weigh(b - 1, 1 - par, E - 1)
                over_batches(dve, body, peel_first=True)
                weigh(B - 1, 1, E - 1)
                add(B - 1)


def decay_attention_phase(nc, x, ident, w, w_parts, w_parts_out):
    with Phase(nc, "dec") as ph:
        wrkv = ph.sb("wrkv", [P, 3 * D])
        brkv = ph.sb("brkv", [P, 3])
        wo = ph.sb("wo", [P, D])
        bo = ph.sb("bo", [P, S])
        nu_log = ph.sb("nu_log", [P, 1])
        gamma_log = ph.sb("gamma_log", [P, 1])
        nu = ph.sb("nu", [P, 1])
        lam = ph.sb("lam", [P, 1])
        egamma = ph.sb("egamma", [P, 1])
        gamma = ph.sb("gamma", [P, 1])
        neg_br = ph.sb("neg_br", [P, 1])
        zeros = ph.sb("zeros", [P, S])
        lam_row = ph.sb("lam_row", [P, S])
        er = [ph.sb(f"er{i}", [P, S]) for i in range(2)]
        k = [ph.sb(f"k{i}", [P, S]) for i in range(2)]
        er1 = ph.sb("one_plus_er", [P, S])
        kv = ph.sb("kv", [P, S])
        u1 = ph.sb("u1", [P, S])
        u2 = ph.sb("u2", [P, S])
        num = ph.sb("num", [P, S])
        den = ph.sb("den", [P, S])
        den_r = ph.sb("den_r", [P, S])
        inv = ph.sb("inv", [P, S])
        mixed = ph.sb("mixed", [P, S])
        rkv_ps = [[ph.ps(f"{n}_ps{i}", [P, S]) for n in "rkv"] for i in range(2)]
        t_ps = ph.ps("t", [P, S])
        o_ps = ph.ps("o", [P, S])
        ln = LayerNorm(ph, x, ident, t_ps)
        loaded = ph.sem("loaded")
        parts_stored = ph.sem("parts_stored")
        nu_done, lam_done, sum_done, egamma_done = ph.sem("nu"), ph.sem("lam"), ph.sem("nugamma"), ph.sem("egamma")
        const_done = ph.sem("const_done")
        lam_row_done = ph.sem("lam_row_done")
        rkv_ready = ph.sem("rkv_ready")
        act_done = ph.sem("act_done")
        er1_done = ph.sem("er1_done")
        kv_done = ph.sem("kv_done")
        scan_done = ph.sem("scan_done")
        frac_done = ph.sem("frac_done")
        den_r_done = ph.sem("den_r_done")
        er1_used = ph.sem("er1_used")
        rkv_used = ph.sem("rkv_used")
        inv_done = ph.sem("inv_done")
        mixed_done = ph.sem("mixed_done")
        o_ready = ph.sem("o_ready")
        o_used = ph.sem("o_used")
        x_done = ph.sem("x_done")
        loads = [(wrkv[:], w["wrkv"]), (brkv[:], w["brkv"]), (wo[:], w["wo"]),
                 (bo[:], w["bo"].to_broadcast([P, S])), (nu_log[:], w["nu_log"]),
                 (gamma_log[:], w["gamma_log"])]
        all_loaded = 16 * len(loads)

        with nc.Block() as block:

            @block.sync
            def _(sp):
                for dst, src in loads:
                    sp.dma_start(dst, src).then_inc(loaded, 16)
                sp.dma_start(w_parts_out, w_parts[:].bitcast(F32)).then_inc(parts_stored, 16)
                sp.wait_ge(parts_stored, 16)

            @block.gpsimd
            def _(pool):
                ln.pool_setup(pool)
                pool.wait_ge(loaded, all_loaded)
                ln.pool_rstd(pool, 0)

                def body(b, par):
                    pool.wait_ge(act_done, b + 1)
                    wait_apart(pool, er1_used, b + 1, ln.passed)
                    pool.tensor_scalar(er1[:], er[par][:], 1.0, None, ALU.add).then_inc(er1_done, 1)
                    if has_next(b):
                        ln.pool_rstd(pool, b + 1)
                    pool.wait_ge(o_used, b + 1)
                    pool.tensor_tensor(rows_at(x, b), rows_at(x, b), bo[:], ALU.add).then_inc(x_done, 1)
                over_batches(pool, body)

            @block.tensor
            def _(pe):
                def project(b, par):
                    pe.wait_ge(ln.xnT_done, b + 1)
                    for i in range(3):
                        last = pe.matmul(rkv_ps[par][i][:], wrkv[:, i * D:(i + 1) * D], ln.xnT[par][:],
                                         start=True, stop=True)
                    last.then_inc(rkv_ready, 1)

                pe.wait_ge(loaded, all_loaded)
                ln.pe_transpose(pe, 0)
                project(0, 0)

                def body(b, par):
                    if has_next(b):
                        ln.pe_transpose(pe, b + 1)
                        pe.wait_ge(rkv_used, b + 1)
                        project(b + 1, 1 - par)
                    pe.wait_ge(mixed_done, b + 1)
                    for t in range(TILES):
                        last = pe.matmul(o_ps[:, t * D:(t + 1) * D], mixed[:, t * P:(t + 1) * P], wo[:],
                                         start=True, stop=True)
                    last.then_inc(o_ready, 1)
                over_batches(pe, body)

            @block.scalar
            def _(act):
                act.wait_ge(loaded, all_loaded)
                act.activation(nu[:], nu_log[:], ACT.Exp).then_inc(nu_done, 1)
                act.wait_ge(nu_done, 1)
                act.activation(lam[:], nu[:], ACT.Exp, scale=-1.0).then_inc(lam_done, 1)
                act.activation(egamma[:], nu_log[:], ACT.Exp, bias=gamma_log[:]).then_inc(egamma_done, 1)
                act.wait_ge(const_done, 1)
                act.wait_ge(lam_done, 1)
                act.activation(lam_row[:], zeros[:], ACT.Identity, bias=lam[:]).then_inc(lam_row_done, 1)
                ln.act_copy(act, 0, 0)

                def body(b, par):
                    act.wait_ge(rkv_ready, b + 1)
                    act.activation(er[par][:], rkv_ps[par][0][:], ACT.Exp, bias=neg_br[:], scale=-1.0)
                    act.activation(k[par][:], rkv_ps[par][1][:], ACT.Exp, bias=brkv[:, 1:2]).then_inc(act_done, 1)
                    if has_next(b):
                        ln.act_copy(act, b + 1, 1 - par)
                over_batches(act, body)

            @block.vector
            def _(dve):
                dve.memset(zeros[:], 0.0)
                dve.sem_inc(er1_used, 1)
                dve.sem_inc(rkv_used, 1)
                dve.wait_ge(loaded, all_loaded)
                dve.tensor_scalar(neg_br[:], brkv[:, 0:1], -1.0, None, ALU.mult).then_inc(const_done, 1)
                dve.wait_ge(egamma_done, 1)
                dve.tensor_scalar(gamma[:], egamma[:], -1.0, None, ALU.add).then_inc(sum_done, 1)
                dve.wait_ge(sum_done, 1)
                dve.wait_ge(lam_row_done, 1)
                ln.dve_stats(dve, 0)
                ln.dve_norm(dve, 0)

                def body(b, par):
                    if has_next(b):
                        ln.dve_stats(dve, b + 1)
                    dve.wait_ge(act_done, b + 1)
                    dve.scalar_tensor_tensor(kv[:], rkv_ps[par][2][:], brkv[:, 2:3], k[par][:], ALU.add,
                                             ALU.mult).then_inc(kv_done, 1)
                    dve.tensor_tensor_scan(u2[:], lam_row[:], k[par][:], 0.0, ALU.mult, ALU.add)
                    dve.wait_ge(kv_done, b + 1)
                    dve.tensor_tensor_scan(u1[:], lam_row[:], kv[:], 0.0, ALU.mult, ALU.add).then_inc(scan_done, 1)
                    if has_next(b):
                        ln.dve_norm(dve, b + 1)
                    dve.wait_ge(scan_done, b + 1)
                    dve.scalar_tensor_tensor(den[:], k[par][:], gamma[:], u2[:], ALU.mult, ALU.add)
                    dve.scalar_tensor_tensor(num[:], kv[:], gamma[:], u1[:], ALU.mult,
                                             ALU.add).then_inc(frac_done, 1)
                    dve.wait_ge(frac_done, b + 1)
                    dve.wait_ge(er1_done, b + 1)
                    dve.scalar_tensor_tensor(den_r[:], den[:], 1e-6, er1[:], ALU.add,
                                             ALU.mult).then_inc(den_r_done, 1)
                    dve.wait_ge(den_r_done, b + 1)
                    dve.sem_inc(er1_used, 1)
                    dve.reciprocal(inv[:], den_r[:]).then_inc(inv_done, 1)
                    dve.wait_ge(inv_done, b + 1)
                    dve.sem_inc(rkv_used, 1)
                    dve.tensor_tensor(mixed[:], num[:], inv[:], ALU.mult).then_inc(mixed_done, 1)
                    dve.wait_ge(o_ready, b + 1)
                    dve.tensor_tensor(rows_at(x, b), o_ps[:], rows_at(x, b), ALU.add).then_inc(o_used, 1)
                over_batches(dve, body)


def split(dve, hi, lo, value, done, count):
    dve.tensor_copy(hi, value).then_inc(done, 1)
    dve.wait_ge(done, count)
    return dve.tensor_tensor(lo, value, hi.bitcast(F32), ALU.subtract)


def qkv_phase(nc, x, ident, w, v_all, scratch):
    SCALE = float(1.0 / np.sqrt(np.float32(HD)))
    STORES = 16 * 2 * (SPANS + 2)
    FREE = 2 * STORES
    with Phase(nc, "qkv") as ph:
        wq, wk, wv, wp = (ph.sb(n, [P, D]) for n in ("wq", "wk", "wv", "wp"))
        bq, bk, bp, u, v = (ph.sb(n, [P, 1]) for n in ("bq", "bk", "bp", "u", "v"))
        bv = ph.sb("bv", [P, S])
        embT = ph.sb("embT", [P, S])
        bias_u, bias_v = ph.sb("bias_u", [P, 1]), ph.sb("bias_v", [P, 1])
        sum_u, sum_v = ph.sb("sum_u", [P, 1]), ph.sb("sum_v", [P, 1])
        qu = [ph.sb(f"qu{i}", [P, S]) for i in range(2)]
        qv = [ph.sb(f"qv{i}", [P, S]) for i in range(2)]
        kT = [ph.sb(f"kT{i}", [P, S]) for i in range(2)]
        qu_parts = [ph.sb(f"qu_parts{i}", [P, 2, S], F32R) for i in range(2)]
        k_parts = [ph.sb(f"k_parts{i}", [P, 2, S], F32R) for i in range(2)]
        qv_parts = ph.sb("qv_parts", [P, 2 * SPANS * ROWS * B * SPAN], F32R)
        pos = ph.sb("pos", [P, S])
        pos_parts = ph.sb("pos_parts", [P, 2, POS_W], F32R)
        q_ps = [ph.ps(f"qps{i}", [P, S]) for i in range(2)]
        k_ps = [ph.ps(f"kps{i}", [P, S]) for i in range(2)]
        v_ps = [ph.ps(f"vps{i}", [P, S]) for i in range(2)]
        t_ps = ph.ps("t", [P, S])
        pos_ps = ph.ps("pos_ps", [P, S])
        ln = LayerNorm(ph, x, ident, t_ps)
        loaded = ph.sem("loaded")
        sums_done = ph.sem("sums_done")
        bias_done = ph.sem("bias_done")
        pos_ready = ph.sem("pos_ready")
        pos_done = ph.sem("pos_done")
        pos_hi_done = ph.sem("pos_hi_done")
        pos_split = ph.sem("pos_split")
        qkv_ready = ph.sem("qkv_ready")
        qk_done = ph.sem("qk_done")
        hi_done = ph.sem("hi_done")
        qk_split = ph.sem("qk_split")
        v_done = ph.sem("v_done")
        parts_used = ph.sem("parts_used")
        stored = ph.sem("stored")
        stored_qk = ph.sem("stored_qk")
        loads = [(wq[:], w["wq"]), (wk[:], w["wk"]), (wv[:], w["wv"]), (wp[:], w["wp"]), (bq[:], w["bq"]),
                 (bk[:], w["bk"]), (bp[:], w["bp"]), (u[:], w["u"]), (v[:], w["v"]),
                 (bv[:], w["bv"].to_broadcast([P, S])), (embT[:], w["embT"])]
        all_loaded = 16 * len(loads)
        qv_view = qv_parts[:].rearrange("p (t s r b g) -> p t s r b g", t=2, s=SPANS, r=ROWS, b=B)

        with nc.Block() as block:

            @block.sync
            def _(sp):
                sp.sem_inc(stored_qk, FREE)
                for dst, src in loads:
                    sp.dma_start(dst, src).then_inc(loaded, 16)
                for b in range(B):
                    sp.dma_start(x_out(scratch, b), rows_at(x, b).rearrange("p (t h) -> p t h", t=TILES))\
                        .then_inc(stored, 16)
                sp.wait_ge(pos_split, 3)
                sp.dma_start(scratch["pos"], pos_parts[:].bitcast(F32)).then_inc(stored, 16)

                for half in range(2):
                    with sp.Fori(half * (HALF // 2), (half + 1) * (HALF // 2)) as i:
                        for par in range(2):
                            b = 2 * i + par
                            wait_apart(sp, qk_split, b + 1, ln.passed)
                            for part in range(2):
                                for span in range(SPANS):
                                    sp.dma_start(qu_out(scratch, b, part, span),
                                                 qu_parts[par][:, part, span * QU_ROW:(span + 1) * QU_ROW]
                                                 .bitcast(F32)).then_inc(stored_qk, 16)
                                for copy in range(2):
                                    sp.dma_start(k_out(scratch, b, part, copy),
                                                 k_parts[par][:, part, :].bitcast(F32)).then_inc(stored_qk, 16)
                            wait_apart(sp, stored_qk, FREE + (b + 1) * STORES, ln.passed)
                    for span in range(SPANS):
                        for part in range(2):
                            sp.dma_start(qv_out(scratch, span, half, part),
                                         qv_view[:, part, span, :, half * HALF:(half + 1) * HALF, :]
                                         .rearrange("p r b g -> p r (b g)").bitcast(F32)).then_inc(stored, 16)
                sp.wait_ge(stored, 16 * (B + 1 + 4 * SPANS))

            @block.gpsimd
            def _(pool):
                ln.pool_setup(pool)
                ln.pool_rstd(pool, 0)

                def body(b, par):
                    if has_next(b):
                        ln.pool_rstd(pool, b + 1)
                over_batches(pool, body)

            @block.tensor
            def _(pe):
                pe.wait_ge(loaded, all_loaded)
                pe.matmul(pos_ps[:], wp[:], embT[:], start=True, stop=True).then_inc(pos_ready, 1)
                ln.pe_transpose(pe, 0)

                def body(b, par):
                    pe.wait_ge(ln.xnT_done, b + 1)
                    pe.matmul(q_ps[par][:], wq[:], ln.xnT[par][:], start=True, stop=True)
                    pe.matmul(k_ps[par][:], wk[:], ln.xnT[par][:], start=True, stop=True)
                    for t in range(TILES):
                        last = pe.matmul(v_ps[par][:, t * D:(t + 1) * D], ln.xnT[par][:, t * P:(t + 1) * P],
                                         wv[:], start=True, stop=True)
                    last.then_inc(qkv_ready, 1)
                    if has_next(b):
                        ln.pe_transpose(pe, b + 1)
                        pe.wait_ge(v_done, 1 + b)
                        pe.wait_ge(qk_done, 1 + b)
                over_batches(pe, body)

            @block.scalar
            def _(act):
                act.sem_inc(qk_done, 1)
                act.wait_ge(bias_done, 1)
                act.wait_ge(pos_ready, 1)
                act.activation(pos[:], pos_ps[:], ACT.Identity, bias=bp[:]).then_inc(pos_done, 1)
                ln.act_copy(act, 0, 0)

                def body(b, par):
                    act.wait_ge(qkv_ready, b + 1)
                    act.wait_ge(parts_used, b + 1)
                    for s in range(SPANS):
                        view = q_ps[par][:, s * (S // SPANS):(s + 1) * (S // SPANS)].rearrange("p (g r) -> p r g", r=ROWS)
                        for dst, bias in ((qu, bias_u), (qv, bias_v)):
                            act.activation(dst[par][:, s * (S // SPANS):(s + 1) * (S // SPANS)]
                                           .rearrange("p (r g) -> p r g", r=ROWS),
                                           view, ACT.Identity, bias=bias[:], scale=SCALE)
                    act.activation(kT[par][:], k_ps[par][:], ACT.Identity, bias=bk[:]).then_inc(qk_done, 1)
                    if has_next(b):
                        ln.act_copy(act, b + 1, 1 - par)
                over_batches(act, body)

            @block.vector
            def _(dve):
                dve.sem_inc(v_done, 1)
                dve.sem_inc(parts_used, 2)
                dve.memset(pos_parts[:, :, 0:POS_0].bitcast(F32), 0.0)
                dve.memset(pos_parts[:, :, POS_0 + S:POS_W].bitcast(F32), 0.0).then_inc(pos_split, 1)
                dve.wait_ge(loaded, all_loaded)
                dve.tensor_tensor(sum_u[:], bq[:], u[:], ALU.add)
                dve.tensor_tensor(sum_v[:], bq[:], v[:], ALU.add).then_inc(sums_done, 1)
                dve.wait_ge(sums_done, 1)
                dve.tensor_scalar(bias_u[:], sum_u[:], SCALE, None, ALU.mult)
                dve.tensor_scalar(bias_v[:], sum_v[:], SCALE, None, ALU.mult).then_inc(bias_done, 1)
                ln.dve_stats(dve, 0)
                ln.dve_norm(dve, 0)
                dve.wait_ge(pos_done, 1)
                split(dve, pos_parts[:, 0, POS_0:POS_0 + S], pos_parts[:, 1, POS_0:POS_0 + S], pos[:],
                      pos_hi_done, 1).then_inc(pos_split, 2)

                def body(b, par):
                    if has_next(b):
                        ln.dve_stats(dve, b + 1)
                        ln.dve_norm(dve, b + 1)
                    dve.wait_ge(qkv_ready, b + 1)
                    for t in range(TILES):
                        last = dve.tensor_tensor(
                            v_slice(v_all, t, b),
                            v_ps[par][:, t * D:(t + 1) * D].rearrange("p (h c) -> p h c", h=HEADS),
                            bv[:, 0:D].rearrange("p (h c) -> p h c", h=HEADS), ALU.add)
                    last.then_inc(v_done, 1)
                    dve.wait_ge(qk_done, 1 + b + 1)
                    dve.wait_ge(stored_qk, FREE + (b - 1) * STORES)
                    split(dve, qu_parts[par][:, 0, :], qu_parts[par][:, 1, :], qu[par][:], hi_done, 3 * b + 1)
                    split(dve, k_parts[par][:, 0, :], k_parts[par][:, 1, :], kT[par][:], hi_done, 3 * b + 2)
                    own = [qv_at(qv_parts, t, b) for t in range(2)]
                    split(dve, own[0], own[1], qv[par][:].rearrange("p (n g) -> p n g", g=SPAN), hi_done,
                          3 * b + 3).then_inc(qk_split, 1)
                    dve.wait_ge(qk_split, b + 1)
                    dve.sem_inc(parts_used, 1)
                over_batches(dve, body)


def qv_at(qv_parts, part, b):
    rows = qv_parts[:, part * (S * B):(part + 1) * (S * B)].rearrange("p (n b g) -> p n b g", b=B, g=SPAN)
    return rows[:, :, bass.ds(b, 1), :].rearrange("p n b g -> p n (b g)")


QU_ROW = ROWS * SPAN
QU_SEQ = 2 * HD * QU_ROW
QV_RUN = HALF * SPAN
QV_ROW = 2 * P * QV_RUN
K_SEQ = 2 * HD * S
K_PART = HEADS * B * K_SEQ


def qu_out(scratch, b, part, span):
    return bass.AP(tensor=scratch["qu"].tensor, offset=b * QU_SEQ + part * (HD * QU_ROW) + span * B * QU_SEQ,
                   ap=[[SPANS * B * QU_SEQ, HEADS], [QU_ROW, HD], [1, QU_ROW]])


def qu_rows(scratch, h, span, b):
    return bass.AP(tensor=scratch["qu"].tensor, offset=h * (SPANS * B * QU_SEQ) + (span * B + b) * QU_SEQ,
                   ap=[[QU_ROW, 2 * HD], [SPAN, ROWS], [1, SPAN]])


def qv_out(scratch, span, half, part):
    return bass.AP(tensor=scratch["qv"].tensor, offset=(span * 2 + half) * (ROWS * QV_ROW) + part * (P * QV_RUN),
                   ap=[[QV_RUN, P], [QV_ROW, ROWS], [1, QV_RUN]])


def qv_rows(scratch, h, span, half, r):
    return bass.AP(tensor=scratch["qv"].tensor,
                   offset=h * (HD * QV_RUN) + ((span * 2 + half) * ROWS + r) * QV_ROW,
                   ap=[[QV_RUN, HD], [P * QV_RUN, 2], [1, QV_RUN]])


def qv_first_rows(scratch, h, span, half, part, g0, n):
    return bass.AP(tensor=scratch["qv"].tensor,
                   offset=h * (HD * QV_RUN) + (span * 2 + half) * (ROWS * QV_ROW) + part * (P * QV_RUN) + g0,
                   ap=[[QV_RUN, HD], [SPAN, HALF], [1, n]])


def k_out(scratch, b, part, copy):
    return bass.AP(tensor=scratch["k"].tensor, offset=b * K_SEQ + part * K_PART + copy * (HD * S),
                   ap=[[B * K_SEQ, HEADS], [S, HD], [1, S]])


def key_rows(scratch, h, half, part):
    return bass.AP(tensor=scratch["k"].tensor, offset=h * (B * K_SEQ) + part * K_PART + half * (HALF * K_SEQ),
                   ap=[[S, P], [1, S]])


def x_out(scratch, b):
    half, seq = divmod(b, HALF)
    return bass.AP(tensor=scratch["x"].tensor, offset=half * (HALF * S * D) + seq * D,
                   ap=[[HALF * D, P], [P * HALF * D, TILES], [1, D]])


def x_tiles(scratch, first, n):
    return bass.AP(tensor=scratch["x"].tensor, offset=first * (P * D), ap=[[D, P], [P * D, n], [1, D]])


def pos_table(scratch, h, first, part):
    return bass.AP(tensor=scratch["pos"].tensor, offset=h * (HD * 2 * POS_W) + part * POS_W + first,
                   ap=[[1, ROWS], [2 * POS_W, HD], [1, S]])


def v_slice(v_all, t, b):
    flat = v_all[:].rearrange("p (j h b c) -> p j h b c", j=TILES, h=HEADS, b=B)
    return flat[:, t, :, bass.ds(b, 1), :].rearrange("p h b c -> p h (b c)")


def relative_attention_phase(nc, ident, w, v_all, o_all, scratch):
    PRE = 4
    N_TILES = 2 * GROUPS
    N_BLOCKS = N_TILES // 8
    with Phase(nc, "rel") as ph:
        left = [ph.sb(f"left{i}", [P, 2, ROWS * HALF * SPAN], F32R) for i in range(SPANS)]
        right = [ph.sb(f"right{i}", [P, 2, ROWS * HALF * SPAN], F32R) for i in range(SPANS)]
        cont = [ph.sb(f"cont{i}", [P, ROWS * HALF * SPAN], F32R) for i in range(SPANS)]
        keys = [[ph.sb(f"keys{i}{t}", [P, S], F32R) for t in range(2)] for i in range(2)]
        pos_l = [[ph.sb(f"pos_l{i}{t}", [P, S], F32R) for t in range(2)] for i in range(2)]
        pos_r = [[ph.sb(f"pos_r{i}{t}", [P, S], F32R) for t in range(2)] for i in range(2)]
        mask = ph.sb("mask", [P, HALF])
        neg_max = ph.sb("neg_max", [P, 4])
        row_sum = ph.sb("row_sum", [P, N_TILES])
        probs = [ph.sb(f"probs{i}", [P, S]) for i in range(4)]
        probsT = [ph.sb(f"probsT{i}", [P, S]) for i in range(2)]
        own = ph.sb("own", [P, 8 * HALF * HD])
        picked = ph.sb("picked", [P, 8 * HD])
        inv_sum = ph.sb("inv_sum", [P, 8, 1])
        s_ps = [ph.ps(f"s{i}", [P, S]) for i in range(4)]
        t_ps = [ph.ps(f"tps{i}", [P, S]) for i in range(2)]
        o_ps = [ph.ps(f"o{i}", [P, S]) for i in range(2)]
        zeroed = [ph.sem(f"zeroed{i}") for i in range(SPANS)]
        passed = ph.sem("passed")
        mask_loaded = ph.sem("mask_loaded")
        loaded = [ph.sem(f"loaded{i}") for i in range(2)]
        s_ready = ph.sem("s_ready")
        max_done = ph.sem("max_done")
        p_done = ph.sem("p_done")
        t_ready = ph.sem("t_ready")
        pt_done = ph.sem("pt_done")
        pv_done = ph.sem("pv_done")
        own_done = ph.sem("own_done")
        picked_done = ph.sem("picked_done")
        o_done = ph.sem("o_done")
        LOADS = [ROWS + (ROWS - 1 + 4) + HALF + 6, ROWS + (ROWS - 1 + 2) + HALF]

        with nc.Block() as block:

            @block.sync
            def _(sp):
                sp.dma_start(mask[:], w["mask"]).then_inc(mask_loaded, 16)

                def get(dst, src, span):
                    sp.dma_start(dst.bitcast(F32), src, allow_slow_non_contiguous=True).then_inc(loaded[span], 16)

                def load_tables(h, half):
                    for part in range(2):
                        get(keys[half][part][:], key_rows(scratch, h, half, part), 0)
                        get(pos_r[half][part][:], pos_table(scratch, h, 0, part), 0)
                        get(pos_l[half][part][:], pos_table(scratch, h, POS_0, part), 0)

                def load_queries(h, half, span):
                    for b in range(HALF):
                        get(cont[span][b * 2 * HD:(b + 1) * 2 * HD, :]
                            .rearrange("c (r b g) -> c r b g", r=ROWS, b=HALF)[:, :, b, :],
                            qu_rows(scratch, h, span, half * HALF + b), span)
                    plane = HALF * SPAN
                    for n in range(ROWS):
                        s = ROWS - 1 - n
                        rows, own = slice(n * HD, (n + 1) * HD), slice(s * plane, (s + 1) * plane)
                        get(left[span][rows, :, own], qv_rows(scratch, h, span, half, s), span)
                        if s < ROWS - 1:
                            get(right[span][rows, :, own], qv_rows(scratch, h, span, half, s + 1), span)
                            continue
                        for part in range(2):
                            dst = right[span][rows, part, own].rearrange("c (b g) -> c b g", b=HALF)
                            get(dst[:, :, 0:SPAN - 1], qv_first_rows(scratch, h, span, half, part, 1, SPAN - 1), span)
                            if span + 1 < SPANS:
                                get(dst[:, :, SPAN - 1:SPAN],
                                    qv_first_rows(scratch, h, span + 1, half, part, 0, 1), span)

                load_tables(0, 0)
                for span in range(SPANS):
                    sp.wait_ge(zeroed[span], 3)
                    load_queries(0, 0, span)

                def load_next(h, half):
                    for span in range(SPANS):
                        wait_apart(sp, s_ready, h * N_TILES + (half - 1) * GROUPS + (span + 1) * SPAN, passed)
                        if span == 0:
                            load_tables(h, half)
                        load_queries(h, half, span)

                load_next(0, 1)
                with sp.Fori(1, HEADS) as h:
                    load_next(h, 0)
                    load_next(h, 1)

            @block.gpsimd
            def _(pool):
                for span in range(SPANS):
                    pool.memset(cont[span][:].bitcast(F32), 0.0).then_inc(zeroed[span], 1)

            @block.tensor
            def _(pe):
                def scores(h, n):
                    half, g = divmod(n, GROUPS)
                    span, gs = divmod(g, SPAN)
                    i0 = g * ROWS
                    N = h * N_TILES + n
                    if gs == 0:
                        pe.wait_ge(loaded[span], (2 * h + half + 1) * (LOADS[span] * 16))
                    pe.wait_ge(p_done, PRE + N - 3)
                    out = s_ps[n % 4]

                    def tile_of(buf):
                        return buf.rearrange("p (r g) -> p r g", g=SPAN)[:, :, gs]

                    for part in range(2):
                        pe.matmul(out[:], tile_of(cont[span][:]), keys[half][part][:], start=part == 0, stop=False)
                    for a, b in ((0, 0), (0, 1), (1, 0)):
                        pe.matmul(out[:, 0:i0 + ROWS], tile_of(left[span][:, a, :]),
                                  pos_l[half][b][:, S - ROWS - i0:S], start=False, stop=False)
                    for a, b in ((0, 0), (0, 1), (1, 0)):
                        last = pe.matmul(out[:, i0:S], tile_of(right[span][:, a, :]), pos_r[half][b][:, 0:S - i0],
                                         start=False, stop=(a, b) == (1, 0))
                    last.then_inc(s_ready, 1)

                def transpose(h, n):
                    N = h * N_TILES + n
                    pe.wait_ge(p_done, PRE + N + 1)
                    pe.wait_ge(pt_done, PRE + N - 1)
                    for j in range(TILES):
                        last = pe.transpose(t_ps[n % 2][:, j * P:(j + 1) * P], probs[n % 4][:, j * P:(j + 1) * P],
                                            ident[:])
                    last.then_inc(t_ready, 1)

                def values(h, n):
                    N = h * N_TILES + n
                    half = n // GROUPS
                    pe.wait_ge(pt_done, PRE + N + 1)
                    if n % 8 == 0:
                        pe.wait_ge(o_done, PRE + h * N_BLOCKS + n // 8 - 1)
                    out = o_ps[n // 8 % 2][:, (n % 8) * (HALF * HD):(n % 8 + 1) * (HALF * HD)]
                    for j in range(TILES):
                        start = j * (HEADS * B * HD) + half * (HALF * HD)
                        last = pe.matmul(out, probsT[n % 2][:, j * P:(j + 1) * P],
                                         v_all[:, bass.ds(h * (B * HD) + start, HALF * HD)],
                                         start=j == 0, stop=j == TILES - 1)
                    last.then_inc(pv_done, 1)

                pe.sem_inc(pv_done, PRE)
                pe.sem_inc(t_ready, PRE)
                with pe.Fori(0, HEADS) as h:
                    for n in range(N_TILES + 3):
                        if n < N_TILES:
                            scores(h, n)
                        if 2 <= n < N_TILES + 2:
                            transpose(h, n - 2)
                        if n >= 3:
                            values(h, n - 3)

            @block.scalar
            def _(act):
                act.sem_inc(p_done, PRE)
                with act.Fori(0, HEADS) as h:
                    for n in range(N_TILES):
                        N = h * N_TILES + n
                        act.wait_ge(max_done, N + 1)
                        act.wait_ge(t_ready, PRE + N - 3)
                        act.activation(probs[n % 4][:], s_ps[n % 4][:], ACT.Exp, bias=neg_max[:, n % 4:n % 4 + 1],
                                       scale=1.0, accum_out=row_sum[:, n:n + 1]).then_inc(p_done, 1)

            @block.vector
            def _(dve):
                dve.sem_inc(pt_done, PRE)
                dve.sem_inc(o_done, PRE)
                for span in range(SPANS):
                    for buf in (left, right):
                        dve.memset(buf[span][:].bitcast(F32), 0.0).then_inc(zeroed[span], 1)
                dve.wait_ge(mask_loaded, 16)

                def maxima(h, n):
                    dve.wait_ge(s_ready, h * N_TILES + n + 1)
                    dve.tensor_reduce(neg_max[:, n % 4:n % 4 + 1], s_ps[n % 4][:], AX.X, ALU.max,
                                      negate=True).then_inc(max_done, 1)

                def copy(h, n):
                    N = h * N_TILES + n
                    dve.wait_ge(t_ready, PRE + N + 1)
                    dve.wait_ge(pv_done, PRE + N - 1)
                    dve.tensor_copy(probsT[n % 2][:], t_ps[n % 2][:]).then_inc(pt_done, 1)

                def outputs(h, g):
                    G = h * N_BLOCKS + g
                    dve.wait_ge(pv_done, PRE + 8 * G + 8)
                    dve.tensor_tensor(
                        own[:].rearrange("p (a b c) -> p a b c", a=8, b=HALF),
                        o_ps[g % 2][:].rearrange("p (a b c) -> p a b c", a=8, b=HALF),
                        mask[:].rearrange("p (a b c) -> p a b c", a=1, c=1).to_broadcast([P, 8, HALF, HD]),
                        ALU.mult).then_inc(own_done, 1)
                    dve.reciprocal(inv_sum[:, :, 0], row_sum[:, 8 * g:8 * g + 8])
                    dve.wait_ge(own_done, G + 1)
                    dve.tensor_reduce(picked[:].rearrange("p (a c) -> p a c", a=8),
                                      own[:].rearrange("p (a b c) -> p a c b", a=8, b=HALF), AX.X,
                                      ALU.add).then_inc(picked_done, 1)
                    dve.wait_ge(picked_done, G + 1)
                    dve.tensor_tensor(
                        o_all[:].rearrange("p (a e) -> p a e", e=D)[:, 8 * g:8 * g + 8, bass.ds(h * HD, HD)],
                        picked[:].rearrange("p (a c) -> p a c", a=8),
                        inv_sum[:].to_broadcast([P, 8, HD]), ALU.mult).then_inc(o_done, 1)

                with dve.Fori(0, HEADS) as h:
                    for n in range(N_TILES + 2):
                        if n < N_TILES:
                            maxima(h, n)
                        if n >= 2:
                            copy(h, n - 2)
                        if n >= 12 and n % 8 == 4:
                            outputs(h, n // 8 - 1)
                    outputs(h, N_BLOCKS - 1)


def out_projection_phase(nc, x, ident, w, scratch, w_parts):
    with Phase(nc, "proj") as ph:
        x_saved = ph.sb("x_saved", [P, B * S])
        wo = ph.sb("wo", [P, D])
        bo = ph.sb("bo", [P, S])
        oT = [ph.sb(f"oT{i}", [P, S]) for i in range(2)]
        t_ps = [ph.ps(f"tps{i}", [P, S]) for i in range(2)]
        y_ps = [ph.ps(f"y{i}", [P, S]) for i in range(2)]
        loaded = ph.sem("loaded")
        x_loaded = ph.sem("x_loaded")
        parts_loaded = ph.sem("parts_loaded")
        t_ready = ph.sem("t_ready")
        oT_done = ph.sem("oT_done")
        y_ready = ph.sem("y_ready")
        x_done = ph.sem("x_done")
        bias_done = ph.sem("bias_done")
        PRE = 2
        loads = [(wo[:], w["wo"]), (bo[:], w["bo"].to_broadcast([P, S]))]

        with nc.Block() as block:

            @block.sync
            def _(sp):
                for dst, src in loads:
                    sp.dma_start(dst, src).then_inc(loaded, 16)
                for b in range(0, B, 4):
                    sp.dma_start(x_saved[:, b * S:(b + 4) * S].rearrange("p (t h) -> p t h", h=D),
                                 x_tiles(scratch, b * TILES, 4 * TILES)).then_inc(x_loaded, 16)
                sp.dma_start(w_parts[:].bitcast(F32), scratch["w_parts"]).then_inc(parts_loaded, 16)
                sp.wait_ge(parts_loaded, 16)

            @block.tensor
            def _(pe):
                def body(b, par):
                    pe.wait_ge(oT_done, PRE + b - 1)
                    for t in range(TILES):
                        last = pe.transpose(t_ps[par][:, t * P:(t + 1) * P], tile_at(x, b, t), ident[:])
                    last.then_inc(t_ready, 1)
                    pe.wait_ge(oT_done, PRE + b + 1)
                    pe.wait_ge(x_done, PRE + b - 1)
                    for t in range(TILES):
                        last = pe.matmul(y_ps[par][:, t * D:(t + 1) * D], oT[par][:, t * P:(t + 1) * P], wo[:],
                                         start=True, stop=True)
                    last.then_inc(y_ready, 1)
                pe.wait_ge(loaded, 16 * len(loads))
                for b in range(B):
                    body(b, b % 2)

            @block.scalar
            def _(act):
                act.sem_inc(oT_done, PRE)

                def body(b, par):
                    act.wait_ge(t_ready, b + 1)
                    act.copy(oT[par][:], t_ps[par][:]).then_inc(oT_done, 1)
                over_batches(act, body)

            @block.gpsimd
            def _(pool):
                pool.wait_ge(loaded, 16 * len(loads))
                pool.wait_ge(x_loaded, 16 * 4)
                with pool.Fori(0, B) as b:
                    pool.tensor_tensor(rows_at(x_saved, b), rows_at(x_saved, b), bo[:], ALU.add).then_inc(bias_done, 1)

            @block.vector
            def _(dve):
                dve.sem_inc(x_done, PRE)

                def body(b, par):
                    dve.wait_ge(y_ready, b + 1)
                    dve.wait_ge(bias_done, b + 1)
                    dve.tensor_tensor(rows_at(x, b), y_ps[par][:], rows_at(x_saved, b), ALU.add).then_inc(x_done, 1)
                over_batches(dve, body)


def token_rows(dram, half, g):
    return bass.AP(tensor=dram.tensor, offset=(half * HALF * S + g * ROWS) * D,
                   ap=[[D, ROWS], [S * D, HALF], [1, D]])


def build(nc, a, out):
    scratch = {
        "x": nc.dram_tensor("x_scratch", [B * S, D], F32).ap(),
        "qu": nc.dram_tensor("qu_scratch", [HEADS * SPANS * B, QU_SEQ], F32).ap(),
        "qv": nc.dram_tensor("qv_scratch", [SPANS * 2 * ROWS, QV_ROW], F32).ap(),
        "k": nc.dram_tensor("k_scratch", [2 * HEADS * B, K_SEQ], F32).ap(),
        "w_parts": nc.dram_tensor("w_parts_scratch", [P, 2, W_COLS], F32).ap(),
        "pos": nc.dram_tensor("pos_scratch", [P, 2, POS_W], F32).ap(),
    }
    x_in = a["x"].rearrange("b (t p) h -> b p t h", p=P)
    moe0 = {n: a["e0_" + n] for n in ("w1", "b1", "w2", "b2", "wg", "bg")}
    moe1 = {n: a["e1_" + n] for n in ("b1", "b2", "wg", "bg")}
    with Phase(nc, "all") as ph:
        x = ph.sb("x", [P, B * S])
        ident = ph.sb("ident", [P, P])
        iota = ph.sb("iota", [P, EXPERTS])
        first_loads = [(ident[:], a["ident"]), (iota[:], a["iota"].to_broadcast([P, EXPERTS]))]

        with Phase(nc, "wp") as wp:
            w_parts = wp.sb("w_parts", [P, 2, W_COLS], F32R)
            top1_ffn_phase(nc, "moe0a", x, ident, iota, moe0, x_in=x_in, first_loads=first_loads, weight_split=(w_parts, a["e1_w"]))
            decay_attention_phase(nc, x, ident, {n: a["d_" + n] for n in ("wrkv", "brkv", "wo", "bo", "nu_log", "gamma_log")},
                                  w_parts, scratch["w_parts"])
            top1_ffn_phase(nc, "moe0b", x, ident, iota, moe0)
            top2_ffn_phase(nc, "moe1a", x, ident, iota, moe1, w_parts)
        o_all = x
        with Phase(nc, "attv") as attv:
            v_all = attv.sb("v_all", [P, B * S])
            qkv_phase(nc, x, ident, {n: a["r_" + n] for n in ("wq", "wk", "wv", "wp", "bq", "bk", "bp", "u", "v",
                                                              "bv", "embT")}, v_all, scratch)
            relative_attention_phase(nc, ident, {"mask": a["mask"]}, v_all, o_all, scratch)
        w_parts = ph.sb("w_parts_again", [P, 2, W_COLS], F32R)
        out_projection_phase(nc, x, ident, {"wo": a["r_wo"], "bo": a["r_bo"]}, scratch, w_parts)
        top2_ffn_phase(nc, "moe1b", x, ident, iota, moe1, w_parts,
                       store_to=out.rearrange("b s h -> (b s) h"))


def lay_out(i):
    def col(v):
        return np.ascontiguousarray(np.reshape(v, (D, 1)))

    def row(v, times):
        return np.ascontiguousarray(np.tile(np.reshape(v, (1, -1)), (1, times)))

    a = {"x": i["L0_attn_inputs"]}
    f = "L0_ffn_"
    a["e0_w1"] = i[f + "W1"].transpose(1, 0, 2).reshape(P, -1)
    a["e0_b1"] = i[f + "b1"].T
    a["e0_w2"] = i[f + "W2"].transpose(1, 0, 2).reshape(P, -1)
    a["e0_b2"] = i[f + "b2"]
    a["e0_wg"] = i[f + "Wg"]
    a["e0_bg"] = row(i[f + "bg"], TILES)
    f = "L1_ffn_"
    w1 = np.concatenate([i[f + "w1"], i[f + "sw1"][None]])
    w2 = np.concatenate([i[f + "w2"], i[f + "sw2"][None]])
    b1 = np.concatenate([i[f + "b1"], i[f + "sb1"][None]])
    a["e1_b1"] = b1.reshape(-1, P).T
    a["e1_w"] = np.concatenate([w1.transpose(1, 0, 2).reshape(P, -1),
                                w2.reshape(9, 4, P, D).transpose(2, 0, 1, 3).reshape(P, -1)], axis=1)
    b2 = np.concatenate([i[f + "b2"], i[f + "sb2"][None]])
    a["e1_b2"] = np.concatenate([b2, np.zeros((LO_ROW - len(b2), D), np.float32), b2])
    a["e1_wg"] = i[f + "gate_w"].T
    a["e1_bg"] = row(i[f + "gate_b"], TILES)
    f = "L0_attn_"
    a["d_wrkv"] = i[f + "W_rkv"]
    a["d_brkv"] = i[f + "b_rkv"].reshape(3, D).T
    a["d_wo"] = i[f + "W_o"]
    a["d_bo"] = row(i[f + "b_o"], TILES)
    a["d_nu_log"] = col(i[f + "nu_log"])
    a["d_gamma_log"] = col(i[f + "gamma_log"])
    f = "L1_attn_"
    for n in "qkvp":
        a["r_w" + n] = i[f + "W" + n]
    a["r_wo"] = i[f + "Wo"]
    for n in "qkp":
        a["r_b" + n] = col(i[f + "b" + n])
    a["r_bv"] = row(i[f + "bv"], TILES)
    a["r_bo"] = row(i[f + "bo"], TILES)
    a["r_u"] = col(i[f + "u"])
    a["r_v"] = col(i[f + "v"])
    pos = np.arange(S, dtype=np.float32)
    freq = (1.0 / np.float32(10000.0) ** (np.float32(2.0) * np.arange(D // 2, dtype=np.float32) / np.float32(D))).astype(np.float32)
    ang = pos[:, None] * freq[None, :]
    a["r_embT"] = np.concatenate([np.sin(ang), np.cos(ang)], axis=-1).astype(np.float32).T
    a["ident"] = np.eye(P, dtype=np.float32)
    a["iota"] = np.arange(EXPERTS, dtype=np.float32)[None]
    a["mask"] = (np.arange(P)[:, None] % HALF == np.arange(HALF)[None]).astype(np.float32)
    return {n: np.ascontiguousarray(v) for n, v in a.items()}





def kernel(**inputs):
    import concourse.bacc as bacc
    from concourse.bass_utils import run_bass_kernel_spmd

    arrays = lay_out({n: np.asarray(v) for n, v in inputs.items()})
    nc = bacc.Bacc("TRN2", target_bir_lowering=False, num_devices=1)
    aps = {n: nc.dram_tensor(f"in_{n}", v.shape, mybir.dt.from_np(v.dtype), kind="ExternalInput").ap()
           for n, v in arrays.items()}
    out = nc.dram_tensor("out", (B, S, D), F32, kind="ExternalOutput").ap()
    build(nc, aps, out)
    r = run_bass_kernel_spmd(nc, [{f"in_{n}": v for n, v in arrays.items()}], core_ids=[0])
    return r.results[0]["out"]
```

```python
from contextlib import ExitStack

import numpy as np

import concourse.bass as bass
from concourse import mybir

F32 = mybir.dt.float32
U32 = mybir.dt.uint32
F32R = mybir.dt.float32r
ALU = mybir.AluOpType
ACT = mybir.ActivationFunctionType
AX = mybir.AxisListType

P = 128
B = 16
S = 512
D = 128
TILES = S // P
EXPERTS = 8
HEADS = 16
HD = D // HEADS
EPS = 1e-5

HALF = 8
ROWS = P // HALF
GROUPS = S // ROWS
SPANS = 2
SPAN = GROUPS // SPANS
POS_W = 560
POS_0 = 17
W_COLS = 2 * (EXPERTS + 1) * 4 * P
LO_ROW = 32


class Phase:

    def __init__(self, nc, name):
        self.nc, self.name, self.ctx, self.sems = nc, name, ExitStack(), []

    def __enter__(self):
        return self

    def __exit__(self, *exc):
        if self.sems and exc[0] is None:
            with self.nc.Block() as block:
                @block.sync
                def _(sp):
                    for sem in self.sems:
                        sp.sem_clear(sem)
        return self.ctx.__exit__(*exc)

    def sb(self, name, shape, dt=F32):
        return self.ctx.enter_context(self.nc.sbuf_tensor(f"{self.name}_{name}", shape, dt))

    def ps(self, name, shape):
        return self.ctx.enter_context(self.nc.psum_tensor(f"{self.name}_{name}", shape, F32))

    def sem(self, name):
        self.sems.append(self.ctx.enter_context(self.nc.semaphore(f"{self.name}_{name}")))
        return self.sems[-1]


def rows_at(x, b):
    return x[:, bass.ds(b * (TILES * D), TILES * D)]


def tile_at(x, b, t):
    return x[:, bass.ds(b * (TILES * D) + t * D, D)]


def over_batches(eng, body, peel_first=False):
    if peel_first:
        body(0, 0)
        body(1, 1)
    with eng.Fori(1 if peel_first else 0, B // 2 - 1) as i:
        body(2 * i, 0)
        body(2 * i + 1, 1)
    body(B - 2, 0)
    body(B - 1, 1)


def has_next(b):
    return not (isinstance(b, int) and b >= B - 1)


def has_previous(b):
    return not (isinstance(b, int) and b == 0)


def wait_from(eng, sem, value):
    if not (isinstance(value, int) and value <= 0):
        eng.wait_ge(sem, value)


def wait_apart(eng, sem, value, passed):
    eng.wait_ge(sem, value)
    eng.sem_inc(passed, 1)


class LayerNorm:

    def __init__(self, ph, x, ident, transposed_psum):
        self.x, self.ident, self.xT = x, ident, transposed_psum
        self.stats = ph.sb("stats", [P, TILES * 6])
        self.mv = ph.sb("mv", [P, TILES * 2])
        self.var = ph.sb("var", [P, TILES])
        self.rstd = ph.sb("rstd", [P, TILES])
        self.minus_half = ph.sb("minus_half", [P, TILES])
        self.xn = ph.sb("xn", [P, S])
        self.xnT = [ph.sb(f"xnT{i}", [P, S]) for i in range(2)]
        self.passed = ph.sem("passed")
        self.stats_done = ph.sem("stats_done")
        self.mv_done = ph.sem("mv_done")
        self.const_done = ph.sem("ln_const")
        self.var_done = ph.sem("var_done")
        self.rstd_done = ph.sem("rstd_done")
        self.xn_done = ph.sem("xn_done")
        self.xT_ready = ph.sem("xT_ready")
        self.xnT_done = ph.sem("xnT_done")

    def pool_setup(self, pool):
        pool.memset(self.minus_half[:], -0.5).then_inc(self.const_done, 1)
        pool.wait_ge(self.const_done, 1)

    def dve_stats(self, dve, b):
        for t in range(TILES):
            last = dve.bn_stats(self.stats[:, t * 6:(t + 1) * 6], tile_at(self.x, b, t))
        last.then_inc(self.stats_done, 1)
        wait_apart(dve, self.stats_done, b + 1, self.passed)
        for t in range(TILES):
            last = dve.bn_aggr(self.mv[:, 2 * t:2 * t + 2], self.stats[:, t * 6:(t + 1) * 6])
        last.then_inc(self.mv_done, 1)

    def pool_rstd(self, pool, b):
        wait_apart(pool, self.mv_done, b + 1, self.passed)
        pool.tensor_scalar(self.var[:], self.mv[:].rearrange("p (t two) -> p t two", two=2)[:, :, 1],
                           EPS, None, ALU.add).then_inc(self.var_done, 1)
        pool.wait_ge(self.var_done, b + 1)
        pool.tensor_tensor(self.rstd[:], self.var[:], self.minus_half[:], ALU.pow).then_inc(self.rstd_done, 1)

    def dve_norm(self, dve, b):
        dve.wait_ge(self.rstd_done, b + 1)
        dve.wait_ge(self.xT_ready, b)
        for t in range(TILES):
            last = dve.tensor_scalar(self.xn[:, t * D:(t + 1) * D], tile_at(self.x, b, t),
                                     self.mv[:, 2 * t:2 * t + 1], self.rstd[:, t:t + 1],
                                     ALU.subtract, ALU.mult)
        last.then_inc(self.xn_done, 1)

    def pe_transpose(self, pe, b):
        pe.wait_ge(self.xn_done, b + 1)
        pe.wait_ge(self.xnT_done, b)
        for t in range(TILES):
            last = pe.transpose(self.xT[:, t * P:(t + 1) * P], self.xn[:, t * D:(t + 1) * D], self.ident[:])
        last.then_inc(self.xT_ready, 1)

    def act_copy(self, act, b, par):
        act.wait_ge(self.xT_ready, b + 1)
        act.copy(self.xnT[par][:], self.xT[:]).then_inc(self.xnT_done, 1)


class Router:

    WEIGHT = 0.5

    def __init__(self, ph, ln, iota, bg, logits_psum, top2, width, copies=(0,)):
        self.ln, self.iota, self.bg, self.top2, self.copies = ln, iota, bg, top2, copies
        self.lg_ps = logits_psum
        self.logits = ph.sb("logits", [P, TILES * EXPERTS])
        self.top = ph.sb("top", [P, TILES, 8])
        self.idx = ph.sb("idx", [P, TILES, 8], U32)
        self.idxf = ph.sb("idxf", [P, TILES, 8])
        self.comb = [ph.sb(f"comb{i}", [P, TILES, width]) for i in range(2)]
        if top2:
            self.neg_exp = ph.sb("neg_exp", [P, TILES, 2])
            self.one_plus = ph.sb("one_plus", [P, TILES, 2])
            self.score = ph.sb("score", [P, TILES, 2])
            self.total = ph.sb("total", [P, TILES, 1])
            self.inv_total = ph.sb("inv_total", [P, TILES, 1])
            self.share = ph.sb("share", [P, TILES, 2])
            self.pick = [ph.sb(f"pick{i}", [P, TILES, EXPERTS]) for i in range(2)]
            self.neg_exp_done = ph.sem("neg_exp_done")
            self.one_plus_done = ph.sem("one_plus_done")
            self.score_done = ph.sem("score_done")
            self.total_done = ph.sem("total_done")
            self.inv_done = ph.sem("inv_done")
            self.share_done = ph.sem("share_done")
            self.pick_done = ph.sem("pick_done")
        self.logits_ready = ph.sem("logits_ready")
        self.logits_done = ph.sem("logits_done")
        self.top_done = ph.sem("top_done")
        self.idx_done = ph.sem("idx_done")
        self.idxf_done = ph.sem("idxf_done")
        self.comb_done = ph.sem("comb_done")

    def pe_logits(self, pe, b, par, wg):
        pe.wait_ge(self.ln.xnT_done, b + 1)
        for t in range(TILES):
            last = pe.matmul(self.lg_ps[:, t * EXPERTS:(t + 1) * EXPERTS],
                             self.ln.xnT[par][:, t * P:(t + 1) * P], wg[:], start=True, stop=True)
        last.then_inc(self.logits_ready, 1)

    def act_exp(self, act, b):
        if self.top2:
            act.wait_ge(self.top_done, b + 1)
            act.activation(self.neg_exp[:], self.top[:, :, 0:2], ACT.Exp, scale=-1.0).then_inc(self.neg_exp_done, 1)

    def dve_choose(self, dve, b, par):
        dve.wait_ge(self.logits_ready, b + 1)
        dve.tensor_tensor(self.logits[:], self.lg_ps, self.bg[:], ALU.add).then_inc(self.logits_done, 1)
        wait_apart(dve, self.logits_done, b + 1, self.ln.passed)
        for t in range(TILES):
            last = dve.max(self.top[:, t, :], self.logits[:, t * 8:(t + 1) * 8])
        last.then_inc(self.top_done, 1)
        wait_apart(dve, self.top_done, b + 1, self.ln.passed)
        for t in range(TILES):
            last = dve.max_index(self.idx[:, t, :], self.top[:, t, :], self.logits[:, t * 8:(t + 1) * 8])
        last.then_inc(self.idx_done, 1)
        dve.wait_ge(self.idx_done, b + 1)
        dve.tensor_copy(self.idxf[:], self.idx[:]).then_inc(self.idxf_done, 1)
        dve.wait_ge(self.idxf_done, b + 1)
        if not self.top2:
            for t in range(TILES):
                last = dve.tensor_scalar(self.comb[par][:, t, :], self.iota[:], self.idxf[:, t, 0:1], self.WEIGHT,
                                         ALU.is_equal, ALU.mult)
            last.then_inc(self.comb_done, 1)

    def dve_weigh(self, dve, b, par):
        if self.top2:
            dve.wait_ge(self.neg_exp_done, b + 1)
            dve.tensor_scalar(self.one_plus[:], self.neg_exp[:], 1.0, None, ALU.add).then_inc(self.one_plus_done, 1)
            dve.wait_ge(self.one_plus_done, b + 1)
            dve.reciprocal(self.score[:], self.one_plus[:]).then_inc(self.score_done, 1)
            dve.wait_ge(self.score_done, b + 1)
            dve.scalar_tensor_tensor(self.total[:], self.score[:, :, 0:1], 1e-6, self.score[:, :, 1:2], ALU.add,
                                     ALU.add).then_inc(self.total_done, 1)
            dve.wait_ge(self.total_done, b + 1)
            dve.reciprocal(self.inv_total[:], self.total[:]).then_inc(self.inv_done, 1)
            dve.wait_ge(self.inv_done, b + 1)
            dve.scalar_tensor_tensor(self.share[:], self.score[:], self.WEIGHT,
                                     self.inv_total[:].to_broadcast([P, TILES, 2]), ALU.mult,
                                     ALU.mult).then_inc(self.share_done, 1)
            dve.wait_ge(self.share_done, b + 1)
            for i in range(2):
                for t in range(TILES):
                    last = dve.tensor_scalar(self.pick[i][:, t, :], self.iota[:], self.idxf[:, t, i:i + 1],
                                             self.share[:, t, i:i + 1], ALU.is_equal, ALU.mult)
            last.then_inc(self.pick_done, 1)
            dve.wait_ge(self.pick_done, b + 1)
            for at in self.copies:
                last = dve.tensor_tensor(self.comb[par][:, :, at:at + EXPERTS], self.pick[0][:], self.pick[1][:],
                                         ALU.add)
            last.then_inc(self.comb_done, 1)


class WeightSplit:

    def __init__(self, ph, parts, src):
        self.parts, self.src = parts, src
        self.raw = ph.sb("raw_weights", [P, W_COLS])
        self.raw_loaded = ph.sem("raw_loaded")
        self.hi_done = ph.sem("w_hi_done")

    def sp_load(self, sp):
        sp.dma_start(self.raw[:], self.src).then_inc(self.raw_loaded, 16)

    def pool_split(self, pool, b):
        own = bass.ds(b * (W_COLS // B), W_COLS // B)
        pool.wait_ge(self.raw_loaded, 16)
        pool.tensor_copy(self.parts[:, 0, own], self.raw[:, own]).then_inc(self.hi_done, 1)
        pool.wait_ge(self.hi_done, b + 1)
        pool.tensor_tensor(self.parts[:, 1, own], self.raw[:, own], self.parts[:, 0, own].bitcast(F32),
                           ALU.subtract)


def top1_ffn_phase(nc, name, x, ident, iota, w, x_in=None, first_loads=(), weight_split=None):
    E = EXPERTS
    units = E + 1
    H_PRE, Y_PRE = 4, 3
    with Phase(nc, name) as ph:
        w1 = ph.sb("w1", [P, E * P])
        w1_parts = ph.sb("w1_parts", [P, 2, E * P], F32R)
        xnT_parts = [ph.sb(f"xnT_parts{i}", [P, 2, S], F32R) for i in range(2)]
        b1 = ph.sb("b1", [P, E])
        w2 = ph.sb("w2", [P, E * D])
        b2 = ph.sb("b2", [E, D])
        wg = ph.sb("wg", [P, EXPERTS])
        bg = ph.sb("bg", [P, TILES * EXPERTS])
        hT = [ph.sb(f"hT{i}", [P, S]) for i in range(2)]
        combT = [ph.sb(f"combT{i}", [E, S]) for i in range(2)]
        h_ps = [ph.ps(f"h{i}", [P, S]) for i in range(4)]
        y_ps = [ph.ps(f"y{i}", [P, S]) for i in range(2)]
        t_ps = ph.ps("t", [P, S])
        c_ps = ph.ps("c", [P, S])
        lg_ps = t_ps[:, 0:TILES * EXPERTS]
        ln = LayerNorm(ph, x, ident, t_ps)
        router = Router(ph, ln, iota, bg, lg_ps, False, E)
        comb = router.comb
        prepare = WeightSplit(ph, *weight_split) if weight_split else None
        loaded = ph.sem("loaded")
        x_loaded = ph.sem("x_loaded")
        w1_hi_done = ph.sem("w1_hi_done")
        w1_split = ph.sem("w1_split")
        xnT_split = ph.sem("xnT_split")
        combT_ready = ph.sem("combT_ready")
        combT_done = ph.sem("combT_done")
        h_ready = ph.sem("h_ready")
        h_done = ph.sem("h_done")
        y_ready = ph.sem("y_ready")
        y_used = ph.sem("y_used")

        loads = [(w1[:], w["w1"]), (b1[:], w["b1"]), (w2[:], w["w2"]), (b2[:], w["b2"]), (wg[:], w["wg"]),
                 (bg[:], w["bg"].to_broadcast([P, TILES * EXPERTS]))]
        loads += first_loads
        later_loads = []
        if x_in is not None:
            x_loads = [(rows_at(x, b).rearrange("p (t h) -> p t h", t=TILES), x_in[b]) for b in range(B)]
            loads = x_loads[:1] + loads
            later_loads = x_loads[1:]
        all_loaded = 16 * len(loads)
        all_x_loaded = 16 * len(later_loads)

        def ring(b, par, per, k, slots):
            return (par * per + k) % slots

        with nc.Block() as block:

            @block.sync
            def _(sp):
                for dst, src in loads:
                    sp.dma_start(dst, src).then_inc(loaded, 16)
                for dst, src in later_loads:
                    sp.dma_start(dst, src).then_inc(x_loaded, 16)
                if prepare:
                    prepare.sp_load(sp)

            @block.gpsimd
            def _(pool):
                ln.pool_setup(pool)
                ln.pool_rstd(pool, 0)

                def body(b, par):
                    if has_next(b):
                        ln.pool_rstd(pool, b + 1)
                    if prepare:
                        prepare.pool_split(pool, b)
                over_batches(pool, body)

            @block.tensor
            def _(pe):
                pe.sem_inc(y_ready, Y_PRE)

                def transpose(b):
                    pe.wait_ge(router.logits_done, b)
                    ln.pe_transpose(pe, b)

                def comb_transpose(b, par):
                    pe.wait_ge(router.comb_done, b + 1)
                    pe.wait_ge(combT_done, b)
                    for t in range(TILES):
                        last = pe.matmul(c_ps[0:E, t * P:(t + 1) * P], comb[par][:, t, :], ident[:],
                                         start=True, stop=True)
                    last.then_inc(combT_ready, 1)

                def up(b, par, e):
                    pe.wait_ge(h_done, H_PRE + b * E + e - 3)
                    for i, (p, q) in enumerate(((0, 0), (1, 0), (0, 1))):
                        last = pe.matmul(h_ps[ring(b, par, E, e, 4)][:], w1_parts[:, p, e * P:(e + 1) * P],
                                         xnT_parts[par][:, q, :], start=i == 0, stop=i == 2)
                    last.then_inc(h_ready, 1)

                def down(b, par, e):
                    y = y_ps[ring(b, par, units, e, 2)]
                    h = hT[ring(b, par, E, e, 2)]
                    pe.wait_ge(h_done, H_PRE + b * E + e + 1)
                    pe.wait_ge(y_used, Y_PRE + b * units + e - 1)
                    for t in range(TILES):
                        last = pe.matmul(y[:, t * D:(t + 1) * D], h[:, t * P:(t + 1) * P],
                                         w2[:, e * D:(e + 1) * D], start=True, stop=True)
                    last.then_inc(y_ready, 1)

                def bias_term(b, par):
                    y = y_ps[ring(b, par, units, E, 2)]
                    pe.wait_ge(combT_done, b + 1)
                    pe.wait_ge(y_used, Y_PRE + b * units + E - 1)
                    for t in range(TILES):
                        last = pe.matmul(y[:, t * D:(t + 1) * D], combT[par][:, t * P:(t + 1) * P], b2[:],
                                         start=True, stop=True)
                    last.then_inc(y_ready, 1)

                pe.wait_ge(loaded, all_loaded)
                transpose(0)
                router.pe_logits(pe, 0, 0, wg)
                comb_transpose(0, 0)
                pe.wait_ge(w1_split, 1)

                def body(b, par):
                    for e in range(E):
                        if e == 0:
                            pe.wait_ge(xnT_split, b + 1)
                        up(b, par, e)
                        if e:
                            down(b, par, e - 1)
                        if has_next(b):
                            if e == 3:
                                transpose(b + 1)
                            if e == 5:
                                router.pe_logits(pe, b + 1, 1 - par, wg)
                            if e == 7:
                                comb_transpose(b + 1, 1 - par)
                    down(b, par, E - 1)
                    bias_term(b, par)
                over_batches(pe, body)

            @block.scalar
            def _(act):
                act.sem_inc(h_done, H_PRE)
                act.wait_ge(loaded, all_loaded)

                def copy_xnT(b, par):
                    act.wait_ge(ln.xT_ready, b + 1)
                    act.copy(xnT_parts[par][:, 0, :], t_ps[:])
                    act.copy(ln.xnT[par][:], t_ps[:]).then_inc(ln.xnT_done, 1)

                copy_xnT(0, 0)

                def body(b, par):
                    for e in range(E):
                        h = hT[ring(b, par, E, e, 2)]
                        before = e - 2 if e >= 2 else e - 3
                        act.wait_ge(y_ready, Y_PRE + b * units + before + 1)
                        act.wait_ge(h_ready, b * E + e + 1)
                        act.activation(h[:], h_ps[ring(b, par, E, e, 4)][:], ACT.Gelu, bias=b1[:, e:e + 1],
                                       scale=1.0).then_inc(h_done, 1)
                        if has_next(b) and e == 4:
                            copy_xnT(b + 1, 1 - par)
                over_batches(act, body)

            @block.vector
            def _(dve):
                dve.sem_inc(y_used, Y_PRE)
                dve.wait_ge(loaded, all_loaded)

                def comb_copy(b, par):
                    dve.wait_ge(combT_ready, b + 1)
                    dve.tensor_copy(combT[par][:], c_ps[0:E, :]).then_inc(combT_done, 1)

                def add(b, par, e):
                    y = y_ps[ring(b, par, units, e, 2)]
                    dve.wait_ge(y_ready, Y_PRE + b * units + e + 1)
                    dve.wait_ge(y_used, Y_PRE + b * units + e)
                    if e < E:
                        for t in range(TILES):
                            last = dve.scalar_tensor_tensor(tile_at(x, b, t), y[:, t * D:(t + 1) * D],
                                                            comb[par][:, t, e:e + 1], tile_at(x, b, t),
                                                            ALU.mult, ALU.add)
                    else:
                        last = dve.tensor_tensor(rows_at(x, b), y[:], rows_at(x, b), ALU.add)
                    last.then_inc(y_used, 1)

                def split_xnT(b, par):
                    dve.wait_ge(ln.xnT_done, b + 1)
                    dve.tensor_tensor(xnT_parts[par][:, 1, :], ln.xnT[par][:],
                                      xnT_parts[par][:, 0, :].bitcast(F32), ALU.subtract).then_inc(xnT_split, 1)

                ln.dve_stats(dve, 0)
                ln.dve_norm(dve, 0)
                split(dve, w1_parts[:, 0, :], w1_parts[:, 1, :], w1[:], w1_hi_done, 1).then_inc(w1_split, 1)
                split_xnT(0, 0)
                router.dve_choose(dve, 0, 0)
                comb_copy(0, 0)

                def body(b, par):
                    dve.wait_ge(router.comb_done, b + 1)
                    for e in range(E):
                        if has_next(b):
                            if e == 0:
                                if later_loads:
                                    dve.wait_ge(x_loaded, all_x_loaded)
                                ln.dve_stats(dve, b + 1)
                            if e == 1:
                                ln.dve_norm(dve, b + 1)
                            if e == 5:
                                split_xnT(b + 1, 1 - par)
                                router.dve_choose(dve, b + 1, 1 - par)
                            if e == 7:
                                comb_copy(b + 1, 1 - par)
                        add(b, par, e)
                    add(b, par, E)
                over_batches(dve, body)


def top2_ffn_phase(nc, name, x, ident, iota, w, w_parts, parts_loaded=None, store_to=None):
    E = EXPERTS + 1
    C = 4
    SHARED = Router.WEIGHT * float(np.float32(0.1))
    CW = LO_ROW + E
    PRODUCTS = ((0, 0), (1, 0), (0, 1))
    with Phase(nc, name) as ph:
        b1 = ph.sb("b1", [P, E * C])
        b2 = ph.sb("b2", [CW, D])
        wg = ph.sb("wg", [P, EXPERTS])
        bg = ph.sb("bg", [P, TILES * EXPERTS])
        b2_parts = ph.sb("b2_parts", [CW, 2, D], F32R)
        sel = ph.sb("sel", [CW, E, P], F32R)
        h32 = ph.sb("h32", [P, C, S])
        hT = [ph.sb(f"hT{i}", [P, 2, C, S], F32R) for i in range(2)]
        xnT_parts = [ph.sb(f"xnT_parts{i}", [P, 2, S], F32R) for i in range(2)]
        combT = [ph.sb(f"combT{i}", [CW, S], F32R) for i in range(2)]
        comb_all = [ph.sb(f"comb_all{i}", [P, S]) for i in range(2)]
        weighted = [ph.sb(f"weighted{i}", [P, S]) for i in range(2)]
        acc = [ph.sb(f"acc{i}", [P, S]) for i in range(2)]
        h_ps = [ph.ps(f"h{i}", [P, S]) for i in range(3)]
        y_ps = [ph.ps(f"y{i}", [P, S]) for i in range(2)]
        comb_ps = ph.ps("comb_ps", [P, S])
        t_ps = ph.ps("t", [P, S])
        c_ps = ph.ps("c", [P, S])
        ln = LayerNorm(ph, x, ident, t_ps)
        router = Router(ph, ln, iota, bg, t_ps[:, 0:TILES * EXPERTS], True, CW, (0, LO_ROW))
        comb = router.comb
        loaded = ph.sem("loaded")
        zero_done = ph.sem("zero_done")
        const_done = ph.sem("const_done")
        b2_hi_done = ph.sem("b2_hi_done")
        xnT_split = ph.sem("xnT_split")
        combT_ready = ph.sem("combT_ready")
        combT_hi = ph.sem("combT_hi")
        combT_done = ph.sem("combT_done")
        bias_ready = ph.sem("bias_ready")
        acc_set = ph.sem("acc_set")
        back_ready = ph.sem("back_ready")
        x_done = ph.sem("x_done")
        h_ready = ph.sem("h_ready")
        h_done = ph.sem("h_done")
        hi_done = ph.sem("hi_done")
        h_split = ph.sem("h_split")
        comb_ready = ph.sem("comb_ready")
        comb_copied = ph.sem("comb_copied")
        y_ready = ph.sem("y_ready")
        y_used = ph.sem("y_used")
        summed = ph.sem("summed")
        stored = ph.sem("stored")

        loads = [(b1[:], w["b1"]), (b2[:], w["b2"]), (wg[:], w["wg"]),
                 (bg[:], w["bg"].to_broadcast([P, TILES * EXPERTS]))]
        all_loaded = 16 * len(loads)

        def slot(par, e, slots):
            return (par * E + e) % slots

        with nc.Block() as block:

            @block.sync
            def _(sp):
                for dst, src in loads:
                    sp.dma_start(dst, src).then_inc(loaded, 16)
                if store_to is not None:
                    for half in range(2):
                        with sp.Fori(0, B // 2) as i:
                            wait_apart(sp, x_done, i + half * (B // 2) + 1, ln.passed)
                            for t in range(TILES):
                                sp.dma_start(token_rows(store_to, half, i * TILES + t),
                                             tile_at(x, i + half * (B // 2), t)).then_inc(stored, 16)
                    sp.wait_ge(stored, 16 * B * TILES)

            @block.gpsimd
            def _(pool):
                ln.pool_setup(pool)
                ln.pool_rstd(pool, 0)

                def body(b, par):
                    if has_next(b):
                        ln.pool_rstd(pool, b + 1)
                    pool.wait_ge(acc_set, b + 1)
                    for e in range(E):
                        N = b * E + e
                        wait_from(pool, summed, N)
                        pool.wait_ge(y_used, N + 1)
                        pool.tensor_tensor(acc[par][:], acc[par][:], weighted[slot(par, e, 2)][:],
                                           ALU.add).then_inc(summed, 1)
                over_batches(pool, body, peel_first=True)

            @block.tensor
            def _(pe):
                def transpose(b):
                    wait_from(pe, router.logits_done, b)
                    ln.pe_transpose(pe, b)

                def comb_transpose(b, par):
                    pe.wait_ge(router.comb_done, b + 1)
                    wait_from(pe, x_done, b - 1)
                    for t in range(TILES):
                        last = pe.matmul(c_ps[0:CW, t * P:(t + 1) * P], comb[par][:, t, :], ident[:],
                                         start=True, stop=True)
                    last.then_inc(combT_ready, 1)

                def bias_term(b, par):
                    pe.wait_ge(combT_done, b + 1)
                    for a in range(2):
                        last = pe.matmul(c_ps[:], b2_parts[:, a, :], combT[par][:], start=a == 0, stop=a == 1)
                    last.then_inc(bias_ready, 1)

                def back(b, par):
                    pe.wait_ge(summed, (b + 1) * E)
                    pe.wait_ge(acc_set, b + 2 if has_next(b) else B)
                    for t in range(TILES):
                        last = pe.transpose(c_ps[:, t * D:(t + 1) * D], acc[par][:, t * P:(t + 1) * P], ident[:])
                    last.then_inc(back_ready, 1)

                def up(b, par, e):
                    for c in range(C):
                        K = (b * E + e) * C + c
                        k = e * C + c
                        wait_from(pe, h_done, K - 2)
                        for i, (p, q) in enumerate(PRODUCTS):
                            last = pe.matmul(h_ps[((par * E + e) * C + c) % 3][:],
                                             w_parts[:, p, k * P:(k + 1) * P], xnT_parts[par][:, q, :],
                                             start=i == 0, stop=i == 2)
                        last.then_inc(h_ready, 1)

                def down(b, par, e):
                    N = b * E + e
                    wait_from(pe, comb_copied, N)
                    pe.matmul(comb_ps[:], sel[:, e, :], combT[par][:], start=True, stop=True).then_inc(comb_ready, 1)
                    wait_from(pe, y_used, N - 1)
                    for c in range(C):
                        pe.wait_ge(h_split, N * C + c + 1)
                        k = E * C + e * C + c
                        for i, (p, q) in enumerate(PRODUCTS):
                            last = pe.matmul(y_ps[slot(par, e, 2)][:], w_parts[:, p, k * D:(k + 1) * D],
                                             hT[slot(par, e, 2)][:, q, c, :],
                                             start=c == 0 and i == 0, stop=c == C - 1 and i == 2)
                    last.then_inc(y_ready, 1)

                pe.wait_ge(loaded, all_loaded)
                pe.wait_ge(const_done, 1)
                transpose(0)
                router.pe_logits(pe, 0, 0, wg)
                comb_transpose(0, 0)
                if parts_loaded is not None:
                    pe.wait_ge(parts_loaded, 16)

                def body(b, par):
                    pe.wait_ge(xnT_split, b + 1)
                    for e in range(E):
                        up(b, par, e)
                        if e:
                            down(b, par, e - 1)
                        elif has_previous(b):
                            down(b - 1, 1 - par, E - 1)
                        if e == 0:
                            bias_term(b, par)
                        if e == 3 and has_previous(b):
                            back(b - 1, 1 - par)
                        if has_next(b):
                            if e == 2:
                                transpose(b + 1)
                            if e == 4:
                                router.pe_logits(pe, b + 1, 1 - par, wg)
                            if e == 7:
                                comb_transpose(b + 1, 1 - par)
                over_batches(pe, body, peel_first=True)
                down(B - 1, 1, E - 1)
                back(B - 1, 1)

            @block.scalar
            def _(act):
                act.wait_ge(loaded, all_loaded)

                def copy_xnT(b, par):
                    act.wait_ge(ln.xT_ready, b + 1)
                    act.copy(xnT_parts[par][:, 0, :], t_ps[:])
                    act.copy(ln.xnT[par][:], t_ps[:]).then_inc(ln.xnT_done, 1)

                def copy_comb(b, par, e):
                    N = b * E + e
                    act.wait_ge(comb_ready, N + 1)
                    wait_from(act, y_used, N - 1)
                    act.copy(comb_all[slot(par, e, 2)][:], comb_ps[:]).then_inc(comb_copied, 1)

                copy_xnT(0, 0)
                router.act_exp(act, 0)

                def body(b, par):
                    for e in range(E):
                        N = b * E + e
                        wait_from(act, y_ready, N - 1)
                        for c in range(C):
                            K = N * C + c
                            act.wait_ge(h_ready, K + 1)
                            wait_from(act, h_split, K - 3)
                            h = h_ps[((par * E + e) * C + c) % 3]
                            bias = b1[:, e * C + c:e * C + c + 1]
                            last = act.activation(h32[:, c, :], h[:], ACT.Gelu, bias=bias, scale=1.0)
                            if c % 2:
                                last = act.activation(hT[slot(par, e, 2)][:, 0, c, :], h[:], ACT.Gelu, bias=bias,
                                                      scale=1.0)
                            last.then_inc(h_done, 1)
                        if e:
                            copy_comb(b, par, e - 1)
                        elif has_previous(b):
                            copy_comb(b - 1, 1 - par, E - 1)
                        if e == 0:
                            act.wait_ge(bias_ready, b + 1)
                            wait_from(act, back_ready, b - 1)
                            act.copy(acc[par][:], c_ps[:]).then_inc(acc_set, 1)
                        if has_next(b):
                            if e == 3:
                                copy_xnT(b + 1, 1 - par)
                            if e == 6:
                                router.act_exp(act, b + 1)
                over_batches(act, body, peel_first=True)
                copy_comb(B - 1, 1, E - 1)

            @block.vector
            def _(dve):
                dve.memset(sel[:].bitcast(F32), 0.0)
                for i in range(2):
                    last = dve.memset(comb[i][:], 0.0)
                last.then_inc(zero_done, 1)
                dve.wait_ge(zero_done, 1)
                for at in (0, LO_ROW):
                    dve.tensor_copy(sel[at:at + E, :, :],
                                    ident[at:at + E, at:at + E].rearrange("p (e m) -> p e m", m=1).to_broadcast([E, E, P]))
                    for i in range(2):
                        dve.memset(comb[i][:, :, at + EXPERTS:at + E], SHARED)
                dve.wait_ge(loaded, all_loaded)
                split(dve, b2_parts[:, 0, :], b2_parts[:, 1, :], b2[:], b2_hi_done, 1).then_inc(const_done, 1)

                def split_xnT(b, par):
                    dve.wait_ge(ln.xnT_done, b + 1)
                    dve.tensor_tensor(xnT_parts[par][:, 1, :], ln.xnT[par][:],
                                      xnT_parts[par][:, 0, :].bitcast(F32), ALU.subtract).then_inc(xnT_split, 1)

                def split_combT(b, par):
                    dve.wait_ge(combT_ready, b + 1)
                    dve.tensor_copy(combT[par][:], c_ps[0:CW, :]).then_inc(combT_hi, 1)
                    dve.wait_ge(combT_hi, b + 1)
                    lo = combT[par][LO_ROW:CW, :]
                    dve.tensor_tensor(lo, c_ps[LO_ROW:CW, :], lo.bitcast(F32), ALU.subtract).then_inc(combT_done, 1)

                def split_hidden(b, par, e):
                    N = b * E + e
                    for c in range(C):
                        K = N * C + c
                        hi, lo = (hT[slot(par, e, 2)][:, a, c, :] for a in range(2))
                        dve.wait_ge(h_done, K + 1)
                        if c % 2 == 0:
                            dve.tensor_copy(hi, h32[:, c, :]).then_inc(hi_done, 1)
                            dve.wait_ge(hi_done, N * (C // 2) + c // 2 + 1)
                        dve.tensor_tensor(lo, h32[:, c, :], hi.bitcast(F32), ALU.subtract).then_inc(h_split, 1)

                def weigh(b, par, e):
                    N = b * E + e
                    dve.wait_ge(comb_copied, N + 1)
                    dve.wait_ge(y_ready, N + 1)
                    wait_from(dve, summed, N - 1)
                    dve.tensor_tensor(weighted[slot(par, e, 2)][:], y_ps[slot(par, e, 2)][:],
                                      comb_all[slot(par, e, 2)][:], ALU.mult).then_inc(y_used, 1)

                def add(b):
                    dve.wait_ge(back_ready, b + 1)
                    dve.tensor_tensor(rows_at(x, b), c_ps[:], rows_at(x, b), ALU.add).then_inc(x_done, 1)

                ln.dve_stats(dve, 0)
                ln.dve_norm(dve, 0)
                split_xnT(0, 0)
                router.dve_choose(dve, 0, 0)
                router.dve_weigh(dve, 0, 0)
                split_combT(0, 0)

                def body(b, par):
                    for e in range(E):
                        split_hidden(b, par, e)
                        if has_next(b):
                            if e == 0:
                                ln.dve_stats(dve, b + 1)
                            if e == 1:
                                ln.dve_norm(dve, b + 1)
                            if e == 3:
                                split_xnT(b + 1, 1 - par)
                            if e == 5:
                                router.dve_choose(dve, b + 1, 1 - par)
                            if e == 6:
                                router.dve_weigh(dve, b + 1, 1 - par)
                            if e == 8:
                                split_combT(b + 1, 1 - par)
                        if e == 4 and has_previous(b):
                            add(b - 1)
                        if e:
                            weigh(b, par, e - 1)
                        elif has_previous(b):
                            weigh(b - 1, 1 - par, E - 1)
                over_batches(dve, body, peel_first=True)
                weigh(B - 1, 1, E - 1)
                add(B - 1)


def decay_attention_phase(nc, x, ident, w, w_parts, w_parts_out):
    with Phase(nc, "dec") as ph:
        wrkv = ph.sb("wrkv", [P, 3 * D])
        brkv = ph.sb("brkv", [P, 3])
        wo = ph.sb("wo", [P, D])
        bo = ph.sb("bo", [P, S])
        nu_log = ph.sb("nu_log", [P, 1])
        gamma_log = ph.sb("gamma_log", [P, 1])
        nu = ph.sb("nu", [P, 1])
        lam = ph.sb("lam", [P, 1])
        egamma = ph.sb("egamma", [P, 1])
        gamma = ph.sb("gamma", [P, 1])
        neg_br = ph.sb("neg_br", [P, 1])
        zeros = ph.sb("zeros", [P, S])
        lam_row = ph.sb("lam_row", [P, S])
        er = [ph.sb(f"er{i}", [P, S]) for i in range(2)]
        k = [ph.sb(f"k{i}", [P, S]) for i in range(2)]
        er1 = ph.sb("one_plus_er", [P, S])
        kv = ph.sb("kv", [P, S])
        u1 = ph.sb("u1", [P, S])
        u2 = ph.sb("u2", [P, S])
        num = ph.sb("num", [P, S])
        den = ph.sb("den", [P, S])
        den_r = ph.sb("den_r", [P, S])
        inv = ph.sb("inv", [P, S])
        mixed = ph.sb("mixed", [P, S])
        rkv_ps = [[ph.ps(f"{n}_ps{i}", [P, S]) for n in "rkv"] for i in range(2)]
        t_ps = ph.ps("t", [P, S])
        o_ps = ph.ps("o", [P, S])
        ln = LayerNorm(ph, x, ident, t_ps)
        loaded = ph.sem("loaded")
        parts_stored = ph.sem("parts_stored")
        nu_done, lam_done, sum_done, egamma_done = ph.sem("nu"), ph.sem("lam"), ph.sem("nugamma"), ph.sem("egamma")
        const_done = ph.sem("const_done")
        lam_row_done = ph.sem("lam_row_done")
        rkv_ready = ph.sem("rkv_ready")
        act_done = ph.sem("act_done")
        er1_done = ph.sem("er1_done")
        kv_done = ph.sem("kv_done")
        scan_done = ph.sem("scan_done")
        frac_done = ph.sem("frac_done")
        den_r_done = ph.sem("den_r_done")
        inv_done = ph.sem("inv_done")
        mixed_done = ph.sem("mixed_done")
        o_ready = ph.sem("o_ready")
        o_used = ph.sem("o_used")
        x_done = ph.sem("x_done")
        loads = [(wrkv[:], w["wrkv"]), (brkv[:], w["brkv"]), (wo[:], w["wo"]),
                 (bo[:], w["bo"].to_broadcast([P, S])), (nu_log[:], w["nu_log"]),
                 (gamma_log[:], w["gamma_log"])]
        all_loaded = 16 * len(loads)

        with nc.Block() as block:

            @block.sync
            def _(sp):
                for dst, src in loads:
                    sp.dma_start(dst, src).then_inc(loaded, 16)
                sp.dma_start(w_parts_out, w_parts[:].bitcast(F32)).then_inc(parts_stored, 16)
                sp.wait_ge(parts_stored, 16)

            @block.gpsimd
            def _(pool):
                ln.pool_setup(pool)
                pool.wait_ge(loaded, all_loaded)
                ln.pool_rstd(pool, 0)
                ln.pool_rstd(pool, 1)

                def add_bias(b):
                    pool.wait_ge(o_used, b + 1)
                    pool.tensor_tensor(rows_at(x, b), rows_at(x, b), bo[:], ALU.add).then_inc(x_done, 1)

                def body(b, par):
                    pool.wait_ge(act_done, b + 1)
                    if has_previous(b):
                        wait_apart(pool, den_r_done, b, ln.passed)
                    pool.tensor_scalar(er1[:], er[par][:], 1.0, None, ALU.add).then_inc(er1_done, 1)
                    if has_next(b) and has_next(b + 1):
                        ln.pool_rstd(pool, b + 2)
                    if has_previous(b):
                        add_bias(b - 1)
                over_batches(pool, body, peel_first=True)
                add_bias(B - 1)

            @block.tensor
            def _(pe):
                def project(b, par):
                    pe.wait_ge(ln.xnT_done, b + 1)
                    wait_from(pe, kv_done, b - 1)
                    for i in range(3):
                        last = pe.matmul(rkv_ps[par][i][:], wrkv[:, i * D:(i + 1) * D], ln.xnT[par][:],
                                         start=True, stop=True)
                    last.then_inc(rkv_ready, 1)

                pe.wait_ge(loaded, all_loaded)
                ln.pe_transpose(pe, 0)
                project(0, 0)

                def body(b, par):
                    if has_next(b):
                        ln.pe_transpose(pe, b + 1)
                        project(b + 1, 1 - par)
                    pe.wait_ge(mixed_done, b + 1)
                    for t in range(TILES):
                        last = pe.matmul(o_ps[:, t * D:(t + 1) * D], mixed[:, t * P:(t + 1) * P], wo[:],
                                         start=True, stop=True)
                    last.then_inc(o_ready, 1)
                over_batches(pe, body, peel_first=True)

            @block.scalar
            def _(act):
                act.wait_ge(loaded, all_loaded)
                act.activation(nu[:], nu_log[:], ACT.Exp).then_inc(nu_done, 1)
                act.wait_ge(nu_done, 1)
                act.activation(lam[:], nu[:], ACT.Exp, scale=-1.0).then_inc(lam_done, 1)
                act.activation(egamma[:], nu_log[:], ACT.Exp, bias=gamma_log[:]).then_inc(egamma_done, 1)
                act.wait_ge(const_done, 1)
                act.wait_ge(lam_done, 1)
                act.activation(lam_row[:], zeros[:], ACT.Identity, bias=lam[:]).then_inc(lam_row_done, 1)

                def exponentials(b, par):
                    act.wait_ge(rkv_ready, b + 1)
                    wait_from(act, er1_done, b - 1)
                    wait_from(act, frac_done, b - 1)
                    act.activation(er[par][:], rkv_ps[par][0][:], ACT.Exp, bias=neg_br[:], scale=-1.0)
                    act.activation(k[par][:], rkv_ps[par][1][:], ACT.Exp, bias=brkv[:, 1:2]).then_inc(act_done, 1)

                ln.act_copy(act, 0, 0)
                exponentials(0, 0)

                def body(b, par):
                    if has_next(b):
                        ln.act_copy(act, b + 1, 1 - par)
                        exponentials(b + 1, 1 - par)
                over_batches(act, body, peel_first=True)

            @block.vector
            def _(dve):
                dve.memset(zeros[:], 0.0)
                dve.wait_ge(loaded, all_loaded)
                dve.tensor_scalar(neg_br[:], brkv[:, 0:1], -1.0, None, ALU.mult).then_inc(const_done, 1)
                dve.wait_ge(egamma_done, 1)
                dve.tensor_scalar(gamma[:], egamma[:], -1.0, None, ALU.add).then_inc(sum_done, 1)
                dve.wait_ge(sum_done, 1)
                dve.wait_ge(lam_row_done, 1)
                ln.dve_stats(dve, 0)
                ln.dve_norm(dve, 0)
                ln.dve_stats(dve, 1)

                def add(b):
                    dve.wait_ge(o_ready, b + 1)
                    dve.tensor_tensor(rows_at(x, b), o_ps[:], rows_at(x, b), ALU.add).then_inc(o_used, 1)

                def body(b, par):
                    if has_next(b):
                        ln.dve_norm(dve, b + 1)
                    dve.wait_ge(act_done, b + 1)
                    dve.scalar_tensor_tensor(kv[:], rkv_ps[par][2][:], brkv[:, 2:3], k[par][:], ALU.add,
                                             ALU.mult).then_inc(kv_done, 1)
                    dve.tensor_tensor_scan(u2[:], lam_row[:], k[par][:], 0.0, ALU.mult, ALU.add)
                    dve.wait_ge(kv_done, b + 1)
                    dve.tensor_tensor_scan(u1[:], lam_row[:], kv[:], 0.0, ALU.mult, ALU.add).then_inc(scan_done, 1)
                    if has_next(b) and has_next(b + 1):
                        ln.dve_stats(dve, b + 2)
                    if has_previous(b):
                        add(b - 1)
                    dve.wait_ge(scan_done, b + 1)
                    dve.scalar_tensor_tensor(den[:], k[par][:], gamma[:], u2[:], ALU.mult, ALU.add)
                    dve.scalar_tensor_tensor(num[:], kv[:], gamma[:], u1[:], ALU.mult,
                                             ALU.add).then_inc(frac_done, 1)
                    dve.wait_ge(frac_done, b + 1)
                    dve.wait_ge(er1_done, b + 1)
                    dve.scalar_tensor_tensor(den_r[:], den[:], 1e-6, er1[:], ALU.add,
                                             ALU.mult).then_inc(den_r_done, 1)
                    dve.wait_ge(den_r_done, b + 1)
                    dve.reciprocal(inv[:], den_r[:]).then_inc(inv_done, 1)
                    dve.wait_ge(inv_done, b + 1)
                    dve.tensor_tensor(mixed[:], num[:], inv[:], ALU.mult).then_inc(mixed_done, 1)
                over_batches(dve, body, peel_first=True)
                add(B - 1)


def split(dve, hi, lo, value, done, count):
    dve.tensor_copy(hi, value).then_inc(done, 1)
    dve.wait_ge(done, count)
    return dve.tensor_tensor(lo, value, hi.bitcast(F32), ALU.subtract)


def qkv_phase(nc, x, ident, w, v_all, scratch):
    SCALE = float(1.0 / np.sqrt(np.float32(HD)))
    STORES = 16 * 2 * (SPANS + 2)
    FREE_BANKS = 2
    with Phase(nc, "qkv") as ph:
        wq, wk, wv, wp = (ph.sb(n, [P, D]) for n in ("wq", "wk", "wv", "wp"))
        bq, bk, bp, u, v = (ph.sb(n, [P, 1]) for n in ("bq", "bk", "bp", "u", "v"))
        bv = ph.sb("bv", [P, S])
        embT = ph.sb("embT", [P, S])
        bias_u, bias_v = ph.sb("bias_u", [P, 1]), ph.sb("bias_v", [P, 1])
        sum_u, sum_v = ph.sb("sum_u", [P, 1]), ph.sb("sum_v", [P, 1])
        qu = [ph.sb(f"qu{i}", [P, S]) for i in range(2)]
        qv = [ph.sb(f"qv{i}", [P, S]) for i in range(2)]
        kT = [ph.sb(f"kT{i}", [P, S]) for i in range(2)]
        qu_parts = [ph.sb(f"qu_parts{i}", [P, 2, S], F32R) for i in range(2)]
        k_parts = [ph.sb(f"k_parts{i}", [P, 2, S], F32R) for i in range(2)]
        qv_parts = ph.sb("qv_parts", [P, 2 * SPANS * ROWS * B * SPAN], F32R)
        pos = ph.sb("pos", [P, S])
        pos_parts = ph.sb("pos_parts", [P, 2, POS_W], F32R)
        q_ps = [ph.ps(f"qps{i}", [P, S]) for i in range(2)]
        k_ps = [ph.ps(f"kps{i}", [P, S]) for i in range(2)]
        v_ps = [ph.ps(f"vps{i}", [P, S]) for i in range(2)]
        t_ps = ph.ps("t", [P, S])
        pos_ps = ph.ps("pos_ps", [P, S])
        ln = LayerNorm(ph, x, ident, t_ps)
        loaded = ph.sem("loaded")
        sums_done = ph.sem("sums_done")
        bias_done = ph.sem("bias_done")
        pos_ready = ph.sem("pos_ready")
        pos_done = ph.sem("pos_done")
        pos_hi_done = ph.sem("pos_hi_done")
        pos_split = ph.sem("pos_split")
        qkv_ready = ph.sem("qkv_ready")
        qk_done = ph.sem("qk_done")
        hi_done = ph.sem("hi_done")
        qk_split = ph.sem("qk_split")
        v_done = ph.sem("v_done")
        parts_used = ph.sem("parts_used")
        stored = ph.sem("stored")
        stored_qk = [ph.sem(f"stored_qk{i}") for i in range(2)]
        loads = [(wq[:], w["wq"]), (wk[:], w["wk"]), (wv[:], w["wv"]), (wp[:], w["wp"]), (bq[:], w["bq"]),
                 (bk[:], w["bk"]), (bp[:], w["bp"]), (u[:], w["u"]), (v[:], w["v"]),
                 (bv[:], w["bv"].to_broadcast([P, S])), (embT[:], w["embT"])]
        all_loaded = 16 * len(loads)
        qv_view = qv_parts[:].rearrange("p (t s r b g) -> p t s r b g", t=2, s=SPANS, r=ROWS, b=B)

        with nc.Block() as block:

            @block.sync
            def _(sp):
                for par in range(2):
                    sp.sem_inc(stored_qk[par], STORES)
                for dst, src in loads:
                    sp.dma_start(dst, src).then_inc(loaded, 16)
                for b in range(B):
                    sp.dma_start(x_out(scratch, b), rows_at(x, b).rearrange("p (t h) -> p t h", t=TILES))\
                        .then_inc(stored, 16)
                sp.wait_ge(pos_split, 3)
                sp.dma_start(scratch["pos"], pos_parts[:].bitcast(F32)).then_inc(stored, 16)

                for half in range(2):
                    with sp.Fori(half * (HALF // 2), (half + 1) * (HALF // 2)) as i:
                        for par in range(2):
                            b = 2 * i + par
                            wait_apart(sp, qk_split, b + 1, ln.passed)
                            for part in range(2):
                                for span in range(SPANS):
                                    sp.dma_start(qu_out(scratch, b, part, span),
                                                 qu_parts[par][:, part, span * QU_ROW:(span + 1) * QU_ROW]
                                                 .bitcast(F32)).then_inc(stored_qk[par], 16)
                                for copy in range(2):
                                    sp.dma_start(k_out(scratch, b, part, copy),
                                                 k_parts[par][:, part, :].bitcast(F32)).then_inc(stored_qk[par], 16)
                    for span in range(SPANS):
                        for part in range(2):
                            sp.dma_start(qv_out(scratch, span, half, part),
                                         qv_view[:, part, span, :, half * HALF:(half + 1) * HALF, :]
                                         .rearrange("p r b g -> p r (b g)").bitcast(F32)).then_inc(stored, 16)
                sp.wait_ge(stored, 16 * (B + 1 + 4 * SPANS))
                for par in range(2):
                    sp.wait_ge(stored_qk[par], (B // 2 + 1) * STORES)

            @block.gpsimd
            def _(pool):
                ln.pool_setup(pool)
                ln.pool_rstd(pool, 0)
                ln.pool_rstd(pool, 1)

                def body(b, par):
                    if has_next(b + 1):
                        ln.pool_rstd(pool, b + 2)
                over_batches(pool, body)

            @block.tensor
            def _(pe):
                pe.wait_ge(loaded, all_loaded)
                pe.matmul(pos_ps[:], wp[:], embT[:], start=True, stop=True).then_inc(pos_ready, 1)
                ln.pe_transpose(pe, 0)

                def body(b, par):
                    if has_next(b):
                        ln.pe_transpose(pe, b + 1)
                    pe.wait_ge(ln.xnT_done, b + 1)
                    pe.wait_ge(v_done, FREE_BANKS + b - 1)
                    pe.wait_ge(qk_done, FREE_BANKS + b - 1)
                    pe.matmul(q_ps[par][:], wq[:], ln.xnT[par][:], start=True, stop=True)
                    pe.matmul(k_ps[par][:], wk[:], ln.xnT[par][:], start=True, stop=True)
                    for t in range(TILES):
                        last = pe.matmul(v_ps[par][:, t * D:(t + 1) * D], ln.xnT[par][:, t * P:(t + 1) * P],
                                         wv[:], start=True, stop=True)
                    last.then_inc(qkv_ready, 1)
                over_batches(pe, body)

            @block.scalar
            def _(act):
                act.sem_inc(qk_done, FREE_BANKS)
                act.wait_ge(bias_done, 1)
                act.wait_ge(pos_ready, 1)
                act.activation(pos[:], pos_ps[:], ACT.Identity, bias=bp[:]).then_inc(pos_done, 1)
                ln.act_copy(act, 0, 0)

                def body(b, par):
                    if has_next(b):
                        ln.act_copy(act, b + 1, 1 - par)
                    act.wait_ge(qkv_ready, b + 1)
                    act.wait_ge(parts_used, b + 1)
                    for s in range(SPANS):
                        view = q_ps[par][:, s * (S // SPANS):(s + 1) * (S // SPANS)].rearrange("p (g r) -> p r g", r=ROWS)
                        for dst, bias in ((qu, bias_u), (qv, bias_v)):
                            act.activation(dst[par][:, s * (S // SPANS):(s + 1) * (S // SPANS)]
                                           .rearrange("p (r g) -> p r g", r=ROWS),
                                           view, ACT.Identity, bias=bias[:], scale=SCALE)
                    act.activation(kT[par][:], k_ps[par][:], ACT.Identity, bias=bk[:]).then_inc(qk_done, 1)
                over_batches(act, body)

            @block.vector
            def _(dve):
                dve.sem_inc(v_done, FREE_BANKS)
                dve.sem_inc(parts_used, 2)
                dve.memset(pos_parts[:, :, 0:POS_0].bitcast(F32), 0.0)
                dve.memset(pos_parts[:, :, POS_0 + S:POS_W].bitcast(F32), 0.0).then_inc(pos_split, 1)
                dve.wait_ge(loaded, all_loaded)
                dve.tensor_tensor(sum_u[:], bq[:], u[:], ALU.add)
                dve.tensor_tensor(sum_v[:], bq[:], v[:], ALU.add).then_inc(sums_done, 1)
                dve.wait_ge(sums_done, 1)
                dve.tensor_scalar(bias_u[:], sum_u[:], SCALE, None, ALU.mult)
                dve.tensor_scalar(bias_v[:], sum_v[:], SCALE, None, ALU.mult).then_inc(bias_done, 1)
                ln.dve_stats(dve, 0)
                ln.dve_norm(dve, 0)
                dve.wait_ge(pos_done, 1)
                split(dve, pos_parts[:, 0, POS_0:POS_0 + S], pos_parts[:, 1, POS_0:POS_0 + S], pos[:],
                      pos_hi_done, 1).then_inc(pos_split, 2)
                ln.dve_stats(dve, 1)
                ln.dve_norm(dve, 1)

                def body(b, par):
                    if has_next(b + 1):
                        ln.dve_stats(dve, b + 2)
                    dve.wait_ge(qkv_ready, b + 1)
                    for t in range(TILES):
                        last = dve.tensor_tensor(
                            v_slice(v_all, t, b),
                            v_ps[par][:, t * D:(t + 1) * D].rearrange("p (h c) -> p h c", h=HEADS),
                            bv[:, 0:D].rearrange("p (h c) -> p h c", h=HEADS), ALU.add)
                    last.then_inc(v_done, 1)
                    if has_next(b + 1):
                        ln.dve_norm(dve, b + 2)
                    dve.wait_ge(qk_done, FREE_BANKS + b + 1)
                    dve.wait_ge(stored_qk[par], STORES + (b - par) * (STORES // 2))
                    split(dve, qu_parts[par][:, 0, :], qu_parts[par][:, 1, :], qu[par][:], hi_done, 3 * b + 1)
                    split(dve, k_parts[par][:, 0, :], k_parts[par][:, 1, :], kT[par][:], hi_done, 3 * b + 2)
                    own = [qv_at(qv_parts, t, b) for t in range(2)]
                    split(dve, own[0], own[1], qv[par][:].rearrange("p (n g) -> p n g", g=SPAN), hi_done,
                          3 * b + 3).then_inc(qk_split, 1)
                    dve.wait_ge(qk_split, b + 1)
                    dve.sem_inc(parts_used, 1)
                over_batches(dve, body)


def qv_at(qv_parts, part, b):
    rows = qv_parts[:, part * (S * B):(part + 1) * (S * B)].rearrange("p (n b g) -> p n b g", b=B, g=SPAN)
    return rows[:, :, bass.ds(b, 1), :].rearrange("p n b g -> p n (b g)")


QU_ROW = ROWS * SPAN
QU_SEQ = 2 * HD * QU_ROW
QV_RUN = HALF * SPAN
QV_ROW = 2 * P * QV_RUN
K_SEQ = 2 * HD * S
K_PART = HEADS * B * K_SEQ


def qu_out(scratch, b, part, span):
    return bass.AP(tensor=scratch["qu"].tensor, offset=b * QU_SEQ + part * (HD * QU_ROW) + span * B * QU_SEQ,
                   ap=[[SPANS * B * QU_SEQ, HEADS], [QU_ROW, HD], [1, QU_ROW]])


def qu_rows(scratch, h, span, b):
    return bass.AP(tensor=scratch["qu"].tensor, offset=h * (SPANS * B * QU_SEQ) + (span * B + b) * QU_SEQ,
                   ap=[[QU_ROW, 2 * HD], [SPAN, ROWS], [1, SPAN]])


def qv_out(scratch, span, half, part):
    return bass.AP(tensor=scratch["qv"].tensor, offset=(span * 2 + half) * (ROWS * QV_ROW) + part * (P * QV_RUN),
                   ap=[[QV_RUN, P], [QV_ROW, ROWS], [1, QV_RUN]])


def qv_rows(scratch, h, span, half, r):
    return bass.AP(tensor=scratch["qv"].tensor,
                   offset=h * (HD * QV_RUN) + ((span * 2 + half) * ROWS + r) * QV_ROW,
                   ap=[[QV_RUN, HD], [P * QV_RUN, 2], [1, QV_RUN]])


def qv_first_rows(scratch, h, span, half, part, g0, n):
    return bass.AP(tensor=scratch["qv"].tensor,
                   offset=h * (HD * QV_RUN) + (span * 2 + half) * (ROWS * QV_ROW) + part * (P * QV_RUN) + g0,
                   ap=[[QV_RUN, HD], [SPAN, HALF], [1, n]])


def k_out(scratch, b, part, copy):
    return bass.AP(tensor=scratch["k"].tensor, offset=b * K_SEQ + part * K_PART + copy * (HD * S),
                   ap=[[B * K_SEQ, HEADS], [S, HD], [1, S]])


def key_rows(scratch, h, half, part):
    return bass.AP(tensor=scratch["k"].tensor, offset=h * (B * K_SEQ) + part * K_PART + half * (HALF * K_SEQ),
                   ap=[[S, P], [1, S]])


def x_out(scratch, b):
    half, seq = divmod(b, HALF)
    return bass.AP(tensor=scratch["x"].tensor, offset=half * (HALF * S * D) + seq * D,
                   ap=[[HALF * D, P], [P * HALF * D, TILES], [1, D]])


def x_tiles(scratch, first, n):
    return bass.AP(tensor=scratch["x"].tensor, offset=first * (P * D), ap=[[D, P], [P * D, n], [1, D]])


def pos_table(scratch, h, first, part):
    return bass.AP(tensor=scratch["pos"].tensor, offset=h * (HD * 2 * POS_W) + part * POS_W + first,
                   ap=[[1, ROWS], [2 * POS_W, HD], [1, S]])


def v_slice(v_all, t, b):
    flat = v_all[:].rearrange("p (j h b c) -> p j h b c", j=TILES, h=HEADS, b=B)
    return flat[:, t, :, bass.ds(b, 1), :].rearrange("p h b c -> p h (b c)")


def relative_attention_phase(nc, ident, w, v_all, o_all, scratch):
    N_TILES = 2 * GROUPS
    N_PAIRS = N_TILES // 2
    N_BLOCKS = N_TILES // 8

    def lag(h, n, tiles):
        if n >= tiles:
            return (h, n - tiles) if not (isinstance(h, int) and h == HEADS) else None
        return (h - 1, n - tiles + N_TILES) if has_previous(h) else None

    def over_heads(eng, step):
        for n in range(N_TILES):
            step(0, n)
        with eng.Fori(1, HEADS) as h:
            for n in range(N_TILES):
                step(h, n)
        for n in range(PICK_LAG):
            step(HEADS, n)

    T_LAG = 2
    PV_LAG = 4
    BACK_LAG = 5
    PICK_LAG = 6

    with Phase(nc, "rel") as ph:
        left = [ph.sb(f"left{i}", [P, 2, ROWS * HALF * SPAN], F32R) for i in range(SPANS)]
        right = [ph.sb(f"right{i}", [P, 2, ROWS * HALF * SPAN], F32R) for i in range(SPANS)]
        cont = [ph.sb(f"cont{i}", [P, ROWS * HALF * SPAN], F32R) for i in range(SPANS)]
        keys = [[ph.sb(f"keys{i}{t}", [P, S], F32R) for t in range(2)] for i in range(2)]
        pos_l = [[ph.sb(f"pos_l{i}{t}", [P, S], F32R) for t in range(2)] for i in range(2)]
        pos_r = [[ph.sb(f"pos_r{i}{t}", [P, S], F32R) for t in range(2)] for i in range(2)]
        mask = ph.sb("mask", [P, P])
        picked = ph.sb("picked", [P, 8, HD])
        neg_max = ph.sb("neg_max", [P, 4])
        row_sum = ph.sb("row_sum", [P, N_TILES])
        probs = [ph.sb(f"probs{i}", [P, S]) for i in range(4)]
        probsT = [ph.sb(f"probsT{i}", [P, 2, TILES, 2, P], F32R) for i in range(2)]
        values = [ph.sb(f"values{i}", [P, TILES, 2, HALF * HD], F32R) for i in range(2)]
        own = [ph.sb(f"own{i}", [P, 2, P]) for i in range(2)]
        inv_sum = ph.sb("inv_sum", [P, 8, 1])
        s_ps = [ph.ps(f"s{i}", [P, S]) for i in range(4)]
        t_ps = [ph.ps(f"tps{i}", [P, S]) for i in range(2)]
        o_ps = ph.ps("o", [P, 2 * P])
        back_ps = ph.ps("back", [P, 4 * P])
        zeroed = [ph.sem(f"zeroed{i}") for i in range(SPANS)]
        passed = ph.sem("passed")
        mask_loaded = ph.sem("mask_loaded")
        loaded = [ph.sem(f"loaded{i}") for i in range(2)]
        s_ready = ph.sem("s_ready")
        max_done = ph.sem("max_done")
        p_done = ph.sem("p_done")
        t_ready = ph.sem("t_ready")
        hi_copied = ph.sem("hi_copied")
        pt_split = ph.sem("pt_split")
        v_hi_done = ph.sem("v_hi_done")
        v_split = ph.sem("v_split")
        pv_ready = ph.sem("pv_ready")
        own_done = ph.sem("own_done")
        back_ready = ph.sem("back_ready")
        picked_done = ph.sem("picked_done")
        inv_done = ph.sem("inv_done")
        o_done = ph.sem("o_done")
        LOADS = [ROWS + (ROWS - 1 + 4) + HALF + 6, ROWS + (ROWS - 1 + 2) + HALF]

        with nc.Block() as block:

            @block.sync
            def _(sp):
                sp.dma_start(mask[:], w["mask"]).then_inc(mask_loaded, 16)

                def get(dst, src, span):
                    sp.dma_start(dst.bitcast(F32), src, allow_slow_non_contiguous=True).then_inc(loaded[span], 16)

                def load_tables(h, half):
                    for part in range(2):
                        get(keys[half][part][:], key_rows(scratch, h, half, part), 0)
                        get(pos_r[half][part][:], pos_table(scratch, h, 0, part), 0)
                        get(pos_l[half][part][:], pos_table(scratch, h, POS_0, part), 0)

                def load_queries(h, half, span):
                    for b in range(HALF):
                        get(cont[span][b * 2 * HD:(b + 1) * 2 * HD, :]
                            .rearrange("c (r b g) -> c r b g", r=ROWS, b=HALF)[:, :, b, :],
                            qu_rows(scratch, h, span, half * HALF + b), span)
                    plane = HALF * SPAN
                    for n in range(ROWS):
                        s = ROWS - 1 - n
                        rows, own = slice(n * HD, (n + 1) * HD), slice(s * plane, (s + 1) * plane)
                        get(left[span][rows, :, own], qv_rows(scratch, h, span, half, s), span)
                        if s < ROWS - 1:
                            get(right[span][rows, :, own], qv_rows(scratch, h, span, half, s + 1), span)
                            continue
                        for part in range(2):
                            dst = right[span][rows, part, own].rearrange("c (b g) -> c b g", b=HALF)
                            get(dst[:, :, 0:SPAN - 1], qv_first_rows(scratch, h, span, half, part, 1, SPAN - 1), span)
                            if span + 1 < SPANS:
                                get(dst[:, :, SPAN - 1:SPAN],
                                    qv_first_rows(scratch, h, span + 1, half, part, 0, 1), span)

                load_tables(0, 0)
                for span in range(SPANS):
                    sp.wait_ge(zeroed[span], 3)
                    load_queries(0, 0, span)

                def load_next(h, half):
                    for span in range(SPANS):
                        wait_apart(sp, s_ready, h * N_TILES + (half - 1) * GROUPS + (span + 1) * SPAN, passed)
                        if span == 0:
                            load_tables(h, half)
                        load_queries(h, half, span)

                load_next(0, 1)
                with sp.Fori(1, HEADS) as h:
                    load_next(h, 0)
                    load_next(h, 1)

            @block.gpsimd
            def _(pool):
                for span in range(SPANS):
                    pool.memset(cont[span][:].bitcast(F32), 0.0).then_inc(zeroed[span], 1)

                def split_values(h, half):
                    H = 2 * h + half
                    own_v = v_all[:].rearrange("p (j e) -> p j e", j=TILES)[
                        :, :, bass.ds(h * (B * HD) + half * (HALF * HD), HALF * HD)]
                    hi, lo = (values[half][:, :, part, :] for part in range(2))
                    pool.tensor_copy(hi, own_v).then_inc(v_hi_done, 1)
                    wait_apart(pool, v_hi_done, H + 1, passed)
                    pool.tensor_tensor(lo, own_v, hi.bitcast(F32), ALU.subtract).then_inc(v_split, 1)

                split_values(0, 0)
                split_values(0, 1)
                with pool.Fori(1, HEADS) as h:
                    for half in range(2):
                        wait_apart(pool, pv_ready, (2 * (h - 1) + half + 1) * (N_PAIRS // 2), passed)
                        split_values(h, half)

            @block.tensor
            def _(pe):
                def scores(h, n):
                    half, g = divmod(n, GROUPS)
                    span, gs = divmod(g, SPAN)
                    i0 = g * ROWS
                    N = h * N_TILES + n
                    if gs == 0:
                        pe.wait_ge(loaded[span], (2 * h + half + 1) * (LOADS[span] * 16))
                    wait_from(pe, p_done, N - 3)
                    out = s_ps[n % 4]

                    def tile_of(buf):
                        return buf.rearrange("p (r g) -> p r g", g=SPAN)[:, :, gs]

                    for part in range(2):
                        pe.matmul(out[:], tile_of(cont[span][:]), keys[half][part][:], start=part == 0, stop=False)
                    for a, b in ((0, 0), (0, 1), (1, 0)):
                        pe.matmul(out[:, 0:i0 + ROWS], tile_of(left[span][:, a, :]),
                                  pos_l[half][b][:, S - ROWS - i0:S], start=False, stop=False)
                    for a, b in ((0, 0), (0, 1), (1, 0)):
                        last = pe.matmul(out[:, i0:S], tile_of(right[span][:, a, :]), pos_r[half][b][:, 0:S - i0],
                                         start=False, stop=(a, b) == (1, 0))
                    last.then_inc(s_ready, 1)

                def transpose(h, n):
                    N = h * N_TILES + n
                    pe.wait_ge(p_done, N + 1)
                    wait_from(pe, pt_split, N - 1)
                    for j in range(TILES):
                        last = pe.transpose(t_ps[n % 2][:, j * P:(j + 1) * P], probs[n % 4][:, j * P:(j + 1) * P],
                                            ident[:])
                    last.then_inc(t_ready, 1)

                def weigh_values(h, m):
                    M = h * N_PAIRS + m
                    half = m // (N_PAIRS // 2)
                    pe.wait_ge(v_split, 2 * h + half + 1)
                    pe.wait_ge(pt_split, 2 * M + 2)
                    wait_from(pe, own_done, M)
                    for j in range(TILES):
                        for part in range(2):
                            last = pe.matmul(o_ps[:], values[half][:, j, :, :].rearrange("p t e -> p (t e)"),
                                             probsT[m % 2][:, part, j, :, :].rearrange("p q r -> p (q r)"),
                                             start=j == 0 and part == 0, stop=j == TILES - 1 and part == 1)
                    last.then_inc(pv_ready, 1)

                def transpose_back(h, m):
                    M = h * N_PAIRS + m
                    pe.wait_ge(own_done, M + 1)
                    wait_from(pe, picked_done, M - 1)
                    for q in range(2):
                        at = (m % 2 * 2 + q) * P
                        last = pe.transpose(back_ps[:, at:at + P], own[m % 2][:, q, :], ident[:])
                    last.then_inc(back_ready, 1)

                def step(h, n):
                    if lag(h, n, 0):
                        scores(h, n)
                    if lag(h, n, T_LAG):
                        transpose(*lag(h, n, T_LAG))
                    if n % 2 == PV_LAG % 2 and lag(h, n, PV_LAG):
                        hp, at = lag(h, n, PV_LAG)
                        weigh_values(hp, at // 2)
                    if n % 2 == BACK_LAG % 2 and lag(h, n, BACK_LAG):
                        hp, at = lag(h, n, BACK_LAG)
                        transpose_back(hp, at // 2)
                over_heads(pe, step)

            @block.scalar
            def _(act):
                def copy_hi(h, n):
                    N = h * N_TILES + n
                    act.wait_ge(t_ready, N + 1)
                    if n % 2 == 0:
                        wait_from(act, pv_ready, h * N_PAIRS + n // 2 - 1)
                    act.copy(probsT[n // 2 % 2][:, 0, :, n % 2, :],
                             t_ps[n % 2][:].rearrange("p (j r) -> p j r", j=TILES)).then_inc(hi_copied, 1)

                def step(h, n):
                    if lag(h, n, T_LAG):
                        copy_hi(*lag(h, n, T_LAG))
                    if lag(h, n, 0):
                        act.wait_ge(max_done, h * N_TILES + n + 1)
                        act.activation(probs[n % 4][:], s_ps[n % 4][:], ACT.Exp, bias=neg_max[:, n % 4:n % 4 + 1],
                                       scale=1.0, accum_out=row_sum[:, n:n + 1]).then_inc(p_done, 1)
                over_heads(act, step)

            @block.vector
            def _(dve):
                for span in range(SPANS):
                    for buf in (left, right):
                        dve.memset(buf[span][:].bitcast(F32), 0.0).then_inc(zeroed[span], 1)
                dve.wait_ge(mask_loaded, 16)

                def maxima(h, n):
                    dve.wait_ge(s_ready, h * N_TILES + n + 1)
                    dve.tensor_reduce(neg_max[:, n % 4:n % 4 + 1], s_ps[n % 4][:], AX.X, ALU.max,
                                      negate=True).then_inc(max_done, 1)

                def split_lo(h, n):
                    N = h * N_TILES + n
                    dve.wait_ge(hi_copied, N + 1)
                    hi, lo = (probsT[n // 2 % 2][:, part, :, n % 2, :] for part in range(2))
                    dve.tensor_tensor(lo, t_ps[n % 2][:].rearrange("p (j r) -> p j r", j=TILES),
                                      hi.bitcast(F32), ALU.subtract).then_inc(pt_split, 1)

                def mask_own(h, m):
                    M = h * N_PAIRS + m
                    dve.wait_ge(pv_ready, M + 1)
                    wait_from(dve, back_ready, M - 1)
                    dve.tensor_tensor(own[m % 2][:], o_ps[:].rearrange("p (q r) -> p q r", q=2),
                                      mask[:].rearrange("p (q r) -> p q r", q=1).to_broadcast([P, 2, P]),
                                      ALU.mult).then_inc(own_done, 1)

                def pick(h, m):
                    M = h * N_PAIRS + m
                    dve.wait_ge(back_ready, M + 1)
                    if m % 4 == 0:
                        wait_from(dve, o_done, h * N_BLOCKS + m // 4)
                    dve.tensor_reduce(picked[:, m % 4 * 2:m % 4 * 2 + 2, :],
                                      back_ps[:, m % 2 * (2 * P):(m % 2 + 1) * (2 * P)]
                                      .rearrange("p (q b c) -> p q c b", q=2, c=HD), AX.X,
                                      ALU.add).then_inc(picked_done, 1)

                def outputs(h, g):
                    G = h * N_BLOCKS + g
                    dve.reciprocal(inv_sum[:, :, 0], row_sum[:, 8 * g:8 * g + 8]).then_inc(inv_done, 1)
                    dve.wait_ge(inv_done, G + 1)
                    dve.wait_ge(picked_done, 4 * G + 4)
                    dve.tensor_tensor(
                        o_all[:].rearrange("p (a e) -> p a e", e=D)[:, 8 * g:8 * g + 8, bass.ds(h * HD, HD)],
                        picked[:], inv_sum[:].to_broadcast([P, 8, HD]), ALU.mult).then_inc(o_done, 1)

                def step(h, n):
                    if n % 2 == BACK_LAG % 2 and lag(h, n, BACK_LAG):
                        hp, at = lag(h, n, BACK_LAG)
                        mask_own(hp, at // 2)
                    if lag(h, n, 0):
                        maxima(h, n)
                    if lag(h, n, T_LAG):
                        split_lo(*lag(h, n, T_LAG))
                    if n % 2 == PICK_LAG % 2 and lag(h, n, PICK_LAG):
                        hp, at = lag(h, n, PICK_LAG)
                        pick(hp, at // 2)
                        if at % 8 == 6:
                            outputs(hp, at // 8)
                over_heads(dve, step)


def out_projection_phase(nc, x, ident, w, scratch, w_parts, parts_loaded):
    with Phase(nc, "proj") as ph:
        x_saved = ph.sb("x_saved", [P, B * S])
        wo = ph.sb("wo", [P, D])
        bo = ph.sb("bo", [P, S])
        oT = [ph.sb(f"oT{i}", [P, S]) for i in range(2)]
        t_ps = [ph.ps(f"tps{i}", [P, S]) for i in range(2)]
        y_ps = [ph.ps(f"y{i}", [P, S]) for i in range(2)]
        loaded = ph.sem("loaded")
        x_loaded = ph.sem("x_loaded")
        t_ready = ph.sem("t_ready")
        oT_done = ph.sem("oT_done")
        y_ready = ph.sem("y_ready")
        x_done = ph.sem("x_done")
        bias_done = ph.sem("bias_done")
        PRE = 2
        loads = [(wo[:], w["wo"]), (bo[:], w["bo"].to_broadcast([P, S]))]

        with nc.Block() as block:

            @block.sync
            def _(sp):
                for dst, src in loads:
                    sp.dma_start(dst, src).then_inc(loaded, 16)
                for b in range(0, B, 4):
                    sp.dma_start(x_saved[:, b * S:(b + 4) * S].rearrange("p (t h) -> p t h", h=D),
                                 x_tiles(scratch, b * TILES, 4 * TILES)).then_inc(x_loaded, 16)
                sp.dma_start(w_parts[:].bitcast(F32), scratch["w_parts"]).then_inc(parts_loaded, 16)

            @block.tensor
            def _(pe):
                pe.sem_inc(y_ready, PRE)
                def transpose(b, par):
                    pe.wait_ge(oT_done, PRE + b - 1)
                    for t in range(TILES):
                        last = pe.transpose(t_ps[par][:, t * P:(t + 1) * P], tile_at(x, b, t), ident[:])
                    last.then_inc(t_ready, 1)

                def project(b, par):
                    pe.wait_ge(oT_done, PRE + b + 1)
                    pe.wait_ge(x_done, PRE + b - 1)
                    for t in range(TILES):
                        last = pe.matmul(y_ps[par][:, t * D:(t + 1) * D], oT[par][:, t * P:(t + 1) * P], wo[:],
                                         start=True, stop=True)
                    last.then_inc(y_ready, 1)
                pe.wait_ge(loaded, 16 * len(loads))
                transpose(0, 0)
                for b in range(B):
                    if b + 1 < B:
                        transpose(b + 1, (b + 1) % 2)
                    project(b, b % 2)

            @block.scalar
            def _(act):
                act.sem_inc(oT_done, PRE)

                def body(b, par):
                    act.wait_ge(t_ready, b + 1)
                    act.wait_ge(y_ready, PRE + b - 1)
                    act.copy(oT[par][:], t_ps[par][:]).then_inc(oT_done, 1)
                over_batches(act, body)

            @block.gpsimd
            def _(pool):
                pool.wait_ge(loaded, 16 * len(loads))
                pool.wait_ge(x_loaded, 16 * 4)
                with pool.Fori(0, B) as b:
                    pool.tensor_tensor(rows_at(x_saved, b), rows_at(x_saved, b), bo[:], ALU.add).then_inc(bias_done, 1)

            @block.vector
            def _(dve):
                dve.sem_inc(x_done, PRE)

                def body(b, par):
                    dve.wait_ge(y_ready, PRE + b + 1)
                    dve.wait_ge(bias_done, b + 1)
                    dve.tensor_tensor(rows_at(x, b), y_ps[par][:], rows_at(x_saved, b), ALU.add).then_inc(x_done, 1)
                over_batches(dve, body)


def token_rows(dram, half, g):
    return bass.AP(tensor=dram.tensor, offset=(half * HALF * S + g * ROWS) * D,
                   ap=[[D, ROWS], [S * D, HALF], [1, D]])


def build(nc, a, out):
    scratch = {
        "x": nc.dram_tensor("x_scratch", [B * S, D], F32).ap(),
        "qu": nc.dram_tensor("qu_scratch", [HEADS * SPANS * B, QU_SEQ], F32).ap(),
        "qv": nc.dram_tensor("qv_scratch", [SPANS * 2 * ROWS, QV_ROW], F32).ap(),
        "k": nc.dram_tensor("k_scratch", [2 * HEADS * B, K_SEQ], F32).ap(),
        "w_parts": nc.dram_tensor("w_parts_scratch", [P, 2, W_COLS], F32).ap(),
        "pos": nc.dram_tensor("pos_scratch", [P, 2, POS_W], F32).ap(),
    }
    x_in = a["x"].rearrange("b (t p) h -> b p t h", p=P)
    moe0 = {n: a["e0_" + n] for n in ("w1", "b1", "w2", "b2", "wg", "bg")}
    moe1 = {n: a["e1_" + n] for n in ("b1", "b2", "wg", "bg")}
    with Phase(nc, "all") as ph:
        x = ph.sb("x", [P, B * S])
        ident = ph.sb("ident", [P, P])
        iota = ph.sb("iota", [P, EXPERTS])
        first_loads = [(ident[:], a["ident"]), (iota[:], a["iota"].to_broadcast([P, EXPERTS]))]

        with Phase(nc, "wp") as wp:
            w_parts = wp.sb("w_parts", [P, 2, W_COLS], F32R)
            top1_ffn_phase(nc, "moe0a", x, ident, iota, moe0, x_in=x_in, first_loads=first_loads, weight_split=(w_parts, a["e1_w"]))
            decay_attention_phase(nc, x, ident, {n: a["d_" + n] for n in ("wrkv", "brkv", "wo", "bo", "nu_log", "gamma_log")},
                                  w_parts, scratch["w_parts"])
            top1_ffn_phase(nc, "moe0b", x, ident, iota, moe0)
            top2_ffn_phase(nc, "moe1a", x, ident, iota, moe1, w_parts)
        o_all = x
        with Phase(nc, "attv") as attv:
            v_all = attv.sb("v_all", [P, B * S])
            qkv_phase(nc, x, ident, {n: a["r_" + n] for n in ("wq", "wk", "wv", "wp", "bq", "bk", "bp", "u", "v",
                                                              "bv", "embT")}, v_all, scratch)
            relative_attention_phase(nc, ident, {"mask": a["mask"]}, v_all, o_all, scratch)
        w_parts = ph.sb("w_parts_again", [P, 2, W_COLS], F32R)
        parts_loaded = ph.sem("parts_loaded")
        out_projection_phase(nc, x, ident, {"wo": a["r_wo"], "bo": a["r_bo"]}, scratch, w_parts,
                             parts_loaded)
        top2_ffn_phase(nc, "moe1b", x, ident, iota, moe1, w_parts, parts_loaded=parts_loaded,
                       store_to=out.rearrange("b s h -> (b s) h"))


def lay_out(i):
    def col(v):
        return np.ascontiguousarray(np.reshape(v, (D, 1)))

    def row(v, times):
        return np.ascontiguousarray(np.tile(np.reshape(v, (1, -1)), (1, times)))

    a = {"x": i["L0_attn_inputs"]}
    f = "L0_ffn_"
    a["e0_w1"] = i[f + "W1"].transpose(1, 0, 2).reshape(P, -1)
    a["e0_b1"] = i[f + "b1"].T
    a["e0_w2"] = i[f + "W2"].transpose(1, 0, 2).reshape(P, -1)
    a["e0_b2"] = i[f + "b2"]
    a["e0_wg"] = i[f + "Wg"]
    a["e0_bg"] = row(i[f + "bg"], TILES)
    f = "L1_ffn_"
    w1 = np.concatenate([i[f + "w1"], i[f + "sw1"][None]])
    w2 = np.concatenate([i[f + "w2"], i[f + "sw2"][None]])
    b1 = np.concatenate([i[f + "b1"], i[f + "sb1"][None]])
    a["e1_b1"] = b1.reshape(-1, P).T
    a["e1_w"] = np.concatenate([w1.transpose(1, 0, 2).reshape(P, -1),
                                w2.reshape(9, 4, P, D).transpose(2, 0, 1, 3).reshape(P, -1)], axis=1)
    b2 = np.concatenate([i[f + "b2"], i[f + "sb2"][None]])
    a["e1_b2"] = np.concatenate([b2, np.zeros((LO_ROW - len(b2), D), np.float32), b2])
    a["e1_wg"] = i[f + "gate_w"].T
    a["e1_bg"] = row(i[f + "gate_b"], TILES)
    f = "L0_attn_"
    a["d_wrkv"] = i[f + "W_rkv"]
    a["d_brkv"] = i[f + "b_rkv"].reshape(3, D).T
    a["d_wo"] = i[f + "W_o"]
    a["d_bo"] = row(i[f + "b_o"], TILES)
    a["d_nu_log"] = col(i[f + "nu_log"])
    a["d_gamma_log"] = col(i[f + "gamma_log"])
    f = "L1_attn_"
    for n in "qkvp":
        a["r_w" + n] = i[f + "W" + n]
    a["r_wo"] = i[f + "Wo"]
    for n in "qkp":
        a["r_b" + n] = col(i[f + "b" + n])
    a["r_bv"] = row(i[f + "bv"], TILES)
    a["r_bo"] = row(i[f + "bo"], TILES)
    a["r_u"] = col(i[f + "u"])
    a["r_v"] = col(i[f + "v"])
    pos = np.arange(S, dtype=np.float32)
    freq = (1.0 / np.float32(10000.0) ** (np.float32(2.0) * np.arange(D // 2, dtype=np.float32) / np.float32(D))).astype(np.float32)
    ang = pos[:, None] * freq[None, :]
    a["r_embT"] = np.concatenate([np.sin(ang), np.cos(ang)], axis=-1).astype(np.float32).T
    a["ident"] = np.eye(P, dtype=np.float32)
    a["iota"] = np.arange(EXPERTS, dtype=np.float32)[None]
    a["mask"] = (np.arange(P)[:, None] // HD % HALF == np.arange(P)[None] % HALF).astype(np.float32)
    return {n: np.ascontiguousarray(v) for n, v in a.items()}





def kernel(**inputs):
    import concourse.bacc as bacc
    from concourse.bass_utils import run_bass_kernel_spmd

    arrays = lay_out({n: np.asarray(v) for n, v in inputs.items()})
    nc = bacc.Bacc("TRN2", target_bir_lowering=False, num_devices=1)
    aps = {n: nc.dram_tensor(f"in_{n}", v.shape, mybir.dt.from_np(v.dtype), kind="ExternalInput").ap()
           for n, v in arrays.items()}
    out = nc.dram_tensor("out", (B, S, D), F32, kind="ExternalOutput").ap()
    build(nc, aps, out)
    r = run_bass_kernel_spmd(nc, [{f"in_{n}": v for n, v in arrays.items()}], core_ids=[0])
    return r.results[0]["out"]
```
